# Optimizing a Trainium2 kernel written in Bass

```python
import numpy as np
import jax
import jax.numpy as jnp

def _softmax(x, axis=-1):
    return jax.nn.softmax(x, axis=axis)

def _gelu(x):
    return jax.nn.gelu(x, approximate=True)

def _silu(x):
    return jax.nn.silu(x)

def _sigmoid(x):
    return jax.nn.sigmoid(x)

def _layernorm(x, axis=-1, eps=1e-05):
    m = jnp.mean(x, axis=axis, keepdims=True)
    v = jnp.var(x, axis=axis, keepdims=True)
    return (x - m) / jnp.sqrt(v + eps)

def _scatter_add(tgt, idx, src, axis=0):
    return tgt.at[idx].add(src)

def _segment_sum(src, seg, n):
    return jax.ops.segment_sum(src, seg, n)
kernel_name = 'mk_pixart_seq_d2_seqx_r4_b3f794'

def setup_inputs(seed: int=0):
    np.random.seed(seed)
    _w = jnp.asarray

    def _rec_inputs():
        import jax
        import jax.numpy as jnp
        _rk = jax.random.key(seed)
        x = -0.0003929 + 0.9999 * jax.random.normal(jax.random.fold_in(_rk, 1), (2, 1024, 256), jnp.float32)
        _lenS = 1024 - jax.random.randint(jax.random.fold_in(_rk, 7), (2,), 0, max(1, 1024 // 4) + 1, jnp.int32)
        _lenS2 = 154 - jax.random.randint(jax.random.fold_in(_rk, 8), (2,), 0, max(1, 154 // 4) + 1, jnp.int32)
        cond_1024 = 0.00782532 + 1.00527 * jax.random.normal(jax.random.fold_in(_rk, 11), (2, 256), jnp.float32)
        _ctx_1024P = jax.random.normal(jax.random.fold_in(_rk, 12), (2, 16, 256), jnp.float32)
        _ctx_1024c = jax.random.dirichlet(jax.random.fold_in(_rk, 512), 0.3 * jnp.ones((16,), jnp.float32), (2, 154))
        _ctx_1024t = jnp.einsum('bsk,bkd->bsd', _ctx_1024c, _ctx_1024P)
        _ctx_1024t = _ctx_1024t * jax.lax.rsqrt(jnp.mean(jnp.square(_ctx_1024t)) + 1e-12) * 0.953939
        ctx_1024 = -0.000761806 + 0.999296 * (_ctx_1024t + 0.3 * jax.random.normal(jax.random.fold_in(_rk, 612), (2, 154, 256), jnp.float32))
        return (x, cond_1024, ctx_1024)
    x, cond_1024, ctx_1024 = _rec_inputs()

    def _L0_xcond_setup():
        import jax, jax.numpy as jnp
        import numpy as np
        H = 256
        RH = 2 * H
        E = 3
        B, T, P = (8, 512, 64)
        LN_EPS = 1e-05

        def _layer_norm(x, gamma, beta):
            mu = jnp.mean(x, axis=-1, keepdims=True)
            var = jnp.mean(jnp.square(x - mu), axis=-1, keepdims=True)
            return (x - mu) * jax.lax.rsqrt(var + LN_EPS) * gamma + beta
        key = jax.random.key(seed)
        ks = jax.random.split(key, 24)
        s = lambda fan_in: 1.0 / np.sqrt(fan_in)
        inp = {'mix_hidden_states': jax.random.normal(ks[0], (B, T, H), jnp.float32), 'global_anchor': jax.random.normal(ks[1], (B, H), jnp.float32), 'prototype_bank': jax.random.normal(ks[2], (B, P, H), jnp.float32), 'ln_gamma': jnp.ones((H,), jnp.float32), 'ln_beta': jnp.zeros((H,), jnp.float32), 'Wq': jax.random.normal(ks[3], (H, H), jnp.float32) * s(H), 'Wk': jax.random.normal(ks[4], (H, H), jnp.float32) * s(H), 'Wv': jax.random.normal(ks[5], (H, H), jnp.float32) * s(H), 'router_W': jax.random.normal(ks[6], (3 * H, E), jnp.float32) * s(3 * H), 'router_b': jnp.zeros((E,), jnp.float32), 'e_w1': jax.random.normal(ks[7], (E, 3 * H, RH), jnp.float32) * s(3 * H), 'e_b1': jnp.zeros((E, RH), jnp.float32), 'e_w2': jax.random.normal(ks[8], (E, RH, H), jnp.float32) * s(RH), 'e_b2': jnp.zeros((E, H), jnp.float32), 'gate_w1': jax.random.normal(ks[9], (3 * H, H), jnp.float32) * s(3 * H), 'gate_b1': jnp.zeros((H,), jnp.float32), 'gate_w2': jax.random.normal(ks[10], (H, H), jnp.float32) * s(H), 'gate_b2': jnp.zeros((H,), jnp.float32), 'out_w': jax.random.normal(ks[11], (H, H), jnp.float32) * s(H), 'out_b': jnp.zeros((H,), jnp.float32)}
        return inp
    _L0_xcond_all = _L0_xcond_setup()
    _L0_xcond_in = {k: v for k, v in _L0_xcond_all.items() if k in ('ln_gamma', 'ln_beta', 'Wq', 'Wk', 'Wv', 'router_W', 'router_b', 'e_w1', 'e_b1', 'e_w2', 'e_b2', 'gate_w1', 'gate_b1', 'gate_w2', 'gate_b2', 'out_w', 'out_b')}
    del _L0_xcond_all

    def _L1_xcond_setup():
        import jax, jax.numpy as jnp
        import numpy as np
        EPS = 1e-05

        def _ada_ln(x, c, W_ss, b_ss):
            mu = jnp.mean(x, axis=-1, keepdims=True)
            var = jnp.mean((x - mu) ** 2, axis=-1, keepdims=True)
            h = (x - mu) / jnp.sqrt(var + EPS)
            ss = jax.nn.silu(c) @ W_ss + b_ss
            scale, bias = jnp.split(ss, 2, axis=-1)
            return (1.0 + scale)[:, None, :] * h + bias[:, None, :]
        key = jax.random.key(seed)
        ks = jax.random.split(key, 12)
        B, Lq, Lkv, H = (8, 512, 128, 256)
        s = 0.02
        return {'x_q': jax.random.normal(ks[0], (B, Lq, H), jnp.float32), 'x_kv': jax.random.normal(ks[1], (B, Lkv, H), jnp.float32), 't_vec': jax.random.normal(ks[2], (B, H), jnp.float32), 'Wq': jax.random.normal(ks[3], (H, H), jnp.float32) * s, 'bq': jnp.zeros((H,), jnp.float32), 'Wkv': jax.random.normal(ks[4], (H, 2 * H), jnp.float32) * s, 'bkv': jnp.zeros((2 * H,), jnp.float32), 'Wp': jax.random.normal(ks[5], (H, H), jnp.float32) * s, 'bp': jnp.zeros((H,), jnp.float32), 'Wss_q': jax.random.normal(ks[6], (H, 2 * H), jnp.float32) * s, 'bss_q': jnp.zeros((2 * H,), jnp.float32), 'Wss_kv': jax.random.normal(ks[7], (H, 2 * H), jnp.float32) * s, 'bss_kv': jnp.zeros((2 * H,), jnp.float32)}
    _L1_xcond_all = _L1_xcond_setup()
    _L1_xcond_in = {k: v for k, v in _L1_xcond_all.items() if k in ('Wq', 'bq', 'Wkv', 'bkv', 'Wp', 'bp', 'Wss_q', 'bss_q', 'Wss_kv', 'bss_kv')}
    del _L1_xcond_all
    return {'x': x, 'cond_1024': cond_1024, 'ctx_1024': ctx_1024, 'L0_xcond_ln_gamma': _L0_xcond_in['ln_gamma'], 'L0_xcond_ln_beta': _L0_xcond_in['ln_beta'], 'L0_xcond_Wq': _L0_xcond_in['Wq'], 'L0_xcond_Wk': _L0_xcond_in['Wk'], 'L0_xcond_Wv': _L0_xcond_in['Wv'], 'L0_xcond_router_W': _L0_xcond_in['router_W'], 'L0_xcond_router_b': _L0_xcond_in['router_b'], 'L0_xcond_e_w1': _L0_xcond_in['e_w1'], 'L0_xcond_e_b1': _L0_xcond_in['e_b1'], 'L0_xcond_e_w2': _L0_xcond_in['e_w2'], 'L0_xcond_e_b2': _L0_xcond_in['e_b2'], 'L0_xcond_gate_w1': _L0_xcond_in['gate_w1'], 'L0_xcond_gate_b1': _L0_xcond_in['gate_b1'], 'L0_xcond_gate_w2': _L0_xcond_in['gate_w2'], 'L0_xcond_gate_b2': _L0_xcond_in['gate_b2'], 'L0_xcond_out_w': _L0_xcond_in['out_w'], 'L0_xcond_out_b': _L0_xcond_in['out_b'], 'L1_xcond_Wq': _L1_xcond_in['Wq'], 'L1_xcond_bq': _L1_xcond_in['bq'], 'L1_xcond_Wkv': _L1_xcond_in['Wkv'], 'L1_xcond_bkv': _L1_xcond_in['bkv'], 'L1_xcond_Wp': _L1_xcond_in['Wp'], 'L1_xcond_bp': _L1_xcond_in['bp'], 'L1_xcond_Wss_q': _L1_xcond_in['Wss_q'], 'L1_xcond_bss_q': _L1_xcond_in['bss_q'], 'L1_xcond_Wss_kv': _L1_xcond_in['Wss_kv'], 'L1_xcond_bss_kv': _L1_xcond_in['bss_kv']}

def reference(x, cond_1024, ctx_1024, L0_xcond_ln_gamma, L0_xcond_ln_beta, L0_xcond_Wq, L0_xcond_Wk, L0_xcond_Wv, L0_xcond_router_W, L0_xcond_router_b, L0_xcond_e_w1, L0_xcond_e_b1, L0_xcond_e_w2, L0_xcond_e_b2, L0_xcond_gate_w1, L0_xcond_gate_b1, L0_xcond_gate_w2, L0_xcond_gate_b2, L0_xcond_out_w, L0_xcond_out_b, L1_xcond_Wq, L1_xcond_bq, L1_xcond_Wkv, L1_xcond_bkv, L1_xcond_Wp, L1_xcond_bp, L1_xcond_Wss_q, L1_xcond_bss_q, L1_xcond_Wss_kv, L1_xcond_bss_kv):
    import jax
    import jax.numpy as jnp

    def _L0_xcond_ref(mix_hidden_states, global_anchor, prototype_bank, ln_gamma, ln_beta, Wq, Wk, Wv, router_W, router_b, e_w1, e_b1, e_w2, e_b2, gate_w1, gate_b1, gate_w2, gate_b2, out_w, out_b):
        import jax, jax.numpy as jnp
        import numpy as np
        H = 256
        RH = 2 * H
        E = 3
        B, T, P = (8, 512, 64)
        LN_EPS = 1e-05

        def _layer_norm(x, gamma, beta):
            mu = jnp.mean(x, axis=-1, keepdims=True)
            var = jnp.mean(jnp.square(x - mu), axis=-1, keepdims=True)
            return (x - mu) * jax.lax.rsqrt(var + LN_EPS) * gamma + beta
        x = mix_hidden_states
        nx = _layer_norm(x, ln_gamma, ln_beta)
        q = nx @ Wq
        k = prototype_bank @ Wk
        v = prototype_bank @ Wv
        scores = jnp.einsum('bth,bph->btp', q, k) * H ** (-0.5)
        weights = jax.nn.softmax(scores, axis=-1)
        evidence = jnp.einsum('btp,bph->bth', weights, v)
        anchor = jnp.broadcast_to(global_anchor[:, None, :], nx.shape)
        combined = jnp.concatenate([nx, evidence, anchor], axis=-1)
        router_logits = combined @ router_W + router_b
        router_probs = jax.nn.softmax(router_logits, axis=-1)
        h = jax.nn.silu(jnp.einsum('btc,ecr->bter', combined, e_w1) + e_b1)
        expert_out = jnp.einsum('bter,erh->bteh', h, e_w2) + e_b2
        routed = jnp.sum(expert_out * router_probs[..., None], axis=-2)
        g = jax.nn.sigmoid(jax.nn.silu(combined @ gate_w1 + gate_b1) @ gate_w2 + gate_b2)
        refined_delta = g * (routed @ out_w + out_b)
        return x + refined_delta

    def _L1_xcond_ref(x_q, x_kv, t_vec, Wq, bq, Wkv, bkv, Wp, bp, Wss_q, bss_q, Wss_kv, bss_kv):
        import jax, jax.numpy as jnp
        import numpy as np
        EPS = 1e-05

        def _ada_ln(x, c, W_ss, b_ss):
            mu = jnp.mean(x, axis=-1, keepdims=True)
            var = jnp.mean((x - mu) ** 2, axis=-1, keepdims=True)
            h = (x - mu) / jnp.sqrt(var + EPS)
            ss = jax.nn.silu(c) @ W_ss + b_ss
            scale, bias = jnp.split(ss, 2, axis=-1)
            return (1.0 + scale)[:, None, :] * h + bias[:, None, :]
        B, Lq, H = x_q.shape
        Lkv = x_kv.shape[1]
        nh = 16
        dh = H // nh
        xq = _ada_ln(x_q, t_vec, Wss_q, bss_q)
        xkv = _ada_ln(x_kv, t_vec, Wss_kv, bss_kv)
        q = (xq @ Wq + bq).reshape(B, Lq, nh, dh)
        kv = (xkv @ Wkv + bkv).reshape(B, Lkv, 2, nh, dh)
        k = kv[:, :, 0]
        v = kv[:, :, 1]
        scores = jnp.einsum('bqhd,bkhd->bhqk', q, k) / jnp.sqrt(jnp.float32(dh))
        attn = jax.nn.softmax(scores, axis=-1)
        out = jnp.einsum('bhqk,bkhd->bqhd', attn, v).reshape(B, Lq, H)
        return x_q + (out @ Wp + bp)
    x = _L0_xcond_ref(x, cond_1024, ctx_1024, L0_xcond_ln_gamma, L0_xcond_ln_beta, L0_xcond_Wq, L0_xcond_Wk, L0_xcond_Wv, L0_xcond_router_W, L0_xcond_router_b, L0_xcond_e_w1, L0_xcond_e_b1, L0_xcond_e_w2, L0_xcond_e_b2, L0_xcond_gate_w1, L0_xcond_gate_b1, L0_xcond_gate_w2, L0_xcond_gate_b2, L0_xcond_out_w, L0_xcond_out_b)
    x = _L1_xcond_ref(x, ctx_1024, cond_1024, L1_xcond_Wq, L1_xcond_bq, L1_xcond_Wkv, L1_xcond_bkv, L1_xcond_Wp, L1_xcond_bp, L1_xcond_Wss_q, L1_xcond_bss_q, L1_xcond_Wss_kv, L1_xcond_bss_kv)
    return x

_drawn_inputs = setup_inputs


def setup_inputs(seed=0):
    import zlib

    import numpy as np

    out = dict(_drawn_inputs(seed))
    spreads = {'L0_xcond_ln_gamma': (1.0, 0.545),
     'L0_xcond_ln_beta': (0.0, 0.67),
     'L0_xcond_router_b': (0.0, 0.8),
     'L0_xcond_e_b1': (0.0, 0.435),
     'L0_xcond_e_b2': (0.0, 0.278),
     'L0_xcond_gate_b1': (0.0, 0.8),
     'L0_xcond_gate_b2': (0.0, 0.8),
     'L0_xcond_out_b': (0.0, 0.1),
     'L1_xcond_bq': (0.0, 2.0),
     'L1_xcond_bkv': (0.0, 0.1),
     'L1_xcond_bp': (0.0, 0.1),
     'L1_xcond_bss_q': (0.0, 2.0),
     'L1_xcond_bss_kv': (0.0, 0.758)}
    factors = {'L1_xcond_Wq': 8.0, 'L1_xcond_Wss_q': 8.0}
    for name, (base, spread) in spreads.items():
        noise = np.random.default_rng([zlib.crc32(name.encode()), seed]).standard_normal(out[name].shape)
        drawn = base * np.exp(spread * noise) if base else spread * noise
        out[name] = jnp.asarray(drawn.astype(out[name].dtype))
    for name, factor in factors.items():
        out[name] = (out[name] * factor).astype(out[name].dtype)
    return out
```

```python
from contextlib import ExitStack

import concourse.bass as bass
from concourse import mybir

F32 = mybir.dt.float32
F32R = mybir.dt.float32r
ALU = mybir.AluOpType
ACT = mybir.ActivationFunctionType
AX = mybir.AxisListType

P = 128
BATCH, SEQ, D, CTX = 2, 1024, 256, 154
KC = D // P
TILE = 512
NSUB = TILE // P
TPB = SEQ // TILE
NT = BATCH * TPB
TAIL = CTX - P
EXPERTS, RH = 3, 512
ZCOLS = D + EXPERTS * RH
NZ = ZCOLS // P
GATES = D // P
PER = RH // P
QN = 448
NQ = ZCOLS // QN
HEADS, DH = 16, D // 16
PAIRS = HEADS // 2
GROUPS = HEADS // 4
STACK = 96
KROWS = STACK + 4
EPS = 1e-5
RING = 3

C_ID, C_HEAD, C_SPLIT, C_ROW, C_ONE = 0, 128, 130, 131, 135
C_PAIR = 136
NCONST = 138
N_VECTORS = 16
N_HIDDEN_BIAS = 7


def shape_constants(np):
    c = np.zeros((P, NCONST), np.float32)
    row = np.arange(P)
    c[:, C_ID:C_ID + P] = np.eye(P)
    c[:, C_HEAD] = row % 32 < DH
    c[:, C_HEAD + 1] = row % 32 >= DH
    c[:, C_SPLIT] = -1.0 * (row % 32 >= DH)
    for i in range(4):
        c[:, C_ROW + i] = (row >= TAIL * i) & (row < TAIL * (i + 1))
    c[:, C_ONE] = 1.0
    c[STACK:KROWS, C_PAIR] = (1, 0, 1, 0)
    c[STACK:KROWS, C_PAIR + 1] = (0, 1, 0, 1)
    return c


STEPS = {
    "tensor": {
        "setup": ["wqT", "mod", "bq"],
        "ctx": ["ctxT", "kT", "vT", "A", "VR", "RC", "vw0", "vw1", "vw2", "vw3"],
        "w2": [f"t{i}" for i in range(6)] + [f"m{j}" for j in range(6)] + ["cb"],
        "kv": ["xT", "k", "v", "vt"],
        "norm": ["t0", "t1"],
        "att": ["s", "p"],
        "z": ["z"],
        "p": ["p"],
        "query": ["t0", "t1", "q0", "q1"],
        "most": [f"c{c}" for c in range(PAIRS)],
        "row": ["m"],
        "score": ["s0", "s1", "s2", "s3", "s4"],
        "value": ["v"],
        "proj": ["o0", "o1"],
    },
    "scalar": {
        "setup": ["tc", "wqT", "wn", "gw", "wq", "wp"],
        "ctx": ["ctxT", "vT", "A", "vw0", "vw1", "vw2", "vw3"],
        "w2": [f"t{i}" for i in range(6)] + [f"m{j}" for j in range(6)],
        "kv": ["x0", "x1"],
        "norm": ["n0", "n1"],
        "att": ["e"],
        "route": ["pm", "pd", "ex"],
        "z": ["t", "h"],
        "res": ["t"],
        "query": ["x0", "x1", "q0", "q1"],
        "row": ["h"],
        "score": ["e0", "e1", "e2", "e3", "e4"],
    },
    "vector": {
        "setup": ["fill", "sc", "mod", "bq", "wn", "gw", "wq", "wp"],
        "ctx": ["fill", "kT", "VR", "RC", "vw0", "vw1", "vw2", "vw3", "th", "tl"],
        "w2": [f"m{j}" for j in range(6)] + ["cb"],
        "kv": ["var", "xh", "rep", "k", "kh", "kl", "ones", "kt", "v", "vt"],
        "norm": ["var", "xh", "n0", "n1"],
        "att": ["max", "p", "lg"],
        "route": ["pl", "dl", "lg", "prob", "acc"],
        "z": ["s"],
        "evac": ["o"],
        "res": ["u", "x"],
        "query": ["var", "xh", "x0", "x1", "q0", "q1"],
        "most": [f"c{c}" for c in range(PAIRS)],
        "row": ["l"],
        "value": ["take", "a"],
        "proj": ["o0", "o1"],
    },
    "gpsimd": {
        "kv": ["rstd"],
        "norm": ["rstd"],
        "p": ["l"],
        "query": ["rstd"],
        "bias": ["x"],
    },
}


def schedule():
    def expert(t, k):
        out = [("z", t, k)] if k < NZ else []
        if 0 <= k - 2 < NZ:
            out.append(("p", t, k - 2))
            if k - 2 == GATES - 1:
                out.append(("evac", t, 0))
            elif k - 2 >= GATES and (k - 2 - GATES) % PER == PER - 1:
                out.append(("evac", t, (k - 2 - GATES) // PER + 1))
        return out

    def first(t, beside):
        out = [("norm", t)]
        beside = list(beside)
        if beside:
            out += beside.pop(0)
        out += [("att", t, s) for s in range(NSUB)] + [("route", t)]
        for k in range(NZ + 2):
            out += expert(t, k)
            if beside:
                out += beside.pop(0)
        out.append(("res", t))
        for piece in beside:
            out += piece
        return out

    def second(t):
        out = [[("query", t), ("bias", t)], [], []] + [[("most", t, s)] for s in range(NSUB)] + [[("row", t)], []]
        out.append([("score", t, 0)])
        for a in range(GROUPS):
            out.append([("value", t, a)] + ([("score", t, a + 1)] if a + 1 < GROUPS else []))
        out.append([("proj", t)])
        return out

    out = [("setup", 0), ("ctx", 0), ("w2", 0), ("kv", 0)]
    for b in range(BATCH):
        if b:
            out += [("ctx", b), ("kv", b)]
        out += first(TPB * b, [])
        for i in range(1, TPB):
            out += first(TPB * b + i, second(TPB * b + i - 1))
        for piece in second(TPB * b + TPB - 1):
            out += piece
    return out


INSTANCE = {
    "att": lambda t, s: NSUB * t + s, "most": lambda t, s: NSUB * t + s,
    "z": lambda t, k: NZ * t + k, "p": lambda t, k: NZ * t + k,
    "evac": lambda t, j: (1 + EXPERTS) * t + j,
    "score": lambda t, a: GROUPS * t + a, "value": lambda t, a: GROUPS * t + a,
}


def build(nc, a, out, consts):
    with ExitStack() as ctx:
        def sem(name):
            return ctx.enter_context(nc.semaphore(name))

        def psum(name, shape):
            return ctx.enter_context(nc.psum_tensor(name, shape, F32))

        Z = psum("hidden_banks", [P, 2, 512])
        O = psum("token_banks", [P, NSUB, D])
        M0 = psum("misc_bank", [P, 512])
        S = psum("score_banks", [P, 2, 512])
        V0 = psum("value_bank", [P, 512])

        at = [(nc.sbuf_base + 63) // 64 * 64]

        def put(name, shape, dt=F32, offset=None):
            size = 4
            for n in shape[1:]:
                size *= n
            o = at[0] if offset is None else offset
            if offset is None:
                at[0] += (size + 31) // 32 * 32
            return nc.alloc_sbuf_tensor_at(name, shape, dt, offset=o)

        def run(start, parts):
            made = []
            for name, shape, dt in parts:
                made.append(put(name, shape, dt, offset=start))
                size = 4
                for n in shape[1:]:
                    size *= n
                start += (size + 31) // 32 * 32
            return made + [start]

        CN = put("constants", [P, NCONST])
        ident = CN[:, C_ID:C_ID + P]
        WNh = put("hidden_w_high", [P, KC, ZCOLS], F32R)
        WNl = put("hidden_w_low", [P, KC, ZCOLS], F32R)
        VWh = put("context_w_high", [P, ZCOLS], F32R)
        VWl = put("context_w_low", [P, ZCOLS], F32R)
        VWD = put("context_w_tail", [STACK, ZCOLS], F32R)
        W2h = put("expert_out_high", [P, EXPERTS * PER, D], F32R)
        W2l = put("expert_out_low", [P, EXPERTS * PER, D], F32R)
        GWh = put("gate_out_high", [P, KC, D], F32R)
        GWl = put("gate_out_low", [P, KC, D], F32R)
        WQh = put("query_w_high", [P, KC, D], F32R)
        WQl = put("query_w_low", [P, KC, D], F32R)
        WPh = put("proj_w_high", [P, GROUPS, D], F32R)
        WPl = put("proj_w_low", [P, GROUPS, D], F32R)
        A = put("score_w", [P, KC, CTX + EXPERTS])
        VR = put("router_context", [P, EXPERTS, CTX])
        RC = put("router_const", [P, EXPERTS])
        RB = put("router_bias", [P, EXPERTS])
        keys_at = at[0]
        KS = put("pair_keys", [KROWS, PAIRS, 2, CTX], F32R)
        KT = put("pair_keys_tail", [KROWS, PAIRS, 4, TAIL], F32R)
        VA = put("head_values", [P, HEADS, 2 * DH])
        VT1 = put("head_values_tail", [4 * TAIL, HEADS, 2 * DH])
        CB = put("expert_bias_out", [P, EXPERTS, D])
        GB = put("gate_b2_row", [P, D])
        BP = put("proj_bias_row", [P, D])
        GAM = put("gamma", [P, KC])
        BET = put("beta", [P, KC])
        CO = put("condition", [P, KC, BATCH])
        COT = put("condition_silu", [P, KC, BATCH])
        BSS = put("modulation_bias", [P, 8])
        MOD = put("modulation", [P, 8, BATCH])
        BQ0 = put("query_bias0", [P, KC])
        BQ = put("query_bias", [P, KC, BATCH])
        BK = put("key_bias", [P, KC])
        RW = put("router_w", [P, 3 * KC, EXPERTS])
        HALF = put("minus_half", [P, NSUB])
        ST0 = put("stats0", [P, NSUB, 6])
        MV0 = put("mean_var0", [P, NSUB, 2])
        RS0 = put("rstd0", [P, NSUB])
        ST1 = put("stats1", [P, NSUB, 6])
        MV1 = put("mean_var1", [P, NSUB, 2])
        RS1 = put("rstd1", [P, NSUB])
        B2T = put("expert_b2_T", [P, KC, EXPERTS])
        WQT = put("score_wq_T", [P, KC, D])
        TC = put("condition_tanh", [P, KC, BATCH])
        ST2 = put("stats2", [P, 2, 6])
        MV2 = put("mean_var2", [P, 2, 2])
        RS2 = put("rstd2", [P, 2])
        SM0 = put("softmax_small", [P, NSUB, 4])
        EV = put("router_dot", [P, NSUB, EXPERTS])
        LG = put("router_logits", [P, NSUB, EXPERTS])
        PR = put("router_probs", [P, NSUB, EXPERTS])
        RT = put("router_small", [P, NSUB, 2])
        MX = put("head_maxima", [P, NSUB, 2, PAIRS])
        tokens_at = at[0]
        X = put("tokens", [P, 2, NSUB, D])
        WQR, WQ1R, GWR, OB, _ = run(keys_at, [
            ("score_wq_raw", [P, KC, D], F32), ("query_w_raw", [P, KC, D], F32),
            ("gate_out_raw", [P, KC, D], F32), ("out_bias_row", [P, D], F32)])
        WPR, _ = run(tokens_at + 4 * NSUB * D, [("proj_w_raw", [P, GROUPS, D], F32)])
        R0 = at[0]
        SH, SL, NXh, NXl, PTh, PTl, PTD, TB, PB, EB, XH0, G, end0 = run(R0, [
            ("hidden_high", [P, RING, TILE], F32R), ("hidden_low", [P, RING, TILE], F32R),
            ("normed_high", [P, KC, TILE], F32R), ("normed_low", [P, KC, TILE], F32R),
            ("probs_T_high", [P, TILE], F32R), ("probs_T_low", [P, TILE], F32R),
            ("probs_T_tail", [P, TILE], F32R),
            ("hidden", [P, 2, TILE], F32), ("probs", [P, 2, D], F32), ("exps", [P, 2, CTX], F32),
            ("x_hat0", [P, NSUB, D], F32), ("gate", [P, NSUB, D], F32)])
        NXf, _ = run(R0, [("normed", [P, KC, TILE], F32)])
        ACC, _ = run(end0 - 2 * 4 * NSUB * D, [("expert_sum", [P, NSUB, D], F32)])
        WS, CX, CXT, KTT, VTT, AN, TF, TH, TL, B1T, WKR, WVR, WSS, end1 = run(R0, [
            ("w_slices", [P, 2, 2 * KC, QN], F32), ("context", [P, 2, D], F32),
            ("context_T", [P, KC, 160], F32), ("keys_T", [P, KC, 160], F32),
            ("values_T", [P, KC, 160], F32), ("anchor_cols", [P, KC, 32], F32),
            ("tail_full", [P, QN], F32), ("tail_high", [P, QN], F32R), ("tail_low", [P, QN], F32R),
            ("hidden_bias", [P, QN], F32), ("wk_raw", [P, KC, D], F32), ("wv_raw", [P, KC, D], F32),
            ("modulation_w", [P, 2, KC, 2 * D], F32)])
        at[0] = max(end0, end1)
        R1 = at[0]
        QS, XH1, XQh, XQl, QH, QL, OD, AH, end2 = run(R1, [
            ("query_stack", [KROWS, PAIRS, TILE], F32R),
            ("x_hat1", [P, NSUB, D], F32), ("query_in_high", [P, KC, TILE], F32R),
            ("query_in_low", [P, KC, TILE], F32R),
            ("queries_high", [P, KC, TILE], F32R), ("queries_low", [P, KC, TILE], F32R),
            ("outs_twice", [P, TILE], F32), ("outs_high", [P, TILE], F32R)])
        NMH, NML, _ = run(end2 - 2 * 4 * TILE, [
            ("max_high", [HEADS, TILE], F32R), ("max_low", [HEADS, TILE], F32R)])
        E, SD, _ = run(R1 + 4 * PAIRS * TILE, [
            ("exp_ring", [P, 5, TILE], F32), ("sums", [P, TILE], F32)])
        AD, _ = run(R1 + 4 * (PAIRS + 6) * TILE, [("attended", [P, GROUPS, TILE], F32R)])
        WNR, W2R, W2T, OW, end3 = run(R1, [
            ("hidden_w_raw", [P, KC, ZCOLS], F32), ("w2_raw", [P, EXPERTS * PER, D], F32),
            ("w2_T", [P, KC, EXPERTS * RH], F32), ("out_w", [P, KC, D], F32)])
        KX, KXR, K1, KMH, KML, VTM, WKV, CX1, XH2, BV, end4 = run(R1, [
            ("ctx_mod_T", [P, KC, 160], F32), ("ctx_tail_rep", [P, KC, 4 * TAIL], F32),
            ("keys1", [P, KC, 160], F32), ("keys1_high", [P, KC, 2, CTX], F32R),
            ("keys1_low", [P, KC, 2, CTX], F32R), ("tail_values", [4 * TAIL, D], F32),
            ("kv_w", [P, KC, 2 * D], F32), ("context1", [P, 2, D], F32), ("x_hat2", [P, 2, D], F32),
            ("value_bias_row", [P, D], F32)])
        at[0] = max(end2, end3, end4)

        steps_of = {}

        def step_sem(engine, stage):
            made = sem(f"{engine}_{stage}")
            steps_of[id(made)] = STEPS[engine][stage]
            return made

        (tensor_setup, tensor_ctx, tensor_w2, tensor_kv, tensor_norm, tensor_att, tensor_z, tensor_p, tensor_query,
         tensor_most, tensor_row, tensor_score, tensor_value, tensor_proj) = (step_sem("tensor", s) for s in STEPS["tensor"])
        (scalar_setup, scalar_ctx, scalar_w2, scalar_kv, scalar_norm, scalar_att, scalar_route, scalar_z, scalar_res,
         scalar_query, scalar_row, scalar_score) = (step_sem("scalar", s) for s in STEPS["scalar"])
        (vector_setup, vector_ctx, vector_w2, vector_kv, vector_norm, vector_att, vector_route, vector_z, vector_evac,
         vector_res, vector_query, vector_most, vector_row, vector_value, vector_proj) = (
            step_sem("vector", s) for s in STEPS["vector"])
        gpsimd_kv, gpsimd_norm, gpsimd_p, gpsimd_query, gpsimd_bias = (step_sem("gpsimd", s) for s in STEPS["gpsimd"])
        vector_results = sem("vector_results")
        consts_loaded = sem("consts_loaded")
        vectors_loaded = sem("vectors_loaded")
        score_w_loaded = sem("score_w_loaded")
        modulation_w_loaded = sem("modulation_w_loaded")
        small_w_loaded = sem("small_w_loaded")
        proj_w_loaded = sem("proj_w_loaded")
        hidden_w_loaded = sem("hidden_w_loaded")
        w2_loaded = sem("w2_loaded")
        x_loaded = sem("x_loaded")
        context_loaded = sem("context_loaded")
        kv_w_loaded = sem("kv_w_loaded")
        hidden_bias_loaded = sem("hidden_bias_loaded")
        slice_even_loaded = sem("slice_even_loaded")
        slice_odd_loaded = sem("slice_odd_loaded")
        tails_placed = sem("tails_placed")
        keys_placed = sem("keys_placed")
        queries_placed = sem("queries_placed")
        maxima_placed = sem("maxima_placed")
        stored = sem("stored")

        def instance(key):
            return key[1] if len(key) == 2 else INSTANCE[key[0]](*key[1:])

        def upto(semaphore, key, step):
            names = steps_of[id(semaphore)]
            return instance(key) * len(names) + names.index(step) + 1

        class Count:
            n = 0

            def one(self):
                self.n += 1
                return 1

        stages = schedule()
        for e in STEPS:
            seen = {}
            for key in stages:
                if key[0] in STEPS[e]:
                    assert instance(key) == seen.get(key[0], 0), (e, key)
                    seen[key[0]] = seen.get(key[0], 0) + 1

        def hidden_columns(lo, hi, rows):
            out_ = []
            if lo < D:
                out_.append((0, min(hi, D) - lo, a["L0_xcond_gate_w1"][rows, lo:min(hi, D)]))
            for e in range(EXPERTS):
                c0 = D + e * RH
                l, h = max(lo, c0), min(hi, c0 + RH)
                if l < h:
                    out_.append((l - lo, h - lo, a["L0_xcond_e_w1"][e, rows, l - c0:h - c0]))
            return out_

        def slices_loaded(b, q):
            each = [2 * len(hidden_columns(i * QN, (i + 1) * QN, slice(0, D))) for i in range(NQ)]
            return b * sum(each[q % 2::2]) + sum(each[q % 2:q + 1:2])

        def hidden_bias(lo, hi):
            out_ = []
            if lo < D:
                out_.append((0, min(hi, D) - lo, a["L0_xcond_gate_b1"][lo:min(hi, D)]))
            for e in range(EXPERTS):
                c0 = D + e * RH
                l, h = max(lo, c0), min(hi, c0 + RH)
                if l < h:
                    out_.append((l - lo, h - lo, a["L0_xcond_e_b1"][e, l - c0:h - c0]))
            return out_

        def feature_rows(w):
            return w.rearrange("(k p) n -> p k n", p=P)

        def columns(v):
            return v.rearrange("(k p) -> p k", p=P)

        def tokens_of(dram, t):
            b, i = t // TPB, t % TPB
            return dram[b, i * TILE:(i + 1) * TILE, :].rearrange("(s p) d -> p s d", p=P)

        def raw(ap):
            return ap.bitcast(F32)

        block = ctx.enter_context(nc.Block())

        @block.sync
        def _(sp):
            def setup(key):
                small = [
                    (GAM[:, :], columns(a["L0_xcond_ln_gamma"])), (BET[:, :], columns(a["L0_xcond_ln_beta"])),
                    (RB[:, :], a["L0_xcond_router_b"].partition_broadcast(P)),
                    (GB[:, :], a["L0_xcond_gate_b2"].partition_broadcast(P)),
                    (BP[:, :], a["L1_xcond_bp"].partition_broadcast(P)),
                    (OB[:, :], a["L0_xcond_out_b"].partition_broadcast(P)),
                    (BSS[:, 0:4], columns(a["L1_xcond_bss_q"])), (BSS[:, 4:8], columns(a["L1_xcond_bss_kv"])),
                    (BQ0[:, :], columns(a["L1_xcond_bq"])), (BK[:, :], columns(a["L1_xcond_bkv"][0:D])),
                ]
                for b in range(BATCH):
                    small.append((CO[:, :, b], columns(a["cond_1024"][b])))
                for e in range(EXPERTS):
                    small.append((B2T[:, :, e], columns(a["L0_xcond_e_b2"][e])))
                small.append((RW[:, :, :], feature_rows(a["L0_xcond_router_W"])))
                assert len(small) == N_VECTORS
                sp.dma_start(CN[:, :], consts).then_inc(consts_loaded, 16)
                sp.dma_start(WQR[:, :, :], feature_rows(a["L0_xcond_Wq"])).then_inc(score_w_loaded, 16)
                for dst, src in small:
                    sp.dma_start(dst, src, allow_slow_non_contiguous=True).then_inc(vectors_loaded, 16)

            def context(key):
                b = key[1]
                if b:
                    sp.wait_ge(tensor_p, upto(tensor_p, ("p", TPB * b - 1, NZ - 1), "p"))
                    sp.wait_ge(vector_res, upto(vector_res, ("res", TPB * b - 1), "x"))
                    sp.wait_ge(gpsimd_p, upto(gpsimd_p, ("p", TPB * b - 1, NZ - 1), "l"))
                sp.dma_start(CX[:, 0, :], a["ctx_1024"][b, 0:P, :]).then_inc(context_loaded, 16)
                sp.dma_start(CX[0:TAIL, 1, :], a["ctx_1024"][b, P:CTX, :]).then_inc(context_loaded, 16)
                sp.dma_start(WKR[:, :, :], feature_rows(a["L0_xcond_Wk"])).then_inc(context_loaded, 16)
                sp.dma_start(WVR[:, :, :], feature_rows(a["L0_xcond_Wv"])).then_inc(context_loaded, 16)
                for q in range(NQ):
                    if q >= 2:
                        sp.wait_ge(tensor_ctx, upto(tensor_ctx, key, f"vw{q - 2}"))
                    for part in range(2):
                        rows = slice((1 + part) * D, (2 + part) * D)
                        for lo, hi, src in hidden_columns(q * QN, (q + 1) * QN, rows):
                            sp.dma_start(WS[:, q % 2, KC * part:KC * part + KC, lo:hi],
                                         feature_rows(src)).then_inc((slice_even_loaded, slice_odd_loaded)[q % 2], 16)
                    if q == 1:
                        sp.wait_ge(vector_ctx, upto(vector_ctx, key, "fill"))
                        for r in range(NQ):
                            for lo, hi, src in hidden_bias(r * QN, (r + 1) * QN):
                                sp.dma_start(B1T[32 * r + TAIL:32 * r + TAIL + 1, lo:hi],
                                             src.partition_broadcast(1)).then_inc(hidden_bias_loaded, 16)
                sp.wait_ge(vector_ctx, upto(vector_ctx, key, "tl"))
                for q in range(NQ):
                    for j, part in enumerate((TH, TH, TL)):
                        sp.dma_start(raw(VWD[32 * j:32 * j + 32, q * QN:(q + 1) * QN]),
                                     raw(part[32 * q:32 * q + 32, :])).then_inc(tails_placed, 16)

            def kv(key):
                b = key[1]
                if b:
                    sp.wait_ge(tensor_proj, upto(tensor_proj, ("proj", TPB * b - 1), "o1"))
                    sp.wait_ge(vector_proj, upto(vector_proj, ("proj", TPB * b - 1), "o1"))
                else:
                    sp.wait_ge(tensor_w2, upto(tensor_w2, ("w2", 0), "cb"))
                    sp.wait_ge(vector_w2, upto(vector_w2, ("w2", 0), "cb"))
                    sp.wait_ge(scalar_setup, upto(scalar_setup, ("setup", 0), "wp"))
                    sp.wait_ge(vector_setup, upto(vector_setup, ("setup", 0), "wp"))
                sp.dma_start(CX1[:, 0, :], a["ctx_1024"][b, 0:P, :]).then_inc(kv_w_loaded, 16)
                sp.dma_start(CX1[0:TAIL, 1, :], a["ctx_1024"][b, P:CTX, :]).then_inc(kv_w_loaded, 16)
                sp.dma_start(WKV[:, :, :], feature_rows(a["L1_xcond_Wkv"])).then_inc(kv_w_loaded, 16)
                sp.dma_start(BV[:, :], a["L1_xcond_bkv"][D:2 * D].partition_broadcast(P)).then_inc(kv_w_loaded, 16)
                if b == 0:
                    sp.dma_start(X[:, 1, :, :], tokens_of(a["x"], 1)).then_inc(x_loaded, 16)
                sp.wait_ge(vector_kv, upto(vector_kv, key, "kl"))
                for c in range(PAIRS):
                    f, r = c // 4, 32 * (c % 4)
                    for j, part in enumerate((KMH, KMH, KML)):
                        sp.dma_start(raw(KS[32 * j:32 * j + 32, c, :, :]),
                                     raw(part[r:r + 32, f, :, :])).then_inc(keys_placed, 16)

            def query(key):
                t = key[1]
                if t:
                    sp.wait_ge(tensor_score, upto(tensor_score, ("score", t - 1, GROUPS - 1), "s4"))
                for f in range(KC):
                    sp.wait_ge(scalar_query, upto(scalar_query, key, f"q{f}"))
                    sp.wait_ge(vector_query, upto(vector_query, key, f"q{f}"))
                    for c in range(4 * f, 4 * f + 4):
                        r = 32 * (c % 4)
                        for j, part in enumerate((QH, QL, QH)):
                            sp.dma_start(raw(QS[32 * j:32 * j + 32, c, :]),
                                         raw(part[r:r + 32, f, :])).then_inc(queries_placed, 16)

            def row(key):
                sp.wait_ge(scalar_row, upto(scalar_row, key, "h"))
                sp.wait_ge(vector_row, upto(vector_row, key, "l"))
                for j in range(2):
                    for i, part in enumerate((NMH, NML)):
                        dst = STACK + 2 * i + j
                        sp.dma_start(raw(QS[dst:dst + 1, :, :]),
                                     raw(part[PAIRS * j:PAIRS * j + PAIRS, :])).then_inc(maxima_placed, 16)

            def proj(key):
                t = key[1]
                for h in range(2):
                    sp.wait_ge(vector_proj, upto(vector_proj, key, f"o{h}"))
                    sp.dma_start(tokens_of(out, t)[:, 2 * h:2 * h + 2, :],
                                 X[:, t % 2, 2 * h:2 * h + 2, :]).then_inc(stored, 16)
                sp.wait_ge(stored, 32 * (t + 1))
                if t + 2 < NT:
                    sp.dma_start(X[:, t % 2, :, :], tokens_of(a["x"], t + 2)).then_inc(x_loaded, 16)

            parts = {"setup": setup, "ctx": context, "kv": kv, "query": query, "row": row, "proj": proj}
            for key in stages:
                if key[0] in parts:
                    parts[key[0]](key)

        @block.scalar
        def _(act):
            def setup(key):
                act.dma_start(WNR[:, :, 0:D], feature_rows(a["L0_xcond_gate_w1"][0:D, :])).then_inc(hidden_w_loaded, 16)
                for e in range(EXPERTS):
                    act.dma_start(WNR[:, :, D + e * RH:D + (e + 1) * RH],
                                  feature_rows(a["L0_xcond_e_w1"][e, 0:D, :])).then_inc(hidden_w_loaded, 16)
                act.dma_start(X[:, 0, :, :], tokens_of(a["x"], 0)).then_inc(x_loaded, 16)
                for e in range(EXPERTS):
                    act.dma_start(W2R[:, PER * e:PER * e + PER, :],
                                  feature_rows(a["L0_xcond_e_w2"][e])).then_inc(w2_loaded, 16)
                act.dma_start(OW[:, :, :], feature_rows(a["L0_xcond_out_w"])).then_inc(w2_loaded, 16)
                act.dma_start(GWR[:, :, :], feature_rows(a["L0_xcond_gate_w2"])).then_inc(small_w_loaded, 16)
                act.dma_start(WQ1R[:, :, :], feature_rows(a["L1_xcond_Wq"])).then_inc(small_w_loaded, 16)
                act.dma_start(WSS[:, 0, :, :], feature_rows(a["L1_xcond_Wss_q"])).then_inc(modulation_w_loaded, 16)
                act.dma_start(WSS[:, 1, :, :], feature_rows(a["L1_xcond_Wss_kv"])).then_inc(modulation_w_loaded, 16)
                heads = a["L1_xcond_Wp"].rearrange("(g i r) n -> i r g n", i=4, r=DH)
                for i in range(4):
                    for twice in range(2):
                        r = 32 * i + DH * twice
                        act.dma_start(WPR[r:r + DH, :, :], heads[i]).then_inc(proj_w_loaded, 16)
                act.wait_ge(vectors_loaded, 16 * N_VECTORS)
                nc.scalar.activation(TC[:, :, :], CO[:, :, :], ACT.Tanh, scale=0.5).then_inc(scalar_setup, 1)
                act.wait_ge(tensor_setup, upto(tensor_setup, key, "wqT"))
                nc.scalar.copy(WQT[:, :, :], V0[:, :].rearrange("p (k n) -> p k n", k=KC)).then_inc(scalar_setup, 1)
                act.wait_ge(hidden_w_loaded, 16 * 4)
                nc.scalar.copy(WNh[:, :, :], WNR[:, :, :]).then_inc(scalar_setup, 1)
                act.wait_ge(small_w_loaded, 16 * 2)
                nc.scalar.copy(GWh[:, :, :], GWR[:, :, :]).then_inc(scalar_setup, 1)
                nc.scalar.copy(WQh[:, :, :], WQ1R[:, :, :]).then_inc(scalar_setup, 1)
                act.wait_ge(proj_w_loaded, 16 * 8)
                nc.scalar.copy(WPh[:, :, :], WPR[:, :, :]).then_inc(scalar_setup, 1)

            def context(key):
                b = key[1]
                act.wait_ge(tensor_ctx, upto(tensor_ctx, key, "ctxT"))
                nc.scalar.copy(CXT[:, :, 0:CTX], M0[:, 0:320].rearrange("p (k n) -> p k n", k=KC)[:, :, 0:CTX]).then_inc(scalar_ctx, 1)
                act.wait_ge(tensor_ctx, upto(tensor_ctx, key, "vT"))
                nc.scalar.copy(VTT[:, :, 0:CTX], Z[:, 1, 0:320].rearrange("p (k n) -> p k n", k=KC)[:, :, 0:CTX]).then_inc(scalar_ctx, 1)
                act.wait_ge(tensor_ctx, upto(tensor_ctx, key, "A"))
                nc.scalar.mul(A[:, :, 0:CTX], V0[:, 0:320].rearrange("p (k n) -> p k n", k=KC)[:, :, 0:CTX],
                                     float(D) ** -0.5).then_inc(scalar_ctx, 1)
                for q in range(NQ):
                    act.wait_ge(tensor_ctx, upto(tensor_ctx, key, f"vw{q}"))
                    nc.scalar.copy(VWh[:, q * QN:(q + 1) * QN], Z[:, q % 2, 0:QN]).then_inc(scalar_ctx, 1)

            def w2(key):
                for i in range(6):
                    act.wait_ge(tensor_w2, upto(tensor_w2, key, f"t{i}"))
                    nc.scalar.copy(W2T[:, i // 3, (i % 3) * 512:(i % 3 + 1) * 512], S[:, i % 2, :]).then_inc(scalar_w2, 1)
                for j in range(6):
                    act.wait_ge(tensor_w2, upto(tensor_w2, key, f"m{j}"))
                    nc.scalar.mul(W2h[:, 2 * j:2 * j + 2, :], S[:, j % 2, :].rearrange("p (k n) -> p k n", k=2),
                                         0.5).then_inc(scalar_w2, 1)

            def kv(key):
                b = key[1]
                act.wait_ge(tensor_kv, upto(tensor_kv, key, "xT"))
                for m in range(KC):
                    nc.scalar.activation(KX[:, m, 0:CTX], V0[:, 160 * m:160 * m + CTX], ACT.Identity,
                                                scale=MOD[:, 4 + m, b:b + 1], bias=MOD[:, 6 + m, b:b + 1]).then_inc(scalar_kv, 1)

            def norm(key):
                t = key[1]
                if t:
                    act.wait_ge(tensor_p, upto(tensor_p, ("p", t - 1, NZ - 1), "p"))
                for m in range(KC):
                    act.wait_ge(tensor_norm, upto(tensor_norm, key, f"t{m}"))
                    nc.scalar.activation(NXf[:, m, :], Z[:, m, :], ACT.Identity, scale=GAM[:, m:m + 1],
                                                bias=BET[:, m:m + 1]).then_inc(scalar_norm, 1)

            def att(key):
                t, s = key[1:]
                act.wait_ge(vector_att, upto(vector_att, key, "max"))
                if s >= 2:
                    act.wait_ge(vector_att, upto(vector_att, ("att", t, s - 2), "lg"))
                nc.scalar.activation(EB[:, s % 2, :], O[:, 2 * (s % 2), 0:CTX], ACT.Exp,
                                            bias=SM0[:, s, 0:1], accum_out=SM0[:, s, 1:2]).then_inc(scalar_att, 1)

            def route(key):
                t = key[1]
                act.wait_ge(tensor_att, upto(tensor_att, ("att", t, NSUB - 1), "p"))
                nc.scalar.copy(PTh[:, :], Z[:, 0, :]).then_inc(scalar_route, 1)
                nc.scalar.copy(PTD[0:STACK, :], Z[0:STACK, 1, :]).then_inc(scalar_route, 1)
                act.wait_ge(vector_route, upto(vector_route, key, "lg"))
                nc.scalar.activation(PR[:, :, :], LG[:, :, :], ACT.Exp).then_inc(scalar_route, 1)

            def hidden(key):
                t, k = key[1:]
                g = NZ * t + k
                act.wait_ge(tensor_z, upto(tensor_z, key, "z"))
                if g >= 2:
                    act.wait_ge(gpsimd_p, upto(gpsimd_p, ("p", (g - 2) // NZ, (g - 2) % NZ), "l"))
                nc.scalar.activation(TB[:, k % 2, :], Z[:, k % 2, :], ACT.Tanh, scale=0.5).then_inc(scalar_z, 1)
                act.wait_ge(vector_z, upto(vector_z, key, "s"))
                if g >= RING:
                    act.wait_ge(tensor_p, upto(tensor_p, ("p", (g - RING) // NZ, (g - RING) % NZ), "p"))
                nc.scalar.copy(SH[:, k % RING, :], TB[:, k % 2, :]).then_inc(scalar_z, 1)

            def res(key):
                t = key[1]
                act.wait_ge(vector_evac, upto(vector_evac, ("evac", t, 0), "o"))
                nc.scalar.activation(G[:, :, :], G[:, :, :], ACT.Tanh, scale=0.5).then_inc(scalar_res, 1)

            def query(key):
                t = key[1]
                b = t // TPB
                for m in range(KC):
                    act.wait_ge(tensor_query, upto(tensor_query, key, f"t{m}"))
                    nc.scalar.mul(XQh[:, m, :], S[:, m, :], MOD[:, m, b:b + 1]).then_inc(scalar_query, 1)
                for f in range(KC):
                    act.wait_ge(tensor_query, upto(tensor_query, key, f"q{f}"))
                    if t:
                        act.wait_ge(tensor_proj, upto(tensor_proj, ("proj", t - 1), "o1"))
                    nc.scalar.activation(QH[:, f, :], (V0[:, :], S[:, 0, :])[f], ACT.Identity,
                                                bias=BQ[:, f, b:b + 1]).then_inc(scalar_query, 1)

            def row(key):
                t = key[1]
                act.wait_ge(tensor_row, upto(tensor_row, key, "m"))
                if t:
                    act.wait_ge(vector_value, upto(vector_value, ("value", t - 1, GROUPS - 1), "a"))
                nc.scalar.mul(NMH[:, :], V0[0:HEADS, :], -1.0).then_inc(scalar_row, 1)

            def score(key):
                t, g = key[1:]
                if g:
                    act.wait_ge(tensor_value, upto(tensor_value, ("value", t, g - 1), "v"))
                for i in range(5):
                    act.wait_ge(tensor_score, upto(tensor_score, key, f"s{i}"))
                    rows = P if i < 4 else 4 * TAIL
                    nc.scalar.activation(E[0:rows, i, :], S[0:rows, (5 * g + i) % 2, :], ACT.Exp).then_inc(scalar_score, 1)

            parts = {"setup": setup, "ctx": context, "w2": w2, "kv": kv, "norm": norm, "att": att,
                     "route": route, "z": hidden, "res": res, "query": query, "row": row, "score": score}
            for key in stages:
                if key[0] in parts:
                    parts[key[0]](key)

        @block.vector
        def _(dve):
            v = nc.vector
            results = Count()

            def normal_form(key, own_sem, rstd_sem, chunks, stats, mean_var, rstd, source, dst):
                for s, rows in chunks:
                    v.bn_stats(stats[0:rows, s, :], source(s, rows)).then_inc(vector_results, results.one())
                    
                dve.wait_ge(vector_results, results.n)
                for s, rows in chunks:
                    v.bn_aggr(mean_var[0:rows, s, :], stats[0:rows, s, :]).then_inc(vector_results, results.one())
                dve.wait_ge(vector_results, results.n)
                v.tensor_scalar(mean_var[:, :, 1], mean_var[:, :, 1], EPS, None, ALU.add).then_inc(own_sem, 1)
                dve.wait_ge(rstd_sem, upto(rstd_sem, key, "rstd"))
                for s, rows in chunks:
                    last = v.tensor_scalar(dst[0:rows, s, :], source(s, rows), mean_var[0:rows, s, 0:1],
                                           rstd[0:rows, s:s + 1], ALU.subtract, ALU.mult)
                last.then_inc(own_sem, 1)

            def split_low(dst, full, high):
                return v.tensor_tensor(dst, full, raw(high), ALU.subtract)

            def setup(key):
                v.memset(HALF[:, :], -0.5)
                v.memset(MV2[:, :, :], 1.0)
                v.memset(KT[:, :, :, :].bitcast(F32), 0.0)
                v.memset(VA[:, :, DH:2 * DH], 1.0)
                v.memset(VT1[:, :, :], 0.0).then_inc(vector_results, results.one())
                dve.wait_ge(consts_loaded, 16 * 1)
                dve.wait_ge(vector_results, results.n)
                for i in range(4):
                    v.tensor_scalar(VT1[:, i::4, DH:2 * DH], VT1[:, i::4, DH:2 * DH],
                                          CN[0:4 * TAIL, C_ROW + i:C_ROW + i + 1], None, ALU.add).then_inc(vector_results, results.one())
                v.memset(RT[:, :, :], 0.0).then_inc(vector_setup, 1)
                dve.wait_ge(scalar_setup, upto(scalar_setup, key, "tc"))
                v.scalar_tensor_tensor(out=COT[:, :, :], in0=TC[:, :, :], scalar=1.0, in1=CO[:, :, :],
                                              op0=ALU.add, op1=ALU.mult).then_inc(vector_setup, 1)
                dve.wait_ge(tensor_setup, upto(tensor_setup, key, "mod"))
                dve.wait_ge(vectors_loaded, 16 * N_VECTORS)
                v.scalar_tensor_tensor(out=MOD[:, :, :], in0=V0[:, 0:8 * BATCH].rearrange("p (m b) -> p m b", m=8),
                                             scalar=0.5, in1=BSS[:, :].unsqueeze(2).to_broadcast([P, 8, BATCH]),
                                             op0=ALU.mult, op1=ALU.add).then_inc(vector_results, results.one())
                dve.wait_ge(vector_results, results.n)
                v.tensor_scalar(MOD[:, 0:2, :], MOD[:, 0:2, :], 1.0, None, ALU.add).then_inc(vector_results, results.one())
                v.tensor_scalar(MOD[:, 4:6, :], MOD[:, 4:6, :], 1.0, None, ALU.add).then_inc(vector_setup, 1)
                dve.wait_ge(tensor_setup, upto(tensor_setup, key, "bq"))
                v.tensor_tensor(BQ[:, :, :], V0[:, 64:64 + KC * BATCH].rearrange("p (f b) -> p f b", f=KC),
                                       BQ0[:, :].unsqueeze(2).to_broadcast([P, KC, BATCH]), ALU.add).then_inc(vector_setup, 1)
                for step, low, full, high in (("wn", WNl, WNR, WNh), ("gw", GWl, GWR, GWh),
                                              ("wq", WQl, WQ1R, WQh), ("wp", WPl, WPR, WPh)):
                    dve.wait_ge(scalar_setup, upto(scalar_setup, key, step))
                    split_low(low[:, :, :], full[:, :, :], high[:, :, :]).then_inc(vector_setup, 1)

            def context(key):
                b = key[1]
                if b:
                    dve.wait_ge(tensor_p, upto(tensor_p, ("p", TPB * b - 1, NZ - 1), "p"))
                    dve.wait_ge(gpsimd_p, upto(gpsimd_p, ("p", TPB * b - 1, NZ - 1), "l"))
                v.memset(B1T[:, :], 0.0)
                v.memset(AN[:, :, :], 0.0)
                v.memset(VTT[:, :, CTX:160], 0.0).then_inc(vector_results, results.one())
                dve.wait_ge(vectors_loaded, 16 * N_VECTORS)
                dve.wait_ge(vector_results, results.n)
                v.tensor_copy(AN[:, :, TAIL:TAIL + 1], CO[:, :, b:b + 1]).then_inc(vector_ctx, 1)
                dve.wait_ge(tensor_ctx, upto(tensor_ctx, key, "kT"))
                v.tensor_copy(KTT[:, :, 0:CTX], Z[:, 0, 0:320].rearrange("p (k n) -> p k n", k=KC)[:, :, 0:CTX]).then_inc(vector_ctx, 1)
                dve.wait_ge(tensor_ctx, upto(tensor_ctx, key, "VR"))
                v.tensor_copy(VR[:, :, :], S[:, 0, 0:480].rearrange("p (e n) -> p e n", e=EXPERTS)[:, :, 0:CTX]).then_inc(vector_ctx, 1)
                dve.wait_ge(tensor_ctx, upto(tensor_ctx, key, "RC"))
                v.tensor_copy(A[:, :, CTX:CTX + EXPERTS], RW[:, 0:KC, :])
                v.tensor_tensor(RC[:, :], S[:, 1, 0:EXPERTS], RB[:, :], ALU.add).then_inc(vector_ctx, 1)
                for q in range(NQ):
                    dve.wait_ge(scalar_ctx, upto(scalar_ctx, key, f"vw{q}"))
                    v.tensor_tensor(VWl[:, q * QN:(q + 1) * QN], Z[:, q % 2, 0:QN],
                                           raw(VWh[:, q * QN:(q + 1) * QN]), ALU.subtract).then_inc(vector_ctx, 1)
                dve.wait_ge(hidden_bias_loaded, 16 * (N_HIDDEN_BIAS * (b + 1)))
                v.tensor_tensor(TF[:, :], M0[:, 0:QN], B1T[:, :], ALU.add).then_inc(vector_results, results.one())
                dve.wait_ge(vector_results, results.n)
                v.tensor_copy(TH[:, :], TF[:, :]).then_inc(vector_ctx, 1)
                dve.wait_ge(vector_ctx, upto(vector_ctx, key, "th"))
                split_low(TL[:, :], TF[:, :], TH[:, :]).then_inc(vector_ctx, 1)

            def w2(key):
                for j in range(6):
                    dve.wait_ge(scalar_w2, upto(scalar_w2, key, f"m{j}"))
                    v.scalar_tensor_tensor(out=W2l[:, 2 * j:2 * j + 2, :].rearrange("p k n -> p (k n)"),
                                                  in0=S[:, j % 2, :], scalar=0.5,
                                                  in1=raw(W2h[:, 2 * j:2 * j + 2, :]).rearrange("p k n -> p (k n)"),
                                                  op0=ALU.mult, op1=ALU.subtract).then_inc(vector_w2, 1)
                dve.wait_ge(tensor_w2, upto(tensor_w2, key, "cb"))
                v.tensor_tensor(CB[:, :, :], O[:, 0:EXPERTS, :], OB[:, :].unsqueeze(1).to_broadcast([P, EXPERTS, D]),
                                       ALU.add).then_inc(vector_w2, 1)

            def kv(key):
                b = key[1]
                dve.wait_ge(kv_w_loaded, 16 * (4 * (b + 1)))
                normal_form(key, vector_kv, gpsimd_kv, [(0, P), (1, TAIL)], ST2, MV2, RS2, lambda s, rows: CX1[0:rows, s, :], XH2)
                for m in range(KC):
                    dve.wait_ge(scalar_kv, upto(scalar_kv, key, f"x{m}"))
                    last = v.tensor_copy(KXR[:, m, :].rearrange("p (i n) -> p i n", i=4),
                                         KX[:, m, P:CTX].unsqueeze(1).to_broadcast([P, 4, TAIL]))
                last.then_inc(vector_kv, 1)
                dve.wait_ge(tensor_kv, upto(tensor_kv, key, "k"))
                for f in range(KC):
                    last = v.tensor_scalar(K1[:, f, 0:CTX], S[:, 0, 160 * f:160 * f + CTX], BK[:, f:f + 1],
                                           float(DH) ** -0.5, ALU.add, ALU.mult)
                last.then_inc(vector_kv, 1)
                dve.wait_ge(vector_kv, upto(vector_kv, key, "k"))
                for f in range(KC):
                    for j in range(2):
                        last = v.tensor_scalar(KMH[:, f, j, :], K1[:, f, 0:CTX], CN[:, C_HEAD + j:C_HEAD + j + 1],
                                               None, ALU.mult)
                last.then_inc(vector_kv, 1)
                dve.wait_ge(vector_kv, upto(vector_kv, key, "kh"))
                for f in range(KC):
                    for j in range(2):
                        last = v.scalar_tensor_tensor(out=KML[:, f, j, :], in0=K1[:, f, 0:CTX],
                                                      scalar=CN[:, C_HEAD + j:C_HEAD + j + 1],
                                                      in1=raw(KMH[:, f, j, :]), op0=ALU.mult, op1=ALU.subtract)
                last.then_inc(vector_kv, 1)
                v.memset(KS[STACK:KROWS, :, :, :].bitcast(F32), 1.0).then_inc(vector_results, results.one())
                dve.wait_ge(vector_results, results.n)
                for j in range(2):
                    last = v.tensor_scalar(KS[STACK:KROWS, :, j, :], raw(KS[STACK:KROWS, :, j, :]),
                                           CN[STACK:KROWS, C_PAIR + j:C_PAIR + j + 1], None, ALU.mult)
                last.then_inc(vector_kv, 1)
                dve.wait_ge(keys_placed, 16 * 3 * PAIRS * (b + 1))
                dve.wait_ge(vector_kv, upto(vector_kv, key, "ones"))
                for j in range(2):
                    last = v.tensor_copy(KT[:, j::2, 2 * j:2 * j + 2, :], raw(KS[:, j::2, :, P:CTX]))
                last.then_inc(vector_kv, 1)
                dve.wait_ge(tensor_kv, upto(tensor_kv, key, "v"))
                v.tensor_tensor(VA[:, :, 0:DH], S[:, 1, 0:D].rearrange("p (h r) -> p h r", r=DH),
                                       BV[:, :].rearrange("p (h r) -> p h r", r=DH), ALU.add).then_inc(vector_kv, 1)
                dve.wait_ge(tensor_kv, upto(tensor_kv, key, "vt"))
                v.tensor_tensor(VTM[:, :], V0[0:4 * TAIL, 0:D], BV[0:4 * TAIL, :], ALU.add).then_inc(vector_results, results.one())
                dve.wait_ge(vector_results, results.n)
                for i in range(4):
                    last = v.tensor_scalar(VT1[:, i::4, 0:DH], VTM[:, :].rearrange("p (h r) -> p h r", r=DH)[:, i::4, :],
                                           CN[0:4 * TAIL, C_ROW + i:C_ROW + i + 1], None, ALU.mult)
                last.then_inc(vector_kv, 1)

            def norm(key):
                t = key[1]
                dve.wait_ge(x_loaded, 16 * (t + 1))
                if t:
                    dve.wait_ge(tensor_p, upto(tensor_p, ("p", t - 1, NZ - 1), "p"))
                    dve.wait_ge(gpsimd_p, upto(gpsimd_p, ("p", t - 1, NZ - 1), "l"))
                    dve.wait_ge(vector_results, results.n)
                    dve.wait_ge(vector_res, upto(vector_res, ("res", t - 1), "x"))
                if t % TPB == 0:
                    dve.wait_ge(tensor_ctx, upto(tensor_ctx, ("ctx", t // TPB), "vw3"))
                    dve.wait_ge(tails_placed, 16 * 3 * NQ * (t // TPB + 1))
                    v.memset(PB[:, :, P:D], 0.0).then_inc(vector_results, results.one())
                    dve.wait_ge(vector_results, results.n)
                    v.memset(PB[:, :, P:P + 3 * 32].rearrange("p r (j n) -> p r j n", j=3)[:, :, :, TAIL:TAIL + 1], 1.0).then_inc(vector_results, results.one())
                normal_form(key, vector_norm, gpsimd_norm, [(s, P) for s in range(NSUB)], ST0, MV0, RS0, lambda s, rows: X[:, t % 2, s, :], XH0)
                for m in range(KC):
                    dve.wait_ge(scalar_norm, upto(scalar_norm, key, f"n{m}"))
                    v.tensor_copy(NXh[:, m, :], NXf[:, m, :]).then_inc(vector_results, results.one())
                    dve.wait_ge(vector_results, results.n)
                    split_low(NXl[:, m, :], NXf[:, m, :], NXh[:, m, :]).then_inc(vector_norm, 1)

            def att(key):
                t, s = key[1:]
                bank = O[:, 2 * (s % 2), :]
                dve.wait_ge(tensor_att, upto(tensor_att, key, "s"))
                v.tensor_reduce(SM0[:, s, 0:1], bank[:, 0:CTX], AX.X, ALU.max, negate=True).then_inc(vector_att, 1)
                dve.wait_ge(scalar_att, upto(scalar_att, key, "e"))
                v.reciprocal(SM0[:, s, 2:3], SM0[:, s, 1:2]).then_inc(vector_results, results.one())
                dve.wait_ge(vector_results, results.n)
                if s >= 2:
                    dve.wait_ge(tensor_att, upto(tensor_att, ("att", t, s - 2), "p"))
                v.tensor_scalar(PB[:, s % 2, 0:P], EB[:, s % 2, 0:P], SM0[:, s, 2:3], None, ALU.mult)
                v.tensor_scalar(PB[:, s % 2, P:P + 3 * 32].rearrange("p (j n) -> p j n", j=3)[:, :, 0:TAIL],
                                       EB[:, s % 2, P:CTX].unsqueeze(1).to_broadcast([P, 3, TAIL]),
                                       SM0[:, s, 2:3], None, ALU.mult).then_inc(vector_att, 1)
                v.tensor_tensor(LG[:, s, :], bank[:, CTX:CTX + EXPERTS], RC[:, :], ALU.add).then_inc(vector_results, results.one())
                for e in range(EXPERTS):
                    v.scalar_tensor_tensor(out=TB[:, 0, e * CTX:(e + 1) * CTX], in0=EB[:, s % 2, :], scalar=SM0[:, s, 2:3],
                                                 in1=VR[:, e, :], op0=ALU.mult, op1=ALU.mult,
                                                 accum_out=EV[:, s, e:e + 1]).then_inc(vector_results, results.one())
                dve.wait_ge(vector_results, results.n)
                v.tensor_tensor(LG[:, s, :], LG[:, s, :], EV[:, s, :], ALU.add).then_inc(vector_att, 1)

            def route(key):
                t = key[1]
                dve.wait_ge(vector_att, upto(vector_att, ("att", t, NSUB - 1), "lg"))
                dve.wait_ge(scalar_route, upto(scalar_route, key, "pm"))
                v.tensor_tensor(PTl[:, :], Z[:, 0, :], raw(PTh[:, :]), ALU.subtract).then_inc(vector_route, 1)
                dve.wait_ge(scalar_route, upto(scalar_route, key, "pd"))
                v.tensor_tensor(PTD[32:64, :], Z[32:64, 1, :], raw(PTD[32:64, :]), ALU.subtract).then_inc(vector_route, 1)
                v.tensor_reduce(RT[:, :, 0], LG[:, :, :], AX.X, ALU.max).then_inc(vector_results, results.one())
                dve.wait_ge(vector_results, results.n)
                v.tensor_tensor(LG[:, :, :], LG[:, :, :], RT[:, :, 0:1].to_broadcast([P, NSUB, EXPERTS]),
                                       ALU.subtract).then_inc(vector_route, 1)
                dve.wait_ge(scalar_route, upto(scalar_route, key, "ex"))
                v.tensor_reduce(RT[:, :, 0], PR[:, :, :], AX.X, ALU.add).then_inc(vector_results, results.one())
                dve.wait_ge(vector_results, results.n)
                v.reciprocal(RT[:, :, 1], RT[:, :, 0]).then_inc(vector_results, results.one())
                dve.wait_ge(vector_results, results.n)
                v.tensor_tensor(PR[:, :, :], PR[:, :, :], RT[:, :, 1:2].to_broadcast([P, NSUB, EXPERTS]),
                                       ALU.mult).then_inc(vector_route, 1)
                dve.wait_ge(vector_route, upto(vector_route, key, "prob"))
                for e in range(EXPERTS):
                    for s in range(NSUB):
                        if e == 0:
                            last = v.tensor_scalar(ACC[:, s, :], CB[:, 0, :], PR[:, s, 0:1], None, ALU.mult)
                        else:
                            last = v.scalar_tensor_tensor(out=ACC[:, s, :], in0=CB[:, e, :], scalar=PR[:, s, e:e + 1],
                                                          in1=ACC[:, s, :], op0=ALU.mult, op1=ALU.add)
                        if (e, s) != (EXPERTS - 1, NSUB - 1):
                            last.then_inc(vector_results, results.one())
                    if e < EXPERTS - 1:
                        dve.wait_ge(vector_results, results.n)
                last.then_inc(vector_route, 1)

            def hidden(key):
                t, k = key[1:]
                dve.wait_ge(scalar_z, upto(scalar_z, key, "t"))
                v.scalar_tensor_tensor(out=TB[:, k % 2, :], in0=TB[:, k % 2, :], scalar=1.0, in1=Z[:, k % 2, :],
                                              op0=ALU.add, op1=ALU.mult).then_inc(vector_z, 1)

            def evac(key):
                t, j = key[1:]
                if j == 0:
                    dve.wait_ge(tensor_p, upto(tensor_p, ("p", t, GATES - 1), "p"))
                    v.scalar_tensor_tensor(out=G[:, :, :], in0=O[:, :, :], scalar=0.5,
                                                  in1=GB[:, :].unsqueeze(1).to_broadcast([P, NSUB, D]),
                                                  op0=ALU.mult, op1=ALU.add).then_inc(vector_evac, 1)
                    return
                dve.wait_ge(tensor_p, upto(tensor_p, ("p", t, GATES + PER * j - 1), "p"))
                if j == 1:
                    dve.wait_ge(vector_route, upto(vector_route, ("route", t), "acc"))
                else:
                    dve.wait_ge(vector_evac, upto(vector_evac, ("evac", t, j - 1), "o"))
                for s in range(NSUB):
                    last = v.scalar_tensor_tensor(out=ACC[:, s, :], in0=O[:, s, :], scalar=PR[:, s, j - 1:j],
                                                  in1=ACC[:, s, :], op0=ALU.mult, op1=ALU.add)
                last.then_inc(vector_evac, 1)

            def res(key):
                t = key[1]
                dve.wait_ge(scalar_res, upto(scalar_res, key, "t"))
                dve.wait_ge(vector_evac, upto(vector_evac, ("evac", t, EXPERTS), "o"))
                v.scalar_tensor_tensor(out=ACC[:, :, :], in0=G[:, :, :], scalar=1.0, in1=ACC[:, :, :],
                                              op0=ALU.add, op1=ALU.mult).then_inc(vector_res, 1)
                dve.wait_ge(vector_res, upto(vector_res, key, "u"))
                v.scalar_tensor_tensor(out=X[:, t % 2, :, :], in0=ACC[:, :, :], scalar=0.5,
                                              in1=X[:, t % 2, :, :], op0=ALU.mult, op1=ALU.add).then_inc(vector_res, 1)

            def query(key):
                t = key[1]
                b = t // TPB
                dve.wait_ge(vector_res, upto(vector_res, ("res", t), "x"))
                if t:
                    dve.wait_ge(tensor_value, upto(tensor_value, ("value", t - 1, GROUPS - 1), "v"))
                if t % TPB == 0:
                    dve.wait_ge(tensor_kv, upto(tensor_kv, ("kv", b), "vt"))
                normal_form(key, vector_query, gpsimd_query, [(s, P) for s in range(NSUB)], ST1, MV1, RS1, lambda s, rows: X[:, t % 2, s, :], XH1)
                for m in range(KC):
                    dve.wait_ge(scalar_query, upto(scalar_query, key, f"x{m}"))
                    v.scalar_tensor_tensor(out=XQl[:, m, :], in0=S[:, m, :], scalar=MOD[:, m, b:b + 1],
                                                  in1=raw(XQh[:, m, :]), op0=ALU.mult, op1=ALU.subtract).then_inc(vector_query, 1)
                for f in range(KC):
                    dve.wait_ge(scalar_query, upto(scalar_query, key, f"q{f}"))
                    v.scalar_tensor_tensor(out=QL[:, f, :], in0=(V0[:, :], S[:, 0, :])[f],
                                                  scalar=BQ[:, f, b:b + 1], in1=raw(QH[:, f, :]),
                                                  op0=ALU.add, op1=ALU.subtract).then_inc(vector_query, 1)

            def most(key):
                t, s = key[1:]
                for c in range(PAIRS):
                    dve.wait_ge(tensor_most, upto(tensor_most, key, f"c{c}"))
                    v.tensor_reduce(MX[:, s, :, c], S[:, c % 2, 0:2 * CTX].rearrange("p (j n) -> p j n", j=2),
                                           AX.X, ALU.max).then_inc(vector_most, 1)

            def row(key):
                dve.wait_ge(scalar_row, upto(scalar_row, key, "h"))
                v.scalar_tensor_tensor(out=NML[:, :], in0=V0[0:HEADS, :], scalar=-1.0, in1=raw(NMH[:, :]),
                                              op0=ALU.mult, op1=ALU.subtract).then_inc(vector_row, 1)

            def value(key):
                t, g = key[1:]
                dve.wait_ge(tensor_value, upto(tensor_value, key, "v"))
                if g == 0:
                    dve.wait_ge(maxima_placed, 16 * 4 * (t + 1))
                dve.wait_ge(vector_results, results.n)
                if g:
                    dve.wait_ge(vector_value, upto(vector_value, ("value", t, g - 1), "a"))
                v.stream_shuffle(OD[:, :], V0[:, :], [i % DH for i in range(32)]).then_inc(vector_results, results.one())
                v.stream_shuffle(SD[:, :], V0[:, :], [DH + i % DH for i in range(32)]).then_inc(vector_value, 1)
                dve.wait_ge(vector_value, upto(vector_value, key, "take"))
                v.reciprocal(SD[:, :], SD[:, :]).then_inc(vector_results, results.one())
                dve.wait_ge(vector_results, results.n)
                v.tensor_tensor(OD[:, :], OD[:, :], SD[:, :], ALU.mult).then_inc(vector_results, results.one())
                dve.wait_ge(vector_results, results.n)
                v.tensor_copy(AH[:, :], OD[:, :]).then_inc(vector_results, results.one())
                dve.wait_ge(vector_results, results.n)
                v.scalar_tensor_tensor(out=AD[:, g, :], in0=raw(AH[:, :]), scalar=CN[:, C_SPLIT:C_SPLIT + 1],
                                              in1=OD[:, :], op0=ALU.mult, op1=ALU.add).then_inc(vector_value, 1)

            def proj(key):
                t = key[1]
                dve.wait_ge(gpsimd_bias, upto(gpsimd_bias, ("bias", t), "x"))
                for h in range(2):
                    dve.wait_ge(tensor_proj, upto(tensor_proj, key, f"o{h}"))
                    x = X[:, t % 2, 2 * h:2 * h + 2, :].rearrange("p s d -> p (s d)")
                    v.tensor_tensor(x, S[:, h, :], x, ALU.add).then_inc(vector_proj, 1)

            parts = {"setup": setup, "ctx": context, "w2": w2, "kv": kv, "norm": norm, "att": att, "route": route,
                     "z": hidden, "evac": evac, "res": res, "query": query, "most": most, "row": row,
                     "value": value, "proj": proj}
            for key in stages:
                if key[0] in parts:
                    parts[key[0]](key)

        @block.gpsimd
        def _(pool):
            def rstd(key, var_sem, own_sem, dst, mv):
                pool.wait_ge(var_sem, upto(var_sem, key, "var"))
                nc.gpsimd.tensor_tensor(dst, mv, HALF[:, 0:dst.shape[1]], ALU.pow).then_inc(own_sem, 1)

            def kv(key):
                rstd(key, vector_kv, gpsimd_kv, RS2[:, :], MV2[:, :, 1])

            def norm(key):
                rstd(key, vector_norm, gpsimd_norm, RS0[:, :], MV0[:, :, 1])

            def query(key):
                rstd(key, vector_query, gpsimd_query, RS1[:, :], MV1[:, :, 1])

            def second(key):
                t, k = key[1:]
                pool.wait_ge(scalar_z, upto(scalar_z, ("z", t, k), "h"))
                if NZ * t + k >= RING:
                    g = NZ * t + k - RING
                    pool.wait_ge(tensor_p, upto(tensor_p, ("p", g // NZ, g % NZ), "p"))
                nc.gpsimd.tensor_tensor(SL[:, k % RING, :], TB[:, k % 2, :], raw(SH[:, k % RING, :]),
                                               ALU.subtract).then_inc(gpsimd_p, 1)

            def bias(key):
                t = key[1]
                pool.wait_ge(vector_query, upto(vector_query, ("query", t), "xh"))
                nc.gpsimd.tensor_tensor(X[:, t % 2, :, :], X[:, t % 2, :, :],
                                               BP[:, :].unsqueeze(1).to_broadcast([P, NSUB, D]), ALU.add).then_inc(gpsimd_bias, 1)

            parts = {"kv": kv, "norm": norm, "query": query, "p": second, "bias": bias}
            for key in stages:
                if key[0] in parts:
                    parts[key[0]](key)

        @block.tensor
        def _(pe):
            mm = nc.tensor.matmul

            def exact(out_, left, right, start, stop, skip=False):
                (lh, ll), (rh, rl) = left, right
                mm(out_, lh, rh, start=start, stop=False, skip_group_check=skip)
                mm(out_, ll, rh, start=False, stop=False, skip_group_check=skip)
                return mm(out_, lh, rl, start=False, stop=stop, skip_group_check=skip)

            def plain(out_, pairs):
                for i, (l, r) in enumerate(pairs):
                    last = mm(out_, l, r, start=(i == 0), stop=(i == len(pairs) - 1))
                return last

            def setup(key):
                pe.wait_ge(consts_loaded, 16 * 1)
                pe.wait_ge(score_w_loaded, 16 * 1)
                for m in range(KC):
                    for k in range(KC):
                        last = pe.transpose(V0[:, D * m + P * k:D * m + P * k + P], WQR[:, k, P * m:P * m + P], ident)
                last.then_inc(tensor_setup, 1)
                pe.wait_ge(modulation_w_loaded, 16 * 2)
                pe.wait_ge(vector_setup, upto(vector_setup, key, "sc"))
                pe.wait_ge(scalar_setup, upto(scalar_setup, key, "wqT"))
                for w in range(2):
                    for m in range(4):
                        c = BATCH * (4 * w + m)
                        last = plain(V0[:, c:c + BATCH], [(WSS[:, w, k, P * m:P * m + P], COT[:, k, :]) for k in range(KC)])
                last.then_inc(tensor_setup, 1)
                pe.wait_ge(vector_setup, upto(vector_setup, key, "mod"))
                pe.wait_ge(small_w_loaded, 16 * 2)
                for f in range(KC):
                    last = plain(V0[:, 64 + BATCH * f:64 + BATCH * f + BATCH],
                                 [(WQ1R[:, k, P * f:P * f + P], MOD[:, 2 + k, :]) for k in range(KC)])
                last.then_inc(tensor_setup, 1)

            def context(key):
                b = key[1]
                pe.wait_ge(context_loaded, 16 * (4 * (b + 1)))
                if b:
                    pe.wait_ge(vector_proj, upto(vector_proj, ("proj", TPB * b - 1), "o1"))
                for k in range(KC):
                    pe.transpose(M0[:, 160 * k:160 * k + P], CX[:, 0, P * k:P * k + P], ident)
                    last = pe.transpose(M0[:, 160 * k + P:160 * k + CTX], CX[0:TAIL, 1, P * k:P * k + P],
                                        CN[0:TAIL, C_ID:C_ID + TAIL])
                last.then_inc(tensor_ctx, 1)
                pe.wait_ge(scalar_ctx, upto(scalar_ctx, key, "ctxT"))
                for step, bank, w in (("kT", Z[:, 0, :], WKR), ("vT", Z[:, 1, :], WVR)):
                    for m in range(KC):
                        last = plain(bank[:, 160 * m:160 * m + CTX],
                                     [(w[:, k, P * m:P * m + P], CXT[:, k, 0:CTX]) for k in range(KC)])
                    last.then_inc(tensor_ctx, 1)
                pe.wait_ge(vector_ctx, upto(vector_ctx, key, "kT"))
                if b == 0:
                    pe.wait_ge(vector_setup, upto(vector_setup, ("setup", 0), "bq"))
                for m in range(KC):
                    last = plain(V0[:, 160 * m:160 * m + CTX],
                                 [(WQT[:, k, P * m:P * m + P], KTT[:, k, 0:CTX]) for k in range(KC)])
                last.then_inc(tensor_ctx, 1)
                pe.wait_ge(scalar_ctx, upto(scalar_ctx, key, "vT"))
                for e in range(EXPERTS):
                    last = plain(S[:, 0, 160 * e:160 * e + CTX],
                                 [(RW[:, KC + k, e:e + 1].to_broadcast([P, P]), VTT[:, k, 0:CTX]) for k in range(KC)])
                last.then_inc(tensor_ctx, 1)
                last = plain(S[:, 1, 0:EXPERTS],
                             [(CO[:, k, b:b + 1].to_broadcast([P, P]), RW[:, 2 * KC + k, :]) for k in range(KC)])
                last.then_inc(tensor_ctx, 1)
                pe.wait_ge(vector_ctx, upto(vector_ctx, key, "fill"))
                pe.wait_ge(scalar_ctx, upto(scalar_ctx, key, "A"))
                for q in range(NQ):
                    slot = WS[:, q % 2, :, :]
                    pe.wait_ge((slice_even_loaded, slice_odd_loaded)[q % 2], 16 * slices_loaded(b, q))
                    if q >= 2:
                        pe.wait_ge(vector_ctx, upto(vector_ctx, key, f"vw{q - 2}"))
                    plain(Z[:, q % 2, 0:QN], [(VTT[:, k, 0:P], slot[:, k, :]) for k in range(KC)])
                    last = plain(M0[32 * q:32 * q + 32, 0:QN],
                                 [(VTT[:, k, P:160], slot[:, k, :]) for k in range(KC)]
                                 + [(AN[:, k, :], slot[:, KC + k, :]) for k in range(KC)])
                    last.then_inc(tensor_ctx, 1)

            def w2(key):
                pe.wait_ge(w2_loaded, 16 * (EXPERTS + 1))
                pe.wait_ge(vector_ctx, upto(vector_ctx, ("ctx", 0), "RC"))
                for i in range(6):
                    if i >= 2:
                        pe.wait_ge(scalar_w2, upto(scalar_w2, key, f"t{i - 2}"))
                    for r in range(4):
                        j = 4 * (i % 3) + r
                        last = pe.transpose(S[:, i % 2, P * r:P * r + P], W2R[:, j, P * (i // 3):P * (i // 3) + P], ident)
                    last.then_inc(tensor_w2, 1)
                pe.wait_ge(scalar_w2, upto(scalar_w2, key, "t5"))
                for j in range(6):
                    if j >= 2:
                        pe.wait_ge(vector_w2, upto(vector_w2, key, f"m{j - 2}"))
                    for r in range(2):
                        row0 = P * (2 * j + r)
                        last = plain(S[:, j % 2, D * r:D * r + D],
                                     [(W2T[:, k, row0:row0 + P], OW[:, k, :]) for k in range(KC)])
                    last.then_inc(tensor_w2, 1)
                pe.wait_ge(vectors_loaded, 16 * N_VECTORS)
                for e in range(EXPERTS):
                    last = plain(O[:, e, :], [(B2T[:, k, e:e + 1].to_broadcast([P, P]), OW[:, k, :]) for k in range(KC)])
                last.then_inc(tensor_w2, 1)

            def kv(key):
                b = key[1]
                pe.wait_ge(vector_kv, upto(vector_kv, key, "xh"))
                if b == 0:
                    pe.wait_ge(vector_w2, upto(vector_w2, ("w2", 0), "m5"))
                for k in range(KC):
                    pe.transpose(V0[:, 160 * k:160 * k + P], XH2[:, 0, P * k:P * k + P], ident)
                    last = pe.transpose(V0[:, 160 * k + P:160 * k + CTX], XH2[0:TAIL, 1, P * k:P * k + P],
                                        CN[0:TAIL, C_ID:C_ID + TAIL])
                last.then_inc(tensor_kv, 1)
                pe.wait_ge(scalar_kv, upto(scalar_kv, key, "x1"))
                pe.wait_ge(kv_w_loaded, 16 * (4 * (b + 1)))
                for f in range(KC):
                    last = plain(S[:, 0, 160 * f:160 * f + CTX],
                                 [(WKV[:, k, P * f:P * f + P], KX[:, k, 0:CTX]) for k in range(KC)])
                last.then_inc(tensor_kv, 1)
                plain(S[:, 1, 0:D], [(KX[:, k, 0:P], WKV[:, k, D:2 * D]) for k in range(KC)]).then_inc(tensor_kv, 1)
                pe.wait_ge(vector_kv, upto(vector_kv, key, "rep"))
                plain(V0[0:4 * TAIL, 0:D], [(KXR[:, k, :], WKV[:, k, D:2 * D]) for k in range(KC)]).then_inc(tensor_kv, 1)

            def norm(key):
                t = key[1]
                pe.wait_ge(vector_norm, upto(vector_norm, key, "xh"))
                for m in range(KC):
                    if t % TPB == 0:
                        pe.wait_ge(vector_ctx, upto(vector_ctx, ("ctx", t // TPB), f"vw{2 + m}"))
                    else:
                        pe.wait_ge(vector_z, upto(vector_z, ("z", t - 1, NZ - 2 + m), "s"))
                    for s in range(NSUB):
                        last = pe.transpose(Z[:, m, P * s:P * s + P], XH0[:, s, P * m:P * m + P], ident)
                    last.then_inc(tensor_norm, 1)

            def att(key):
                t, s = key[1:]
                pe.wait_ge(scalar_norm, upto(scalar_norm, ("norm", t), "n1"))
                if s >= 2:
                    pe.wait_ge(vector_att, upto(vector_att, ("att", t, s - 2), "lg"))
                elif t:
                    pe.wait_ge(vector_evac, upto(vector_evac, ("evac", t - 1, EXPERTS), "o"))
                else:
                    pe.wait_ge(vector_w2, upto(vector_w2, ("w2", 0), "cb"))
                if t % TPB == 0:
                    pe.wait_ge(vector_ctx, upto(vector_ctx, ("ctx", t // TPB), "RC"))
                plain(O[:, 2 * (s % 2), 0:CTX + EXPERTS],
                             [(NXf[:, k, P * s:P * s + P], A[:, k, :]) for k in range(KC)]).then_inc(tensor_att, 1)

                pe.wait_ge(vector_att, upto(vector_att, key, "p"))
                pe.transpose(Z[:, 0, P * s:P * s + P], PB[:, s % 2, 0:P], ident)
                pe.transpose(Z[0:STACK, 1, P * s:P * s + P], PB[:, s % 2, P:P + STACK], ident).then_inc(tensor_att, 1)

            def hidden(key):
                t, k = key[1:]
                if k < 2:
                    pe.wait_ge(vector_norm, upto(vector_norm, ("norm", t), "n1"))
                    pe.wait_ge(vector_route, upto(vector_route, ("route", t), "dl"))
                    if t == 0:
                        pe.wait_ge(vector_setup, upto(vector_setup, ("setup", 0), "wn"))
                    if t % TPB == 0:
                        pe.wait_ge(tails_placed, 16 * 3 * NQ * (t // TPB + 1))
                else:
                    pe.wait_ge(vector_z, upto(vector_z, ("z", t, k - 2), "s"))
                c = slice(P * k, P * k + P)
                bank = Z[:, k % 2, :]
                for m in range(KC):
                    exact(bank, (WNh[:, m, c], WNl[:, m, c]), (NXh[:, m, :], NXl[:, m, :]), m == 0, False)
                exact(bank, (VWh[:, c], VWl[:, c]), (PTh[:, :], PTl[:, :]), False, False)
                mm(bank, VWD[:, c], PTD[0:STACK, :], start=False, stop=True).then_inc(tensor_z, 1)

            def second(key):
                t, k = key[1:]
                pe.wait_ge(scalar_z, upto(scalar_z, ("z", t, k), "h"))
                pe.wait_ge(gpsimd_p, upto(gpsimd_p, key, "l"))
                first = k in (0, GATES) or (k >= GATES and (k - GATES) % PER == 0)
                last_one = k == GATES - 1 or (k >= GATES and (k - GATES) % PER == PER - 1)
                if first:
                    if k == 0:
                        pe.wait_ge(vector_att, upto(vector_att, ("att", t, NSUB - 1), "lg"))
                        if t == 0:
                            pe.wait_ge(vector_setup, upto(vector_setup, ("setup", 0), "gw"))
                    else:
                        pe.wait_ge(vector_evac, upto(vector_evac, ("evac", t, (k - GATES) // PER), "o"))
                wh, wl = (GWh[:, k, :], GWl[:, k, :]) if k < GATES else (W2h[:, k - GATES, :], W2l[:, k - GATES, :])
                for s in range(NSUB):
                    c = slice(P * s, P * s + P)
                    last = exact(O[:, s, :], (SH[:, k % RING, c], SL[:, k % RING, c]), (wh, wl),
                                 first and s % 2 == 0, last_one, skip=True)
                last.then_inc(tensor_p, 1)

            def query(key):
                t = key[1]
                pe.wait_ge(vector_query, upto(vector_query, key, "xh"))
                if t:
                    pe.wait_ge(vector_proj, upto(vector_proj, ("proj", t - 1), "o1"))
                for m in range(KC):
                    for s in range(NSUB):
                        last = pe.transpose(S[:, m, P * s:P * s + P], XH1[:, s, P * m:P * m + P], ident)
                    last.then_inc(tensor_query, 1)
                pe.wait_ge(vector_query, upto(vector_query, key, "x1"))
                if t == 0:
                    pe.wait_ge(vector_setup, upto(vector_setup, ("setup", 0), "wq"))
                for f in range(KC):
                    for k in range(KC):
                        c = slice(P * f, P * f + P)
                        last = exact((V0[:, :], S[:, 0, :])[f], (WQh[:, k, c], WQl[:, k, c]), (XQh[:, k, :], XQl[:, k, :]),
                                     k == 0, k == KC - 1)
                    last.then_inc(tensor_query, 1)

            def most(key):
                t, s = key[1:]
                if s == 0:
                    pe.wait_ge(queries_placed, 16 * 3 * PAIRS * (t + 1))
                    pe.wait_ge(vector_query, upto(vector_query, ("query", t), "q1"))
                    if t % TPB == 0:
                        pe.wait_ge(vector_kv, upto(vector_kv, ("kv", t // TPB), "vt"))
                        pe.wait_ge(keys_placed, 16 * 3 * PAIRS * (t // TPB + 1))
                for c in range(PAIRS):
                    if c >= 2:
                        pe.wait_ge(vector_most, upto(vector_most, key, f"c{c - 2}"))
                    elif s:
                        pe.wait_ge(vector_most, upto(vector_most, ("most", t, s - 1), f"c{PAIRS - 2 + c}"))
                    mm(S[:, c % 2, 0:2 * CTX], QS[0:STACK, c, P * s:P * s + P],
                              KS[0:STACK, c, :, :].rearrange("p j n -> p (j n)"), start=True, stop=True).then_inc(tensor_most, 1)

            def row(key):
                t = key[1]
                pe.wait_ge(vector_most, upto(vector_most, ("most", t, NSUB - 1), f"c{PAIRS - 1}"))
                for s in range(NSUB):
                    last = pe.transpose(V0[0:HEADS, P * s:P * s + P], MX[:, s, :, :].rearrange("p j c -> p (j c)"), ident)
                last.then_inc(tensor_row, 1)

            def score(key):
                t, g = key[1:]
                if g == 0:
                    pe.wait_ge(maxima_placed, 16 * 4 * (t + 1))
                for i in range(5):
                    w = 5 * g + i
                    if w >= 2:
                        pe.wait_ge(scalar_score, upto(scalar_score, ("score", t, (w - 2) // 5), f"e{(w - 2) % 5}"))
                    bank = S[:, w % 2, :]
                    if i < 4:
                        c = 2 * g + i // 2
                        last = mm(bank, KS[:, c, i % 2, 0:P], QS[:, c, :], start=True, stop=True)
                    else:
                        for j in range(2):
                            c = 2 * g + j
                            last = mm(bank[0:4 * TAIL, :], KT[:, c, :, :].rearrange("p i n -> p (i n)"), QS[:, c, :],
                                      start=(j == 0), stop=(j == 1))
                    last.then_inc(tensor_score, 1)

            def value(key):
                t, g = key[1:]
                pe.wait_ge(scalar_score, upto(scalar_score, ("score", t, g), "e4"))
                if g:
                    pe.wait_ge(vector_value, upto(vector_value, ("value", t, g - 1), "take"))
                else:
                    pe.wait_ge(vector_row, upto(vector_row, ("row", t), "l"))
                for i in range(4):
                    mm(V0[32 * i:32 * i + 32, :], VA[:, 4 * g + i, :], E[:, i, :], start=True, stop=False)
                for i in range(4):
                    last = mm(V0[32 * i:32 * i + 32, :], VT1[:, 4 * g + i, :], E[0:4 * TAIL, 4, :], start=False, stop=True)
                last.then_inc(tensor_value, 1)

            def proj(key):
                t = key[1]
                pe.wait_ge(vector_value, upto(vector_value, ("value", t, GROUPS - 1), "a"))
                pe.wait_ge(scalar_score, upto(scalar_score, ("score", t, GROUPS - 1), "e4"))
                if t == 0:
                    pe.wait_ge(vector_setup, upto(vector_setup, ("setup", 0), "wp"))
                for h in range(2):
                    for s in (2 * h, 2 * h + 1):
                        for g in range(GROUPS):
                            for w in (WPh, WPl):
                                last = mm(S[:, h, D * (s % 2):D * (s % 2) + D], AD[:, g, P * s:P * s + P], w[:, g, :],
                                          start=(g == 0 and w is WPh), stop=(g == GROUPS - 1 and w is WPl))
                    last.then_inc(tensor_proj, 1)

            parts = {"setup": setup, "ctx": context, "w2": w2, "kv": kv, "norm": norm, "att": att,
                     "z": hidden, "p": second, "query": query, "most": most, "row": row, "score": score,
                     "value": value, "proj": proj}
            for key in stages:
                if key[0] in parts:
                    parts[key[0]](key)


def kernel(**inputs):
    import numpy as np
    import concourse.bacc as bacc
    from concourse.bass_utils import run_bass_kernel_spmd

    nc = bacc.Bacc("TRN2", target_bir_lowering=False, num_devices=1)
    arrays, aps = {}, {}
    for name, value in inputs.items():
        arrays[name] = np.ascontiguousarray(value)
        aps[name] = nc.dram_tensor(name, arrays[name].shape, F32, kind="ExternalInput").ap()
    arrays["shape_constants"] = shape_constants(np)
    consts = nc.dram_tensor("shape_constants", (P, NCONST), F32, kind="ExternalInput").ap()
    out = nc.dram_tensor("out", (BATCH, SEQ, D), F32, kind="ExternalOutput").ap()
    build(nc, aps, out, consts)
    r = run_bass_kernel_spmd(nc, [arrays], core_ids=[0])
    return r.results[0]["out"]
```

```python
from contextlib import ExitStack

import concourse.bass as bass
from concourse import mybir

F32 = mybir.dt.float32
F32R = mybir.dt.float32r
ALU = mybir.AluOpType
ACT = mybir.ActivationFunctionType
AX = mybir.AxisListType

P = 128
NSPLIT = 4
BATCH, SEQ, D, CTX = 2, 1024, 256, 154
KC = D // P
TILE = 512
NSUB = TILE // P
TPB = SEQ // TILE
NT = BATCH * TPB
TAIL = CTX - P
EXPERTS, RH = 3, 512
ZCOLS = D + EXPERTS * RH
NZ = ZCOLS // P
GATES = D // P
PER = RH // P
QN = 448
NQ = ZCOLS // QN
HEADS, DH = 16, D // 16
PAIRS = HEADS // 2
GROUPS = HEADS // 4
STACK = 96
KROWS = STACK + 4
EPS = 1e-5
RING = 2
SLOTS = 3

C_ID, C_HEAD, C_SPLIT, C_ROW, C_ONE = 0, 128, 130, 131, 135
C_PAIR = 136
C_FOLD = 138
NCONST = 170
N_ROWS = 8
N_ROUTER = 2
N_BROADCAST = 3
V_GAMMA, V_BETA, V_COND, V_B2, V_BSS, V_BQ, V_BK = 0, 2, 4, 8, 14, 22, 24
N_VROWS = 26
N_HIDDEN_BIAS = 7


def shape_constants(np):
    c = np.zeros((P, NCONST), np.float32)
    row = np.arange(P)
    c[:, C_ID:C_ID + P] = np.eye(P)
    c[:, C_HEAD] = row % 32 < DH
    c[:, C_HEAD + 1] = row % 32 >= DH
    c[:, C_SPLIT] = -1.0 * (row % 32 >= DH)
    for i in range(4):
        c[:, C_ROW + i] = (row >= TAIL * i) & (row < TAIL * (i + 1))
    c[:, C_ONE] = 1.0
    c[STACK:KROWS, C_PAIR] = (1, 0, 1, 0)
    c[STACK:KROWS, C_PAIR + 1] = (0, 1, 0, 1)
    c[:, C_FOLD:C_FOLD + 32] = row[:, None] % 32 == np.arange(32)[None, :]
    return c


STEPS = {
    "tensor": {
        "setup": ["wqT"],
        "ctx": ["ctxT", "kT", "vT"],
        "vec": ["v"],
        "fold": ["A", "VR", "RC"],
        "vw": ["m"],
        "tail": ["m"],
        "mod": ["mod"],
        "bq": ["bq"],
        "w2t": ["t0", "t1"],
        "w2": ["m0", "m1"],
        "cb": ["cb"],
        "keyx": ["t"],
        "key": ["k", "v", "vt"],
        "norm": ["t0", "t1"],
        "att": ["s"],
        "prob": ["p"],
        "z": ["z"],
        "p": ["p"],
        "qx": ["t0", "t1"],
        "query": ["q0", "q1"],
        "most": ["s"],
        "row": ["m"],
        "score": ["s"],
        "value": ["v"],
        "proj": ["o"],
    },
    "scalar": {
        "setup": ["wqT"],
        "ctx": ["ctxT", "vT"],
        "fold": ["A"],
        "vw": ["h", "t"],
        "silu": ["tc"],
        "split": ["h"],
        "w2t": ["t0", "t1"],
        "w2": ["m0", "m1"],
        "keyx": ["x0", "x1"],
        "norm": ["n0", "n1"],
        "att": ["e"],
        "prob": ["p"],
        "route": ["pm", "pd", "ex"],
        "z": ["t"],
        "h": ["h"],
        "gate": ["g"],
        "qx": ["x0", "x1"],
        "query": ["q0", "q1"],
        "row": ["h"],
        "score": ["e"],
        "value": ["v"],
        "out": ["h"],
    },
    "vector": {
        "setup": ["fill"],
        "ctx": ["kT"],
        "vec": ["v"],
        "fold": ["fill", "VR", "RC"],
        "vw": ["l"],
        "tail": ["th", "tl"],
        "silu": ["sc"],
        "mod": ["mod"],
        "bq": ["bq"],
        "split": ["l"],
        "w2": ["m0", "m1"],
        "cb": ["cb"],
        "keyn": ["var", "xh"],
        "keyx": ["rep"],
        "key": ["k", "kh", "kl", "ones", "v", "vt"],
        "keyt": ["kt"],
        "ln": ["var"],
        "norm": ["xh"],
        "low": ["n0", "n1"],
        "att": ["t"],
        "prob": ["r", "lg"],
        "route": ["pl", "dl", "lg", "prob"],
        "z": ["s"],
        "evac": ["o"],
        "res": ["u", "x"],
        "qn": ["var"],
        "qx": ["xh"],
        "qlow": ["x0", "x1"],
        "query": ["q0", "q1"],
        "most": ["s"],
        "row": ["l"],
        "sums": ["r"],
        "out": ["o"],
        "outl": ["l"],
        "proj": ["o"],
    },
    "gpsimd": {
        "keyn": ["rstd"],
        "ln": ["rstd"],
        "h": ["l"],
        "qn": ["rstd"],
        "bias": ["x"],
        "sum": ["s"],
    },
}


DELAY = {
    "tensor": {"norm": 1, "prob": 1, "qx": 1, "keyx": 1},
    "scalar": {"norm": 1, "qx": 1, "keyx": 1},
    "vector": {"query": 1, "key": 1, "mod": 1, "bq": 1},
    "gpsimd": {},
    "sync": {},
}


def schedule():
    def lead(t):
        return [[("norm", t)], []]

    def block0(t):
        slots = [] if t % TPB else lead(t)
        slots += [[("att", t, 0), ("att", t, 1)], [("att", t, 2), ("att", t, 3), ("prob", t, 0)],
                  [("prob", t, 1)], [("prob", t, 2), ("low", t)], [("prob", t, 3)], [], [("route", t)]]
        if t % TPB:
            slots[RES].append(("res", t - 1))
        for k in range(NZ + 2):
            slots.append([("z", t, k)] if k < NZ else [])
            if k == 6 and t + 1 < NT and (t + 1) % TPB:
                slots[-1].append(("ln", t + 1))
            if k == NZ and (t + 1) % TPB:
                slots[-1].append(("norm", t + 1))
            slot = []
            if 0 <= k - 2:
                slot.append(("p", t, k - 2))
                if k - 2 == GATES - 1:
                    slot.append(("gate", t))
                elif k - 2 >= GATES and (k - 2 - GATES) % PER == PER - 1:
                    slot.append(("evac", t, (k - 2 - GATES) // PER + 1))
            if k < NZ:
                slot.append(("h", t, k))
            slots.append(slot)
        if (t + 1) % TPB == 0:
            slots[-1].append(("res", t))
        return slots

    def block1(t):
        out = [[("qn", t)], [("qx", t)], [], [("qlow", t)], [("query", t)], [("bias", t)], []]
        for u in range(0, NSUB * PAIRS, 3):
            out.append([("most", t, i) for i in range(u, min(u + 3, NSUB * PAIRS))])
        out += [[("row", t)], [], []]
        w = 0
        while w < 5 * GROUPS:
            n = 3 if len(out) % 2 else 2
            out.append([("score", t, i) for i in range(w, min(w + n, 5 * GROUPS))])
            w += n
        for g in range(GROUPS):
            at = next(i for i, slot in enumerate(out) if ("score", t, 5 * g + 4) in slot) + 1
            while len(out) <= at:
                out.append([])
            out[at].insert(0, ("value", t, g))
            if g:
                out[at].append(("sum", t, g))
        out += [[], [("sums", t, 0), ("out", t, 0)], [("sums", t, 1), ("out", t, 1)],
                [("outl", t, 0)], [("outl", t, 1)], [("proj", t, 0)], [("proj", t, 1)], []]
        return out

    def keys(b):
        return [[("keyn", b)], [("keyx", b)], [], [("key", b)], [], [], [], [("keyt", b)]]

    def context(b):
        return [[("load", b), ("ctx", b)] + ([] if b else [("vec", 0)]) + [("fold", b)]] + [
            [("vw", b, q)] for q in range(NQ)] + [[("tail", b)]]

    def weave(slots, *streams):
        out = []
        for i in range(max(len(slots), *(len(s) for s in streams))):
            out.append([key for s in (slots, *streams) if i < len(s) for key in s[i]])
        return out

    weights = [[("w2t", 0)], [("w2", 0), ("w2t", 1)], [("w2", 1), ("w2t", 2)], [("split", 0), ("w2", 2)], [("split", 1)], [("cb", 0)],
               [], [("silu", 0)], [], [("mod", 0)], [("split", 2)], [("bq", 0)], [("split", 3)]]
    start = [[("setup", 0)]] + context(0) + [[("ln", 0)]]
    middle = context(1) + [[("ln", TPB)]]
    tiles = [block0(t) for t in range(NT)]
    rest = tiles[0] + tiles[1] + middle + tiles[2] + tiles[3]
    at1 = len(tiles[0])
    at2 = at1 + len(tiles[1])
    at3 = at2 + len(middle) + len(tiles[2])
    key1 = at2 + WAIT1 + len(block1(1)) - 1
    begin2 = max(at3 + RES, key1 + 3)
    begin2 += (begin2 - at3) % 2
    streams = [weights, [[]] * KEY0 + keys(0), [[]] * (at1 + RES) + block1(0), [[]] * (at2 + WAIT1) + block1(1),
               [[]] * key1 + keys(1), [[]] * begin2 + block1(2),
               [[]] * max(len(rest), begin2 + len(block1(2))) + block1(3)]
    return start + weave(rest, *streams)


def order(engine):
    placed = []
    for slot, stages in enumerate(schedule()):
        for key in stages:
            placed.append((slot + DELAY[engine].get(key[0], 0), key))
    placed.sort(key=lambda item: item[0])
    return [key for _, key in placed]


RES = 2
WAIT1 = 3
KEY0 = 20
INSTANCE = {
    "vw": lambda b, q: NQ * b + q,
    "att": lambda t, s: NSUB * t + s, "prob": lambda t, s: NSUB * t + s, "most": lambda t, u: NSUB * PAIRS * t + u,
    "z": lambda t, k: NZ * t + k, "h": lambda t, k: NZ * t + k, "p": lambda t, k: NZ * t + k,
    "evac": lambda t, j: EXPERTS * t + j - 1, "sum": lambda t, a: (GROUPS - 1) * t + a - 1, 
    "sums": lambda t, h: 2 * t + h, "out": lambda t, h: 2 * t + h, "outl": lambda t, h: 2 * t + h,
    "proj": lambda t, h: 2 * t + h,
    "score": lambda t, w: 5 * GROUPS * t + w, "value": lambda t, a: GROUPS * t + a,
}


def build(nc, a, out, consts):
    with ExitStack() as ctx:
        def sem(name):
            return ctx.enter_context(nc.semaphore(name))

        def psum(name, shape):
            return ctx.enter_context(nc.psum_tensor(name, shape, F32))

        Z = psum("hidden_banks", [P, 2, 512])
        O = psum("token_banks", [P, NSUB, D])
        OFF = O[:, :, :].rearrange("p (k s) d -> p k (s d)", k=2)
        M0 = psum("misc_bank", [P, 512])
        S = psum("score_banks", [P, 2, 512])
        V0 = psum("value_bank", [P, 512])

        at = [(nc.sbuf_base + 63) // 64 * 64]

        def put(name, shape, dt=F32, offset=None):
            size = 4
            for n in shape[1:]:
                size *= n
            o = at[0] if offset is None else offset
            if offset is None:
                at[0] += (size + 31) // 32 * 32
            return nc.alloc_sbuf_tensor_at(name, shape, dt, offset=o)

        def run(start, parts):
            made = []
            for name, shape, dt in parts:
                made.append(put(name, shape, dt, offset=start))
                size = 4
                for n in shape[1:]:
                    size *= n
                start += (size + 31) // 32 * 32
            return made + [start]

        CN = put("constants", [P, NCONST])
        ident = CN[:, C_ID:C_ID + P]
        WNh = put("hidden_w_high", [P, KC, ZCOLS], F32R)
        WNl = put("hidden_w_low", [P, KC, ZCOLS], F32R)
        VWh = put("context_w_high", [P, ZCOLS], F32R)
        VWl = put("context_w_low", [P, ZCOLS], F32R)
        VWD = put("context_w_tail", [STACK, ZCOLS], F32R)
        W2h = put("expert_out_high", [P, EXPERTS * PER, D], F32R)
        W2l = put("expert_out_low", [P, EXPERTS * PER, D], F32R)
        GWh = put("gate_out_high", [P, KC, D], F32R)
        GWl = put("gate_out_low", [P, KC, D], F32R)
        WQh = put("query_w_high", [P, KC, D], F32R)
        WQl = put("query_w_low", [P, KC, D], F32R)
        WPh = put("proj_w_high", [P, GROUPS, D], F32R)
        WPl = put("proj_w_low", [P, GROUPS, D], F32R)
        A = put("score_w", [P, KC, CTX + EXPERTS])
        VR = put("router_context", [P, EXPERTS, CTX])
        RC = put("router_const", [P, EXPERTS])
        RB = put("router_bias", [P, EXPERTS])
        keys_at = at[0]
        KS = put("pair_keys", [KROWS, PAIRS, 2, CTX], F32R)
        KT = put("pair_keys_tail", [KROWS, PAIRS, 4, TAIL], F32R)
        VA = put("head_values", [P, HEADS, 2 * DH])
        VT1 = put("head_values_tail", [4 * TAIL, HEADS, 2 * DH])
        CB = put("second_bias", [64, 1 + EXPERTS, D], F32R)
        BROW = put("bias_rows", [P, P], F32R)
        BP = put("proj_bias_row", [P, D])
        VC = put("vectors", [P, N_VROWS])
        GAM, BET, BQ0, BK = (VC[:, i:i + KC] for i in (V_GAMMA, V_BETA, V_BQ, V_BK))
        CO = VC[:, V_COND:V_COND + BATCH * KC].rearrange("p (b k) -> p k b", k=KC)
        B2T = VC[:, V_B2:V_B2 + EXPERTS * KC].rearrange("p (e k) -> p k e", k=KC)
        BSS = VC[:, V_BSS:V_BSS + 8]
        COT = put("condition_silu", [P, KC, BATCH])
        MOD = put("modulation", [P, 8, BATCH])
        BQ = put("query_bias", [P, KC, BATCH])
        RW = put("router_w", [P, 3 * KC, EXPERTS])
        HALF = put("minus_half", [P, NSUB])
        ST0 = put("stats0", [P, NSUB, 6])
        MV0 = put("mean_var0", [P, NSUB, 2])
        RS0 = put("rstd0", [P, NSUB])
        ST1 = put("stats1", [P, NSUB, 6])
        MV1 = put("mean_var1", [P, NSUB, 2])
        RS1 = put("rstd1", [P, NSUB])
        WQT = put("score_wq_T", [P, KC, D])
        TC = put("condition_tanh", [P, KC, BATCH])
        ST2 = put("stats2", [P, 2, 6])
        MV2 = put("mean_var2", [P, 2, 2])
        RS2 = put("rstd2", [P, 2])
        SM0 = put("softmax_small", [P, NSUB, 4])
        EV = put("router_dot", [P, NSUB, EXPERTS])
        LG = put("router_logits", [P, NSUB, EXPERTS])
        PR = put("router_probs", [P, NSUB, EXPERTS])
        RT = put("router_small", [P, NSUB, 2])
        MX = put("head_maxima", [P, NSUB, 2, PAIRS])
        tokens_at = at[0]
        X = put("tokens", [P, SLOTS, NSUB, D])
        WQR, WQ1R, GWR, OB, GB, VROWS, WPR, _ = run(keys_at, [
            ("score_wq_raw", [P, KC, D], F32), ("query_w_raw", [P, KC, D], F32),
            ("gate_out_raw", [P, KC, D], F32), ("out_bias_row", [P, D], F32), ("gate_b2_row", [P, D], F32),
            ("vector_rows", [P, P], F32), ("proj_w_raw", [P, GROUPS, D], F32)])
        WSS, _ = run(tokens_at + 4 * NSUB * D, [("modulation_w", [P, 2, KC, 2 * D], F32)])
        R0 = at[0]
        SH, SL, NXh, NXl, PTh, PTl, PTD, TB, ACC, G, end0 = run(R0, [
            ("hidden_high", [P, RING, TILE], F32R), ("hidden_low", [P, RING, TILE], F32R),
            ("normed_high", [P, KC, TILE], F32R), ("normed_low", [P, KC, TILE], F32R),
            ("probs_T_high", [P, TILE], F32R), ("probs_T_low", [P, TILE], F32R),
            ("probs_T_tail", [P, TILE], F32R), ("hidden", [P, 2, TILE], F32),
            ("expert_sum", [P, NSUB, D], F32), ("gate", [P, NSUB, D], F32)])
        PB, EB, _ = run(R0, [("probs", [P, NSUB, D], F32), ("exps", [P, NSUB, CTX], F32)])
        XH0, _ = run(R0 + 4 * 2 * RING * TILE, [("x_hat0", [P, NSUB, D], F32)])
        NXf, _ = run(R0 + 4 * (2 * RING + 2 * KC) * TILE, [("normed", [P, KC, TILE], F32)])
        WS0, _ = run(R0, [("w_slices_even", [P, 2 * KC, QN], F32)])
        CX, CXT, KTT, VTT, AN, WKR, WVR, WS1, TQ, used = run(R0 + 4 * 2 * RING * TILE, [
            ("context", [P, 2, D], F32),
            ("context_T", [P, KC, 160], F32), ("keys_T", [P, KC, 160], F32),
            ("values_T", [P, KC, 160], F32), ("anchor_cols", [P, KC, 32], F32),
            ("wk_raw", [P, KC, D], F32), ("wv_raw", [P, KC, D], F32),
            ("w_slices_odd", [P, 2 * KC, QN], F32), ("tail_quarters", [P, NQ, QN], F32)])
        TH, TL, B1T, end1 = run(used, [
            ("tail_high", [P, QN], F32R), ("tail_low", [P, QN], F32R), ("hidden_bias", [P, QN], F32)])
        TF, _ = run(used - 4 * NQ * QN, [("tail_full", [P, QN], F32)])
        assert used >= end0 - 2 * 4 * NSUB * D
        at[0] = max(end0, end1)
        R1 = at[0]
        QS, XH1, XQh, XQl, QH, QL, ROWS, end2 = run(R1, [
            ("query_stack", [KROWS, PAIRS, TILE], F32R),
            ("x_hat1", [P, NSUB, D], F32), ("query_in_high", [P, KC, TILE], F32R),
            ("query_in_low", [P, KC, TILE], F32R),
            ("queries_high", [P, KC, TILE], F32R), ("queries_low", [P, KC, TILE], F32R),
            ("row_space", [P, 2, TILE], F32)])
        NMH, NML, _ = run(end2 - 2 * 4 * TILE, [
            ("max_high", [HEADS, TILE], F32R), ("max_low", [HEADS, TILE], F32R)])
        SD, _ = run(R1 + 4 * PAIRS * TILE, [("sums_spread", [P, GROUPS, D], F32)])
        E, _, RAW, SUM, _ = run(R1 + 4 * PAIRS * TILE, [
            ("exp_ring", [P, 5, TILE], F32), ("unused", [P, TILE], F32),
            ("outs_and_sums", [P, GROUPS, TILE], F32), ("sums", [P, TILE], F32)])
        AH, AL, _ = run(R1, [("outs_high", [P, GROUPS, TILE], F32R), ("outs_low", [P, GROUPS, TILE], F32R)])
        WNR, W2R, W2T, OW, end3 = run(R1, [
            ("hidden_w_raw", [P, KC, ZCOLS], F32), ("w2_raw", [P, EXPERTS * PER, D], F32),
            ("w2_T", [P, KC, EXPERTS * RH], F32), ("out_w", [P, KC, D], F32)])
        CBF, CBH, _ = run(R1, [("second_bias_full", [64, 1 + EXPERTS, D], F32), ("second_bias_high", [64, 1 + EXPERTS, D], F32R)])
        KX, KXR, K1, KMH, KML, VTM, WKV, CX1, XH2, BV, end4 = run(R1, [
            ("ctx_mod_T", [P, KC, 160], F32), ("ctx_tail_rep", [P, KC, 4 * TAIL], F32),
            ("keys1", [P, KC, 160], F32), ("keys1_high", [P, KC, 2, CTX], F32R),
            ("keys1_low", [P, KC, 2, CTX], F32R), ("tail_values", [4 * TAIL, D], F32),
            ("kv_w", [P, KC, 2 * D], F32), ("context1", [P, 2, D], F32), ("x_hat2", [P, 2, D], F32),
            ("value_bias_row", [P, D], F32)])
        at[0] = max(end2, end3, end4)

        steps_of = {}

        def step_sem(engine, stage):
            made = sem(f"{engine}_{stage}")
            steps_of[id(made)] = STEPS[engine][stage]
            return made

        (tensor_setup, tensor_ctx, tensor_vec, tensor_fold, tensor_vw, tensor_tail,
         tensor_mod, tensor_bq, tensor_w2t, tensor_w2, tensor_cb, tensor_keyx,
         tensor_key, tensor_norm, tensor_att, tensor_prob, tensor_z, tensor_p,
         tensor_qx, tensor_query, tensor_most, tensor_row, tensor_score, tensor_value,
         tensor_proj) = (
            step_sem("tensor", s) for s in STEPS["tensor"])
        (scalar_setup, scalar_ctx, scalar_fold, scalar_vw, scalar_silu, scalar_split,
         scalar_w2t, scalar_w2, scalar_keyx, scalar_norm, scalar_att, scalar_prob,
         scalar_route, scalar_z, scalar_h, scalar_gate, scalar_qx, scalar_query,
         scalar_row, scalar_score, scalar_value, scalar_out) = (
            step_sem("scalar", s) for s in STEPS["scalar"])
        (vector_setup, vector_ctx, vector_vec, vector_fold, vector_vw, vector_tail,
         vector_silu, vector_mod, vector_bq, vector_split, vector_w2, vector_cb,
         vector_keyn, vector_keyx, vector_key, vector_keyt, vector_ln, vector_norm,
         vector_low, vector_att, vector_prob, vector_route, vector_z, vector_evac,
         vector_res, vector_qn, vector_qx, vector_qlow, vector_query, vector_most,
         vector_row, vector_sums, vector_out, vector_outl, vector_proj) = (
            step_sem("vector", s) for s in STEPS["vector"])
        (gpsimd_keyn, gpsimd_ln, gpsimd_h, gpsimd_qn, gpsimd_bias, gpsimd_sum) = (
            step_sem("gpsimd", s) for s in STEPS["gpsimd"])
        vector_results = sem("vector_results")
        consts_loaded = sem("consts_loaded")
        rows_loaded = sem("rows_loaded")
        router_loaded = sem("router_loaded")
        broadcasts_loaded = sem("broadcasts_loaded")
        score_w_loaded = sem("score_w_loaded")
        modulation_w_loaded = sem("modulation_w_loaded")
        small_w_loaded = sem("small_w_loaded")
        proj_w_loaded = sem("proj_w_loaded")
        hidden_w_loaded = sem("hidden_w_loaded")
        w2_loaded = sem("w2_loaded")
        x_loaded = [sem(f"x_slot{i}_loaded") for i in range(SLOTS)]
        context_loaded = sem("context_loaded")
        kv_w_loaded = sem("kv_w_loaded")
        hidden_bias_loaded = sem("hidden_bias_loaded")
        slice_even_loaded = sem("slice_even_loaded")
        slice_odd_loaded = sem("slice_odd_loaded")
        tails_placed = sem("tails_placed")
        keys_placed = sem("keys_placed")
        pair_placed = [sem(f"query_pair{c}_placed") for c in range(PAIRS)]
        maxima_placed = sem("maxima_placed")
        stored = sem("stored")

        def instance(key):
            return key[1] if len(key) == 2 else INSTANCE[key[0]](*key[1:])

        def upto(semaphore, key, step):
            names = steps_of[id(semaphore)]
            return instance(key) * len(names) + names.index(step) + 1

        class Count:
            n = 0

            def one(self):
                self.n += 1
                return 1

        for e in STEPS:
            seen = {}
            for key in order(e):
                if key[0] in STEPS[e]:
                    assert instance(key) == seen.get(key[0], 0), (e, key)
                    seen[key[0]] = seen.get(key[0], 0) + 1

        def hidden_columns(lo, hi, rows):
            out_ = []
            if lo < D:
                out_.append((0, min(hi, D) - lo, a["L0_xcond_gate_w1"][rows, lo:min(hi, D)]))
            for e in range(EXPERTS):
                c0 = D + e * RH
                l, h = max(lo, c0), min(hi, c0 + RH)
                if l < h:
                    out_.append((l - lo, h - lo, a["L0_xcond_e_w1"][e, rows, l - c0:h - c0]))
            return out_

        def slices_loaded(b, q):
            each = [2 * len(hidden_columns(i * QN, (i + 1) * QN, slice(0, D))) for i in range(NQ)]
            return b * sum(each[q % 2::2]) + sum(each[q % 2:q + 1:2])

        def hidden_bias(lo, hi):
            out_ = []
            if lo < D:
                out_.append((0, min(hi, D) - lo, a["L0_xcond_gate_b1"][lo:min(hi, D)]))
            for e in range(EXPERTS):
                c0 = D + e * RH
                l, h = max(lo, c0), min(hi, c0 + RH)
                if l < h:
                    out_.append((l - lo, h - lo, a["L0_xcond_e_b1"][e, l - c0:h - c0]))
            return out_

        def feature_rows(w):
            return w.rearrange("(k p) n -> p k n", p=P)

        def columns(v):
            return v.rearrange("(k p) -> p k", p=P)

        def tokens_of(dram, t):
            b, i = t // TPB, t % TPB
            return dram[b, i * TILE:(i + 1) * TILE, :].rearrange("(s p) d -> p s d", p=P)

        def raw(ap):
            return ap.bitcast(F32)

        block = ctx.enter_context(nc.Block())

        @block.sync
        def _(sp):
            def setup(key):
                sp.dma_start(CN[:, :], consts).then_inc(consts_loaded, 16)
                sp.dma_start(WQR[:, :, :], feature_rows(a["L0_xcond_Wq"])).then_inc(score_w_loaded, 16)

            def load(key):
                b = key[1]
                if b:
                    sp.wait_ge(tensor_z, upto(tensor_z, ("z", TPB * b - 1, NZ - 1), "z"))
                sp.dma_start(CX[:, 0, :], a["ctx_1024"][b, 0:P, :]).then_inc(context_loaded, 16)
                sp.dma_start(CX[0:TAIL, 1, :], a["ctx_1024"][b, P:CTX, :]).then_inc(context_loaded, 16)
                if b:
                    sp.dma_start(WKR[:, :, :], feature_rows(a["L0_xcond_Wk"])).then_inc(context_loaded, 16)
                    sp.dma_start(WVR[:, :, :], feature_rows(a["L0_xcond_Wv"])).then_inc(context_loaded, 16)

            def context(key):
                b = key[1]
                if b:
                    sp.wait_ge(tensor_p, upto(tensor_p, ("p", TPB * b - 1, NZ - 1), "p"))
                    sp.wait_ge(gpsimd_h, upto(gpsimd_h, ("h", TPB * b - 1, NZ - 1), "l"))
                for q in range(NQ):
                    if q >= 2:
                        sp.wait_ge(tensor_vw, upto(tensor_vw, ("vw", b, q - 2), "m"))
                    for part in range(2):
                        rows = slice((1 + part) * D, (2 + part) * D)
                        for lo, hi, src in hidden_columns(q * QN, (q + 1) * QN, rows):
                            sp.dma_start((WS0, WS1)[q % 2][:, KC * part:KC * part + KC, lo:hi],
                                         feature_rows(src)).then_inc((slice_even_loaded, slice_odd_loaded)[q % 2], 16)
                    if b == 0 and q == 1:
                        sp.dma_start(X[:, 0, :, :], tokens_of(a["x"], 0)).then_inc(x_loaded[0], 16)
                        sp.dma_start(WNR[:, :, 0:D], feature_rows(a["L0_xcond_gate_w1"][0:D, :])).then_inc(hidden_w_loaded, 16)
                        for e in range(EXPERTS):
                            sp.dma_start(WNR[:, :, D + e * RH:D + (e + 1) * RH],
                                          feature_rows(a["L0_xcond_e_w1"][e, 0:D, :])).then_inc(hidden_w_loaded, 16)
                        sp.dma_start(GWR[:, :, :], feature_rows(a["L0_xcond_gate_w2"])).then_inc(small_w_loaded, 16)
                        sp.dma_start(WQ1R[:, :, :], feature_rows(a["L1_xcond_Wq"])).then_inc(small_w_loaded, 16)
                        for dst, src in ((GB, "L0_xcond_gate_b2"), (BP, "L1_xcond_bp"), (OB, "L0_xcond_out_b")):
                            sp.dma_start(dst[:, :], a[src].partition_broadcast(P)).then_inc(broadcasts_loaded, 16)
                        sp.dma_start(WSS[:, 0, :, :], feature_rows(a["L1_xcond_Wss_q"])).then_inc(modulation_w_loaded, 16)
                        sp.dma_start(WSS[:, 1, :, :], feature_rows(a["L1_xcond_Wss_kv"])).then_inc(modulation_w_loaded, 16)
                    if q == 1:
                        sp.wait_ge(vector_fold, upto(vector_fold, ("fold", b), "fill"))
                        for r in range(NQ):
                            for lo, hi, src in hidden_bias(r * QN, (r + 1) * QN):
                                sp.dma_start(B1T[32 * r + TAIL:32 * r + TAIL + 1, lo:hi],
                                             src.partition_broadcast(1)).then_inc(hidden_bias_loaded, 16)

            def tail(key):
                sp.wait_ge(vector_tail, upto(vector_tail, key, "tl"))
                for q in range(NQ):
                    for j, part in enumerate((TH, TH, TL)):
                        sp.dma_start(raw(VWD[32 * j:32 * j + 32, q * QN:(q + 1) * QN]),
                                     raw(part[32 * q:32 * q + 32, :])).then_inc(tails_placed, 16)

            def keyn(key):
                b = key[1]
                if b:
                    sp.wait_ge(tensor_proj, upto(tensor_proj, ("proj", TPB * b - 1, 1), "o"))
                    sp.wait_ge(vector_proj, upto(vector_proj, ("proj", TPB * b - 1, 1), "o"))
                else:
                    sp.wait_ge(tensor_cb, upto(tensor_cb, ("cb", 0), "cb"))
                    sp.wait_ge(vector_cb, upto(vector_cb, ("cb", 0), "cb"))
                    sp.wait_ge(scalar_split, upto(scalar_split, ("split", NSPLIT - 1), "h"))
                    sp.wait_ge(vector_split, upto(vector_split, ("split", NSPLIT - 1), "l"))
                sp.dma_start(CX1[:, 0, :], a["ctx_1024"][b, 0:P, :]).then_inc(kv_w_loaded, 16)
                sp.dma_start(CX1[0:TAIL, 1, :], a["ctx_1024"][b, P:CTX, :]).then_inc(kv_w_loaded, 16)
                sp.dma_start(WKV[:, :, :], feature_rows(a["L1_xcond_Wkv"])).then_inc(kv_w_loaded, 16)
                sp.dma_start(BV[:, :], a["L1_xcond_bkv"][D:2 * D].partition_broadcast(P)).then_inc(kv_w_loaded, 16)
                if b == 0:
                    sp.wait_ge(tensor_mod, upto(tensor_mod, ("mod", 0), "mod"))
                    for t in range(1, SLOTS):
                        sp.dma_start(X[:, t, :, :], tokens_of(a["x"], t)).then_inc(x_loaded[t], 16)

            def pair_keys(key):
                sp.wait_ge(vector_key, upto(vector_key, key, "kl"))
                for c in range(PAIRS):
                    f, r = c // 4, 32 * (c % 4)
                    for j, part in enumerate((KMH, KMH, KML)):
                        sp.dma_start(raw(KS[32 * j:32 * j + 32, c, :, :]),
                                     raw(part[r:r + 32, f, :, :])).then_inc(keys_placed, 16)

            def query(key):
                t = key[1]
                if t:
                    sp.wait_ge(tensor_proj, upto(tensor_proj, ("proj", t - 1, 1), "o"))
                for f in range(KC):
                    sp.wait_ge(scalar_query, upto(scalar_query, key, f"q{f}"))
                    sp.wait_ge(vector_query, upto(vector_query, key, f"q{f}"))
                    for c in range(4 * f, 4 * f + 4):
                        r = 32 * (c % 4)
                        for j, part in enumerate((QH, QL, QH)):
                            sp.dma_start(raw(QS[32 * j:32 * j + 32, c, :]),
                                         raw(part[r:r + 32, f, :])).then_inc(pair_placed[c], 16)

            def row(key):
                sp.wait_ge(scalar_row, upto(scalar_row, key, "h"))
                sp.wait_ge(vector_row, upto(vector_row, key, "l"))
                for j in range(2):
                    for i, part in enumerate((NMH, NML)):
                        dst = STACK + 2 * i + j
                        sp.dma_start(raw(QS[dst:dst + 1, :, :]),
                                     raw(part[PAIRS * j:PAIRS * j + PAIRS, :])).then_inc(maxima_placed, 16)

            def proj(key):
                t, h = key[1:]
                sp.wait_ge(vector_proj, upto(vector_proj, key, "o"))
                sp.dma_start(tokens_of(out, t)[:, 2 * h:2 * h + 2, :],
                             X[:, t % SLOTS, 2 * h:2 * h + 2, :]).then_inc(stored, 16)
                if h:
                    sp.wait_ge(stored, 32 * (t + 1))
                    if t + SLOTS < NT:
                        sp.dma_start(X[:, t % SLOTS, :, :], tokens_of(a["x"], t + SLOTS)).then_inc(x_loaded[t % SLOTS], 16)

            parts = {"setup": setup, "load": load, "ctx": context, "tail": tail, "keyn": keyn, "key": pair_keys, "query": query, "row": row, "proj": proj}
            for key in order("sync"):
                if key[0] in parts:
                    parts[key[0]](key)

        @block.scalar
        def _(act):
            def setup(key):
                act.dma_start(WKR[:, :, :], feature_rows(a["L0_xcond_Wk"])).then_inc(context_loaded, 16)
                act.dma_start(WVR[:, :, :], feature_rows(a["L0_xcond_Wv"])).then_inc(context_loaded, 16)
                act.dma_start(RW[:, :, :], feature_rows(a["L0_xcond_router_W"]),
                              allow_slow_non_contiguous=True).then_inc(router_loaded, 16)
                act.dma_start(RB[:, :], a["L0_xcond_router_b"].partition_broadcast(P)).then_inc(router_loaded, 16)
                act.wait_ge(tensor_setup, upto(tensor_setup, key, "wqT"))
                nc.scalar.copy(WQT[:, :, :], V0[:, :].rearrange("p (k n) -> p k n", k=KC)).then_inc(scalar_setup, 1)

            def silu(key):
                act.wait_ge(vector_vec, upto(vector_vec, ("vec", 0), "v"))
                nc.scalar.activation(TC[:, :, :], CO[:, :, :], ACT.Tanh, scale=0.5).then_inc(scalar_silu, 1)

            def split(key):
                high, full, loaded, count = ((WNh, WNR, hidden_w_loaded, 1 + EXPERTS), (GWh, GWR, small_w_loaded, 2),
                                             (WQh, WQ1R, small_w_loaded, 2), (WPh, WPR, proj_w_loaded, 4))[key[1]]
                act.wait_ge(loaded, 16 * count)
                nc.scalar.copy(high[:, :, :], full[:, :, :]).then_inc(scalar_split, 1)

            def context(key):
                b = key[1]
                act.wait_ge(tensor_ctx, upto(tensor_ctx, key, "ctxT"))
                nc.scalar.copy(CXT[:, :, 0:CTX], M0[:, 0:320].rearrange("p (k n) -> p k n", k=KC)[:, :, 0:CTX]).then_inc(scalar_ctx, 1)
                act.wait_ge(tensor_ctx, upto(tensor_ctx, key, "vT"))
                nc.scalar.copy(VTT[:, :, 0:CTX], Z[:, 1, 0:320].rearrange("p (k n) -> p k n", k=KC)[:, :, 0:CTX]).then_inc(scalar_ctx, 1)

            def fold(key):
                act.wait_ge(tensor_fold, upto(tensor_fold, key, "A"))
                nc.scalar.mul(A[:, :, 0:CTX], OFF[:, 0, 0:320].rearrange("p (k n) -> p k n", k=KC)[:, :, 0:CTX],
                                     float(D) ** -0.5).then_inc(scalar_fold, 1)

            def slice_w(key):
                b, q = key[1:]
                if b and q == 0:
                    act.wait_ge(vector_res, upto(vector_res, ("res", TPB * b - 1), "x"))
                act.wait_ge(tensor_vw, upto(tensor_vw, key, "m"))
                nc.scalar.copy(VWh[:, q * QN:(q + 1) * QN], Z[:, q % 2, 0:QN]).then_inc(scalar_vw, 1)
                nc.scalar.copy(TQ[:, q, :], (M0[:, 0:QN], OFF[:, 1, 0:QN])[q % 2]).then_inc(scalar_vw, 1)

            def w2_transposed(key):
                g = key[1]
                for k in range(KC):
                    act.wait_ge(tensor_w2t, upto(tensor_w2t, key, f"t{k}"))
                    nc.scalar.copy(W2T[:, k, PER * P * g:PER * P * (g + 1)], S[:, k, :]).then_inc(scalar_w2t, 1)

            def w2(key):
                g = key[1]
                for i in range(2):
                    act.wait_ge(tensor_w2, upto(tensor_w2, key, f"m{i}"))
                    j = 2 * g + i
                    nc.scalar.mul(W2h[:, 2 * j:2 * j + 2, :], (V0[:, :], OFF[:, 1, :])[i].rearrange("p (k n) -> p k n", k=2),
                                         0.5).then_inc(scalar_w2, 1)

            def keyx(key):
                b = key[1]
                act.wait_ge(tensor_keyx, upto(tensor_keyx, key, "t"))
                for m in range(KC):
                    nc.scalar.activation(KX[:, m, 0:CTX], V0[:, 160 * m:160 * m + CTX], ACT.Identity,
                                                scale=MOD[:, 4 + m, b:b + 1], bias=MOD[:, 6 + m, b:b + 1]).then_inc(scalar_keyx, 1)

            def norm(key):
                t = key[1]
                for m in range(KC):
                    act.wait_ge(tensor_norm, upto(tensor_norm, key, f"t{m}"))
                    nc.scalar.activation(NXf[:, m, :], Z[:, m, :], ACT.Identity, scale=GAM[:, m:m + 1],
                                                bias=BET[:, m:m + 1]).then_inc(scalar_norm, 1)

            def att(key):
                t, s = key[1:]
                act.wait_ge(vector_att, upto(vector_att, key, "t"))
                nc.scalar.activation(EB[:, s, :], (M0[:, 0:CTX], OFF[:, 0, 0:CTX])[s % 2], ACT.Exp,
                                            bias=SM0[:, s, 0:1], accum_out=SM0[:, s, 1:2]).then_inc(scalar_att, 1)

            def prob(key):
                t, s = key[1:]
                act.wait_ge(vector_prob, upto(vector_prob, key, "r"))
                nc.scalar.mul(PB[:, s, 0:P], EB[:, s, 0:P], SM0[:, s, 2:3])
                nc.scalar.mul(PB[:, s, P:P + 3 * 32].rearrange("p (j n) -> p j n", j=3)[:, :, 0:TAIL],
                              EB[:, s, P:CTX].unsqueeze(1).to_broadcast([P, 3, TAIL]), SM0[:, s, 2:3]).then_inc(scalar_prob, 1)

            def route(key):
                t = key[1]
                act.wait_ge(tensor_prob, upto(tensor_prob, ("prob", t, NSUB - 1), "p"))
                act.wait_ge(vector_low, upto(vector_low, ("low", t), "n1"))
                nc.scalar.copy(PTh[:, :], Z[:, 0, :]).then_inc(scalar_route, 1)
                nc.scalar.copy(PTD[0:STACK, :], Z[0:STACK, 1, :]).then_inc(scalar_route, 1)
                act.wait_ge(vector_route, upto(vector_route, key, "lg"))
                nc.scalar.activation(PR[:, :, :], LG[:, :, :], ACT.Exp).then_inc(scalar_route, 1)

            def hidden(key):
                t, k = key[1:]
                g = NZ * t + k
                act.wait_ge(tensor_z, upto(tensor_z, key, "z"))
                if g >= 2:
                    act.wait_ge(gpsimd_h, upto(gpsimd_h, ("h", (g - 2) // NZ, (g - 2) % NZ), "l"))
                nc.scalar.activation(TB[:, k % 2, :], Z[:, k % 2, :], ACT.Tanh, scale=0.5).then_inc(scalar_z, 1)

            def high(key):
                t, k = key[1:]
                g = NZ * t + k
                act.wait_ge(vector_z, upto(vector_z, ("z", t, k), "s"))
                if g >= RING:
                    act.wait_ge(tensor_p, upto(tensor_p, ("p", (g - RING) // NZ, (g - RING) % NZ), "p"))
                nc.scalar.copy(SH[:, k % RING, :], TB[:, k % 2, :]).then_inc(scalar_h, 1)

            def gate(key):
                t = key[1]
                act.wait_ge(tensor_p, upto(tensor_p, ("p", t, GATES - 1), "p"))
                if t % TPB == 0:
                    act.wait_ge(tails_placed, 16 * 3 * NQ * (t // TPB + 1))
                if t:
                    act.wait_ge(vector_res, upto(vector_res, ("res", t - 1), "x"))
                nc.scalar.activation(G[:, :, :], O[:, :, :], ACT.Tanh, scale=0.25).then_inc(scalar_gate, 1)

            def qx(key):
                t = key[1]
                b = t // TPB
                for m in range(KC):
                    act.wait_ge(tensor_qx, upto(tensor_qx, key, f"t{m}"))
                    nc.scalar.mul(XQh[:, m, :], S[:, m, :], MOD[:, m, b:b + 1]).then_inc(scalar_qx, 1)

            def query(key):
                t = key[1]
                b = t // TPB
                for f in range(KC):
                    act.wait_ge(tensor_query, upto(tensor_query, key, f"q{f}"))
                    if t:
                        act.wait_ge(tensor_proj, upto(tensor_proj, ("proj", t - 1, 1), "o"))
                    nc.scalar.activation(QH[:, f, :], (V0[:, :], S[:, 0, :])[f], ACT.Identity,
                                                bias=BQ[:, f, b:b + 1]).then_inc(scalar_query, 1)

            def row(key):
                t = key[1]
                act.wait_ge(tensor_row, upto(tensor_row, key, "m"))
                if t:
                    act.wait_ge(tensor_proj, upto(tensor_proj, ("proj", t - 1, 1), "o"))
                nc.scalar.mul(NMH[:, :], V0[0:HEADS, :], -1.0).then_inc(scalar_row, 1)

            def score(key):
                t, w = key[1:]
                g, i = divmod(w, 5)
                if g and i == 0:
                    act.wait_ge(tensor_value, upto(tensor_value, ("value", t, g - 1), "v"))
                act.wait_ge(tensor_score, upto(tensor_score, key, "s"))
                rows = P if i < 4 else 4 * TAIL
                nc.scalar.activation(E[0:rows, i, :], (S[0:rows, 0, :], S[0:rows, 1, :], M0[0:rows, :])[w % 3], ACT.Exp).then_inc(scalar_score, 1)

            def value(key):
                t, g = key[1:]
                act.wait_ge(tensor_value, upto(tensor_value, key, "v"))
                if g == 0:
                    act.wait_ge(maxima_placed, 16 * 4 * (t + 1))
                nc.scalar.copy(RAW[:, g, :], V0[:, :]).then_inc(scalar_value, 1)

            def outs(key):
                c = slice(D * key[2], D * key[2] + D)
                act.wait_ge(vector_out, upto(vector_out, key, "o"))
                nc.scalar.copy(AH[:, :, c], RAW[:, :, c]).then_inc(scalar_out, 1)

            parts = {"setup": setup, "ctx": context, "fold": fold, "vw": slice_w, "silu": silu, "split": split, "w2t": w2_transposed, "w2": w2,
                     "keyx": keyx, "norm": norm, "att": att, "prob": prob, "qx": qx,
                     "route": route, "z": hidden, "h": high, "gate": gate, "query": query, "row": row, "score": score,
                     "value": value, "out": outs}
            for key in order("scalar"):
                if key[0] in parts:
                    parts[key[0]](key)

        @block.vector
        def _(dve):
            v = nc.vector
            results = Count()

            def statistics(own_sem, key, chunks, stats, mean_var, source):
                for s, rows in chunks:
                    v.bn_stats(stats[0:rows, s, :], source(s)[0:rows, :]).then_inc(vector_results, results.one())
                dve.wait_ge(vector_results, results.n)
                for s, rows in chunks:
                    v.bn_aggr(mean_var[0:rows, s, :], stats[0:rows, s, :]).then_inc(vector_results, results.one())
                dve.wait_ge(vector_results, results.n)
                v.tensor_scalar(mean_var[:, :, 1], mean_var[:, :, 1], EPS, None, ALU.add).then_inc(own_sem, 1)

            def normal_form(chunks, mean_var, rstd, source, dst):
                for s, rows in chunks:
                    last = v.tensor_scalar(dst[0:rows, s, :], source(s)[0:rows, :], mean_var[0:rows, s, 0:1],
                                           rstd[0:rows, s:s + 1], ALU.subtract, ALU.mult)
                return last

            tokens = [(s, P) for s in range(NSUB)]

            def split_low(dst, full, high):
                return v.tensor_tensor(dst, full, raw(high), ALU.subtract)

            def setup(key):
                v.memset(HALF[:, :], -0.5)
                v.memset(MV2[:, :, :], 1.0)
                v.memset(VA[:, :, :], 0.0)
                v.memset(VT1[:, :, :], 0.0)
                v.memset(WPR[:, :, :], 0.0).then_inc(vector_setup, 1)
                dve.wait_ge(vector_setup, upto(vector_setup, key, "fill"))
                dve.wait_ge(consts_loaded, 16 * 1)
                for g in range(GROUPS):
                    v.memset(VA[:, 4 * g:4 * g + 4, DH + 4 * g:DH + 4 * g + 4], 1.0)
                    v.tensor_copy(VT1[:, 4 * g:4 * g + 4, DH + 4 * g:DH + 4 * g + 4],
                                  CN[0:4 * TAIL, C_ROW:C_ROW + 4].unsqueeze(2).to_broadcast([4 * TAIL, 4, 4]))

            def vectors(key):
                dve.wait_ge(tensor_vec, upto(tensor_vec, key, "v"))
                v.tensor_copy(VC[:, :], S[:, 0, 0:N_VROWS]).then_inc(vector_vec, 1)

            def silu(key):
                dve.wait_ge(scalar_silu, upto(scalar_silu, key, "tc"))
                v.scalar_tensor_tensor(out=COT[:, :, :], in0=TC[:, :, :], scalar=1.0, in1=CO[:, :, :],
                                              op0=ALU.add, op1=ALU.mult).then_inc(vector_silu, 1)

            def mod(key):
                dve.wait_ge(tensor_mod, upto(tensor_mod, key, "mod"))
                v.scalar_tensor_tensor(out=MOD[:, :, :], in0=V0[:, 0:8 * BATCH].rearrange("p (m b) -> p m b", m=8),
                                             scalar=0.5, in1=BSS[:, :].unsqueeze(2).to_broadcast([P, 8, BATCH]),
                                             op0=ALU.mult, op1=ALU.add).then_inc(vector_results, results.one())
                dve.wait_ge(vector_results, results.n)
                v.tensor_scalar(MOD[:, 0:2, :], MOD[:, 0:2, :], 1.0, None, ALU.add).then_inc(vector_results, results.one())
                v.tensor_scalar(MOD[:, 4:6, :], MOD[:, 4:6, :], 1.0, None, ALU.add).then_inc(vector_mod, 1)

            def query_bias(key):
                dve.wait_ge(tensor_bq, upto(tensor_bq, key, "bq"))
                v.tensor_tensor(BQ[:, :, :], V0[:, 64:64 + KC * BATCH].rearrange("p (f b) -> p f b", f=KC),
                                       BQ0[:, :].unsqueeze(2).to_broadcast([P, KC, BATCH]), ALU.add).then_inc(vector_bq, 1)

            def split(key):
                low, full, high = ((WNl, WNR, WNh), (GWl, GWR, GWh), (WQl, WQ1R, WQh), (WPl, WPR, WPh))[key[1]]
                dve.wait_ge(scalar_split, upto(scalar_split, key, "h"))
                split_low(low[:, :, :], full[:, :, :], high[:, :, :]).then_inc(vector_split, 1)

            def context(key):
                b = key[1]
                if b:
                    dve.wait_ge(tensor_z, upto(tensor_z, ("z", TPB * b - 1, NZ - 1), "z"))
                v.memset(B1T[:, :], 0.0)
                v.memset(AN[:, :, :], 0.0)
                v.memset(VTT[:, :, CTX:160], 0.0).then_inc(vector_results, results.one())
                dve.wait_ge(tensor_ctx, upto(tensor_ctx, key, "kT"))
                v.tensor_copy(KTT[:, :, 0:CTX], Z[:, 0, 0:320].rearrange("p (k n) -> p k n", k=KC)[:, :, 0:CTX]).then_inc(vector_ctx, 1)

            def fold(key):
                b = key[1]
                dve.wait_ge(vector_vec, upto(vector_vec, ("vec", 0), "v"))
                dve.wait_ge(vector_results, results.n)
                v.tensor_copy(AN[:, :, TAIL:TAIL + 1], CO[:, :, b:b + 1]).then_inc(vector_fold, 1)
                dve.wait_ge(tensor_fold, upto(tensor_fold, key, "VR"))
                v.tensor_copy(VR[:, :, :], OFF[:, 1, 0:480].rearrange("p (e n) -> p e n", e=EXPERTS)[:, :, 0:CTX]).then_inc(vector_fold, 1)
                dve.wait_ge(tensor_fold, upto(tensor_fold, key, "RC"))
                if b == 0:
                    dve.wait_ge(router_loaded, 16 * N_ROUTER)
                v.tensor_copy(A[:, :, CTX:CTX + EXPERTS], RW[:, 0:KC, :])
                v.tensor_tensor(RC[:, :], M0[:, 0:EXPERTS], RB[:, :], ALU.add).then_inc(vector_fold, 1)

            def slice_w(key):
                b, q = key[1:]
                dve.wait_ge(scalar_vw, upto(scalar_vw, key, "h"))
                v.tensor_tensor(VWl[:, q * QN:(q + 1) * QN], Z[:, q % 2, 0:QN],
                                raw(VWh[:, q * QN:(q + 1) * QN]), ALU.subtract).then_inc(vector_vw, 1)

            def tail(key):
                b = key[1]
                dve.wait_ge(tensor_tail, upto(tensor_tail, key, "m"))
                dve.wait_ge(hidden_bias_loaded, 16 * (N_HIDDEN_BIAS * (b + 1)))
                v.tensor_tensor(TF[:, :], M0[:, 0:QN], B1T[:, :], ALU.add).then_inc(vector_results, results.one())
                dve.wait_ge(vector_results, results.n)
                v.tensor_copy(TH[:, :], TF[:, :]).then_inc(vector_tail, 1)
                dve.wait_ge(vector_tail, upto(vector_tail, key, "th"))
                split_low(TL[:, :], TF[:, :], TH[:, :]).then_inc(vector_tail, 1)

            def w2(key):
                g = key[1]
                for i in range(2):
                    j = 2 * g + i
                    dve.wait_ge(scalar_w2, upto(scalar_w2, key, f"m{i}"))
                    v.scalar_tensor_tensor(out=W2l[:, 2 * j:2 * j + 2, :].rearrange("p k n -> p (k n)"),
                                                  in0=(V0[:, :], OFF[:, 1, :])[i], scalar=0.5,
                                                  in1=raw(W2h[:, 2 * j:2 * j + 2, :]).rearrange("p k n -> p (k n)"),
                                                  op0=ALU.mult, op1=ALU.subtract).then_inc(vector_w2, 1)

            def bias_out(key):
                dve.wait_ge(tensor_cb, upto(tensor_cb, key, "cb"))
                dve.wait_ge(broadcasts_loaded, 16 * N_BROADCAST)
                v.memset(raw(BROW[:, :]), 0.0).then_inc(vector_results, results.one())
                dve.wait_ge(vector_results, results.n)
                for r in (0, 32):
                    v.memset(raw(BROW[r:r + 1, :]), 1.0)
                v.tensor_scalar(CBF[:, 0, :], GB[0:64, :], 2.0, None, ALU.mult)
                v.tensor_tensor(CBF[:, 1:3, :], V0[0:64, :].rearrange("p (e n) -> p e n", e=2),
                                OB[0:64, :].unsqueeze(1).to_broadcast([64, 2, D]), ALU.add)
                v.tensor_tensor(CBF[:, 3, :], S[0:64, 0, 0:D], OB[0:64, :], ALU.add).then_inc(vector_results, results.one())
                dve.wait_ge(vector_results, results.n)
                v.tensor_copy(CBH[:, :, :], CBF[:, :, :]).then_inc(vector_results, results.one())
                dve.wait_ge(vector_results, results.n)
                v.tensor_copy(CB[0:32, :, :], raw(CBH[0:32, :, :]))
                split_low(CB[32:64, :, :], CBF[32:64, :, :], CBH[32:64, :, :]).then_inc(vector_cb, 1)

            def keyn(key):
                b = key[1]
                chunks = [(0, P), (1, TAIL)]
                dve.wait_ge(kv_w_loaded, 16 * (4 * (b + 1)))
                statistics(vector_keyn, key, chunks, ST2, MV2, lambda s: CX1[:, s, :])
                dve.wait_ge(gpsimd_keyn, upto(gpsimd_keyn, key, "rstd"))
                normal_form(chunks, MV2, RS2, lambda s: CX1[:, s, :], XH2).then_inc(vector_keyn, 1)

            def keyx(key):
                for m in range(KC):
                    dve.wait_ge(scalar_keyx, upto(scalar_keyx, key, f"x{m}"))
                    last = v.tensor_copy(KXR[:, m, :].rearrange("p (i n) -> p i n", i=4),
                                         KX[:, m, P:CTX].unsqueeze(1).to_broadcast([P, 4, TAIL]))
                last.then_inc(vector_keyx, 1)

            def pair_keys(key):
                dve.wait_ge(tensor_key, upto(tensor_key, key, "k"))
                for f in range(KC):
                    last = v.tensor_scalar(K1[:, f, 0:CTX], S[:, 0, 160 * f:160 * f + CTX], BK[:, f:f + 1],
                                           float(DH) ** -0.5, ALU.add, ALU.mult)
                last.then_inc(vector_key, 1)
                dve.wait_ge(vector_key, upto(vector_key, key, "k"))
                for f in range(KC):
                    for j in range(2):
                        last = v.tensor_scalar(KMH[:, f, j, :], K1[:, f, 0:CTX], CN[:, C_HEAD + j:C_HEAD + j + 1],
                                               None, ALU.mult)
                last.then_inc(vector_key, 1)
                dve.wait_ge(vector_key, upto(vector_key, key, "kh"))
                for f in range(KC):
                    for j in range(2):
                        last = v.scalar_tensor_tensor(out=KML[:, f, j, :], in0=K1[:, f, 0:CTX],
                                                      scalar=CN[:, C_HEAD + j:C_HEAD + j + 1],
                                                      in1=raw(KMH[:, f, j, :]), op0=ALU.mult, op1=ALU.subtract)
                last.then_inc(vector_key, 1)
                if key[1] == 0:
                    v.memset(KT[:, :, :, :].bitcast(F32), 0.0)
                v.memset(KS[STACK:KROWS, :, :, :].bitcast(F32), 1.0).then_inc(vector_results, results.one())
                dve.wait_ge(vector_results, results.n)
                for j in range(2):
                    last = v.tensor_scalar(KS[STACK:KROWS, :, j, :], raw(KS[STACK:KROWS, :, j, :]),
                                           CN[STACK:KROWS, C_PAIR + j:C_PAIR + j + 1], None, ALU.mult)
                last.then_inc(vector_key, 1)
                dve.wait_ge(tensor_key, upto(tensor_key, key, "v"))
                v.tensor_tensor(VA[:, :, 0:DH], S[:, 1, 0:D].rearrange("p (h r) -> p h r", r=DH),
                                       BV[:, :].rearrange("p (h r) -> p h r", r=DH), ALU.add).then_inc(vector_key, 1)
                dve.wait_ge(tensor_key, upto(tensor_key, key, "vt"))
                v.tensor_tensor(VTM[:, :], V0[0:4 * TAIL, 0:D], BV[0:4 * TAIL, :], ALU.add).then_inc(vector_results, results.one())
                dve.wait_ge(vector_results, results.n)
                for i in range(4):
                    last = v.tensor_scalar(VT1[:, i::4, 0:DH], VTM[:, :].rearrange("p (h r) -> p h r", r=DH)[:, i::4, :],
                                           CN[0:4 * TAIL, C_ROW + i:C_ROW + i + 1], None, ALU.mult)
                last.then_inc(vector_key, 1)

            def keyt(key):
                b = key[1]
                dve.wait_ge(keys_placed, 16 * 3 * PAIRS * (b + 1))
                for j in range(2):
                    last = v.tensor_copy(KT[:, j::2, 2 * j:2 * j + 2, :], raw(KS[:, j::2, :, P:CTX]))
                last.then_inc(vector_keyt, 1)

            def ln(key):
                t = key[1]
                dve.wait_ge(x_loaded[t % SLOTS], 16 * (t // SLOTS + 1))
                statistics(vector_ln, key, tokens, ST0, MV0, lambda s: X[:, t % SLOTS, s, :])

            def norm(key):
                t = key[1]
                if t % TPB == 0:
                    dve.wait_ge(tensor_tail, upto(tensor_tail, ("tail", t // TPB), "m"))
                    dve.wait_ge(vector_tail, upto(vector_tail, ("tail", t // TPB), "tl"))
                else:
                    dve.wait_ge(tensor_z, upto(tensor_z, ("z", t - 1, NZ - 1), "z"))
                dve.wait_ge(gpsimd_ln, upto(gpsimd_ln, ("ln", t), "rstd"))
                normal_form(tokens, MV0, RS0, lambda s: X[:, t % SLOTS, s, :], XH0).then_inc(vector_norm, 1)

            def low(key):
                t = key[1]
                dve.wait_ge(tensor_norm, upto(tensor_norm, ("norm", t), "t1"))
                for m in range(KC):
                    dve.wait_ge(scalar_norm, upto(scalar_norm, ("norm", t), f"n{m}"))
                    v.tensor_copy(NXh[:, m, :], NXf[:, m, :]).then_inc(vector_results, results.one())
                    dve.wait_ge(vector_results, results.n)
                    split_low(NXl[:, m, :], NXf[:, m, :], NXh[:, m, :]).then_inc(vector_low, 1)

            def att(key):
                t, s = key[1:]
                dve.wait_ge(tensor_att, upto(tensor_att, key, "s"))
                bank = (M0[:, 0:CTX], OFF[:, 0, 0:CTX])[s % 2]
                if s == 0:
                    v.memset(PB[:, :, P:D], 0.0).then_inc(vector_results, results.one())
                    dve.wait_ge(vector_results, results.n)
                    v.memset(PB[:, :, P:P + 3 * 32].rearrange("p r (j n) -> p r j n", j=3)[:, :, :, TAIL:TAIL + 1], 1.0).then_inc(vector_results, results.one())
                v.tensor_reduce(SM0[:, s, 0:1], bank, AX.X, ALU.max, negate=True)
                logits = (M0, OFF[:, 0, :])[s % 2][:, CTX:CTX + EXPERTS]
                v.tensor_tensor(LG[:, s, :], logits, RC[:, :], ALU.add).then_inc(vector_att, 1)

            def prob(key):
                t, s = key[1:]
                dve.wait_ge(scalar_att, upto(scalar_att, ("att", t, s), "e"))
                v.reciprocal(SM0[:, s, 2:3], SM0[:, s, 1:2]).then_inc(vector_prob, 1)
                dve.wait_ge(vector_prob, upto(vector_prob, key, "r"))
                if s == 0 and t:
                    dve.wait_ge(gpsimd_h, upto(gpsimd_h, ("h", t - 1, NZ - 1), "l"))
                for e in range(EXPERTS):
                    v.scalar_tensor_tensor(out=TB[:, 0, e * CTX:(e + 1) * CTX], in0=EB[:, s, :], scalar=SM0[:, s, 2:3],
                                                 in1=VR[:, e, :], op0=ALU.mult, op1=ALU.mult,
                                                 accum_out=EV[:, s, e:e + 1]).then_inc(vector_results, results.one())
                dve.wait_ge(vector_results, results.n)
                v.tensor_tensor(LG[:, s, :], LG[:, s, :], EV[:, s, :], ALU.add).then_inc(vector_prob, 1)

            def route(key):
                t = key[1]
                dve.wait_ge(vector_prob, upto(vector_prob, ("prob", t, NSUB - 1), "lg"))
                dve.wait_ge(scalar_route, upto(scalar_route, key, "pm"))
                v.tensor_tensor(PTl[:, :], Z[:, 0, :], raw(PTh[:, :]), ALU.subtract).then_inc(vector_route, 1)
                dve.wait_ge(scalar_route, upto(scalar_route, key, "pd"))
                v.tensor_tensor(PTD[32:64, :], Z[32:64, 1, :], raw(PTD[32:64, :]), ALU.subtract).then_inc(vector_route, 1)
                v.tensor_reduce(RT[:, :, 0], LG[:, :, :], AX.X, ALU.max).then_inc(vector_results, results.one())
                dve.wait_ge(vector_results, results.n)
                v.tensor_tensor(LG[:, :, :], LG[:, :, :], RT[:, :, 0:1].to_broadcast([P, NSUB, EXPERTS]),
                                       ALU.subtract).then_inc(vector_route, 1)
                dve.wait_ge(scalar_route, upto(scalar_route, key, "ex"))
                v.tensor_reduce(RT[:, :, 0], PR[:, :, :], AX.X, ALU.add).then_inc(vector_results, results.one())
                dve.wait_ge(vector_results, results.n)
                v.reciprocal(RT[:, :, 1], RT[:, :, 0]).then_inc(vector_results, results.one())
                dve.wait_ge(vector_results, results.n)
                v.tensor_tensor(PR[:, :, :], PR[:, :, :], RT[:, :, 1:2].to_broadcast([P, NSUB, EXPERTS]),
                                       ALU.mult).then_inc(vector_route, 1)

            def hidden(key):
                t, k = key[1:]
                dve.wait_ge(scalar_z, upto(scalar_z, key, "t"))
                v.scalar_tensor_tensor(out=TB[:, k % 2, :], in0=TB[:, k % 2, :], scalar=1.0, in1=Z[:, k % 2, :],
                                              op0=ALU.add, op1=ALU.mult).then_inc(vector_z, 1)

            def evac(key):
                t, j = key[1:]
                dve.wait_ge(tensor_p, upto(tensor_p, ("p", t, GATES + PER * j - 1), "p"))
                if j == 1:
                    dve.wait_ge(vector_route, upto(vector_route, ("route", t), "prob"))
                    if t % TPB == 0:
                        dve.wait_ge(tails_placed, 16 * 3 * NQ * (t // TPB + 1))
                else:
                    dve.wait_ge(vector_evac, upto(vector_evac, ("evac", t, j - 1), "o"))
                for s in range(NSUB):
                    if j == 1:
                        last = v.tensor_scalar(ACC[:, s, :], O[:, s, :], PR[:, s, 0:1], None, ALU.mult)
                    else:
                        last = v.scalar_tensor_tensor(out=ACC[:, s, :], in0=O[:, s, :], scalar=PR[:, s, j - 1:j],
                                                      in1=ACC[:, s, :], op0=ALU.mult, op1=ALU.add)
                last.then_inc(vector_evac, 1)

            def res(key):
                t = key[1]
                dve.wait_ge(scalar_gate, upto(scalar_gate, ("gate", t), "g"))
                dve.wait_ge(vector_evac, upto(vector_evac, ("evac", t, EXPERTS), "o"))
                v.scalar_tensor_tensor(out=ACC[:, :, :], in0=G[:, :, :], scalar=1.0, in1=ACC[:, :, :],
                                              op0=ALU.add, op1=ALU.mult).then_inc(vector_res, 1)
                dve.wait_ge(vector_res, upto(vector_res, key, "u"))
                v.scalar_tensor_tensor(out=X[:, t % SLOTS, :, :], in0=ACC[:, :, :], scalar=0.5,
                                              in1=X[:, t % SLOTS, :, :], op0=ALU.mult, op1=ALU.add).then_inc(vector_res, 1)

            def qn(key):
                t = key[1]
                dve.wait_ge(vector_res, upto(vector_res, ("res", t), "x"))
                statistics(vector_qn, key, tokens, ST1, MV1, lambda s: X[:, t % SLOTS, s, :])

            def qx(key):
                t = key[1]
                b = t // TPB
                dve.wait_ge(gpsimd_qn, upto(gpsimd_qn, ("qn", t), "rstd"))
                if t:
                    dve.wait_ge(tensor_value, upto(tensor_value, ("value", t - 1, GROUPS - 1), "v"))
                if t % TPB == 0:
                    dve.wait_ge(tensor_key, upto(tensor_key, ("key", b), "vt"))
                normal_form(tokens, MV1, RS1, lambda s: X[:, t % SLOTS, s, :], XH1).then_inc(vector_qx, 1)

            def qlow(key):
                t = key[1]
                b = t // TPB
                for m in range(KC):
                    dve.wait_ge(scalar_qx, upto(scalar_qx, ("qx", t), f"x{m}"))
                    v.scalar_tensor_tensor(out=XQl[:, m, :], in0=S[:, m, :], scalar=MOD[:, m, b:b + 1],
                                                  in1=raw(XQh[:, m, :]), op0=ALU.mult, op1=ALU.subtract).then_inc(vector_qlow, 1)

            def query(key):
                t = key[1]
                b = t // TPB
                for f in range(KC):
                    dve.wait_ge(scalar_query, upto(scalar_query, key, f"q{f}"))
                    v.scalar_tensor_tensor(out=QL[:, f, :], in0=(V0[:, :], S[:, 0, :])[f],
                                                  scalar=BQ[:, f, b:b + 1], in1=raw(QH[:, f, :]),
                                                  op0=ALU.add, op1=ALU.subtract).then_inc(vector_query, 1)

            def most(key):
                t, u = key[1:]
                c, s = divmod(u, NSUB)
                bank = (S[:, 0, :], S[:, 1, :], V0[:, :])[u % 3]
                dve.wait_ge(tensor_most, upto(tensor_most, key, "s"))
                v.tensor_reduce(MX[:, s, :, c], bank[:, 0:2 * CTX].rearrange("p (j n) -> p j n", j=2),
                                AX.X, ALU.max).then_inc(vector_most, 1)

            def row(key):
                dve.wait_ge(scalar_row, upto(scalar_row, key, "h"))
                v.scalar_tensor_tensor(out=NML[:, :], in0=V0[0:HEADS, :], scalar=-1.0, in1=raw(NMH[:, :]),
                                              op0=ALU.mult, op1=ALU.subtract).then_inc(vector_row, 1)

            def sums(key):
                t, h = key[1:]
                c = slice(D * h, D * h + D)
                dve.wait_ge(gpsimd_sum, upto(gpsimd_sum, ("sum", t, GROUPS - 1), "s"))
                v.reciprocal(SUM[:, c], SUM[:, c]).then_inc(vector_sums, 1)

            def outs(key):
                t, h = key[1:]
                c = slice(D * h, D * h + D)
                dve.wait_ge(vector_sums, upto(vector_sums, ("sums", t, h), "r"))
                if h:
                    dve.wait_ge(vector_out, upto(vector_out, ("out", t, 0), "o"))
                for g in range(GROUPS):
                    v.stream_shuffle(SD[:, g, :], SUM[:, c], [DH + 4 * g] * 32).then_inc(vector_results, results.one())
                dve.wait_ge(vector_results, results.n)
                v.tensor_tensor(RAW[:, :, c], RAW[:, :, c], SD[:, :, :], ALU.mult).then_inc(vector_out, 1)

            def outs_low(key):
                t, h = key[1:]
                c = slice(D * h, D * h + D)
                dve.wait_ge(scalar_out, upto(scalar_out, ("out", t, h), "h"))
                split_low(AL[:, :, c], RAW[:, :, c], AH[:, :, c]).then_inc(vector_outl, 1)

            def proj(key):
                t, h = key[1:]
                dve.wait_ge(gpsimd_bias, upto(gpsimd_bias, ("bias", t), "x"))
                dve.wait_ge(tensor_proj, upto(tensor_proj, key, "o"))
                x = X[:, t % SLOTS, 2 * h:2 * h + 2, :].rearrange("p s d -> p (s d)")
                v.tensor_tensor(x, S[:, h, :], x, ALU.add).then_inc(vector_proj, 1)

            parts = {"setup": setup, "ctx": context, "vec": vectors, "fold": fold, "vw": slice_w, "tail": tail,
                     "silu": silu, "mod": mod, "bq": query_bias, "split": split, "w2": w2, "cb": bias_out, "keyn": keyn,
                     "keyx": keyx, "key": pair_keys, "keyt": keyt, "ln": ln, "norm": norm, "low": low, "att": att,
                     "prob": prob, "route": route, "z": hidden, "evac": evac, "res": res, "qn": qn, "qx": qx,
                     "qlow": qlow, "query": query, "most": most, "row": row, "sums": sums, "out": outs, "outl": outs_low,
                     "proj": proj}
            for key in order("vector"):
                if key[0] in parts:
                    parts[key[0]](key)

        @block.gpsimd
        def _(pool):
            def setup(key):
                rows = [(V_GAMMA, a["L0_xcond_ln_gamma"]), (V_BETA, a["L0_xcond_ln_beta"]),
                        (V_COND, a["cond_1024"].rearrange("b n -> (b n)")),
                        (V_B2, a["L0_xcond_e_b2"].rearrange("e n -> (e n)")),
                        (V_BSS, a["L1_xcond_bss_q"]), (V_BSS + 4, a["L1_xcond_bss_kv"]),
                        (V_BQ, a["L1_xcond_bq"]), (V_BK, a["L1_xcond_bkv"][0:D])]
                assert len(rows) == N_ROWS
                for row0, vector in rows:
                    chunks = vector.shape[0] // P
                    pool.dma_start(VROWS[row0:row0 + chunks, :], vector.rearrange("(k p) -> k p", p=P)).then_inc(rows_loaded, 16)
                for e in range(EXPERTS):
                    pool.dma_start(W2R[:, PER * e:PER * e + PER, :],
                                  feature_rows(a["L0_xcond_e_w2"][e])).then_inc(w2_loaded, 16)
                pool.dma_start(OW[:, :, :], feature_rows(a["L0_xcond_out_w"])).then_inc(w2_loaded, 16)

                heads = a["L1_xcond_Wp"].rearrange("(g i r) n -> i r g n", i=4, r=DH)
                pool.wait_ge(vector_setup, upto(vector_setup, ("setup", 0), "fill"))
                for i in range(4):
                    pool.dma_start(WPR[32 * i:32 * i + DH, :, :], heads[i]).then_inc(proj_w_loaded, 16)

            def rstd(key, var_sem, own_sem, dst, mv):
                pool.wait_ge(var_sem, upto(var_sem, key, "var"))
                nc.gpsimd.tensor_tensor(dst, mv, HALF[:, 0:dst.shape[1]], ALU.pow).then_inc(own_sem, 1)

            def keyn(key):
                rstd(key, vector_keyn, gpsimd_keyn, RS2[:, :], MV2[:, :, 1])

            def ln(key):
                rstd(key, vector_ln, gpsimd_ln, RS0[:, :], MV0[:, :, 1])

            def qn(key):
                rstd(key, vector_qn, gpsimd_qn, RS1[:, :], MV1[:, :, 1])

            def hidden(key):
                t, k = key[1:]
                pool.wait_ge(scalar_h, upto(scalar_h, ("h", t, k), "h"))
                if NZ * t + k >= RING:
                    g = NZ * t + k - RING
                    pool.wait_ge(tensor_p, upto(tensor_p, ("p", g // NZ, g % NZ), "p"))
                nc.gpsimd.tensor_tensor(SL[:, k % RING, :], TB[:, k % 2, :], raw(SH[:, k % RING, :]),
                                               ALU.subtract).then_inc(gpsimd_h, 1)

            def bias(key):
                t = key[1]
                pool.wait_ge(vector_qx, upto(vector_qx, ("qx", t), "xh"))
                nc.gpsimd.tensor_tensor(X[:, t % SLOTS, :, :], X[:, t % SLOTS, :, :],
                                               BP[:, :].unsqueeze(1).to_broadcast([P, NSUB, D]), ALU.add).then_inc(gpsimd_bias, 1)

            def sums(key):
                t, g = key[1:]
                pool.wait_ge(scalar_value, upto(scalar_value, ("value", t, g), "v"))
                if g > 1:
                    pool.wait_ge(gpsimd_sum, upto(gpsimd_sum, ("sum", t, g - 1), "s"))
                nc.gpsimd.tensor_tensor(SUM[:, :], RAW[:, 0, :] if g == 1 else SUM[:, :], RAW[:, g, :],
                                        ALU.add).then_inc(gpsimd_sum, 1)

            parts = {"setup": setup, "sum": sums, "keyn": keyn, "ln": ln, "qn": qn, "h": hidden, "bias": bias}
            for key in order("gpsimd"):
                if key[0] in parts:
                    parts[key[0]](key)

        @block.tensor
        def _(pe):
            mm = nc.tensor.matmul

            def exact(out_, left, right, start, stop, skip=False):
                (lh, ll), (rh, rl) = left, right
                mm(out_, lh, rh, start=start, stop=False, skip_group_check=skip)
                mm(out_, ll, rh, start=False, stop=False, skip_group_check=skip)
                return mm(out_, lh, rl, start=False, stop=stop, skip_group_check=skip)

            def plain(out_, pairs):
                for i, (l, r) in enumerate(pairs):
                    last = mm(out_, l, r, start=(i == 0), stop=(i == len(pairs) - 1))
                return last

            def setup(key):
                pe.wait_ge(consts_loaded, 16 * 1)
                pe.wait_ge(score_w_loaded, 16 * 1)
                for m in range(KC):
                    for k in range(KC):
                        last = pe.transpose(V0[:, D * m + P * k:D * m + P * k + P], WQR[:, k, P * m:P * m + P], ident)
                last.then_inc(tensor_setup, 1)

            def vectors(key):
                pe.wait_ge(rows_loaded, 16 * N_ROWS)
                pe.transpose(S[:, 0, 0:N_VROWS], VROWS[0:N_VROWS, :], CN[0:N_VROWS, C_ID:C_ID + N_VROWS]).then_inc(tensor_vec, 1)

            def mod(key):
                pe.wait_ge(modulation_w_loaded, 16 * 2)
                pe.wait_ge(vector_silu, upto(vector_silu, ("silu", 0), "sc"))
                pe.wait_ge(vector_cb, upto(vector_cb, ("cb", 0), "cb"))
                for w in range(2):
                    for m in range(4):
                        c = BATCH * (4 * w + m)
                        last = plain(V0[:, c:c + BATCH], [(WSS[:, w, k, P * m:P * m + P], COT[:, k, :]) for k in range(KC)])
                last.then_inc(tensor_mod, 1)

            def query_bias(key):
                pe.wait_ge(vector_mod, upto(vector_mod, ("mod", 0), "mod"))
                pe.wait_ge(small_w_loaded, 16 * 2)
                for f in range(KC):
                    last = plain(V0[:, 64 + BATCH * f:64 + BATCH * f + BATCH],
                                 [(WQ1R[:, k, P * f:P * f + P], MOD[:, 2 + k, :]) for k in range(KC)])
                last.then_inc(tensor_bq, 1)

            def context(key):
                b = key[1]
                pe.wait_ge(context_loaded, 16 * (4 * (b + 1)))
                if b:
                    pe.wait_ge(vector_z, upto(vector_z, ("z", TPB * b - 1, NZ - 1), "s"))
                    pe.wait_ge(vector_evac, upto(vector_evac, ("evac", TPB * b - 1, EXPERTS), "o"))
                    pe.wait_ge(scalar_score, upto(scalar_score, ("score", TPB * b - 2, 5 * GROUPS - 1), "e"))
                for k in range(KC):
                    pe.transpose(M0[:, 160 * k:160 * k + P], CX[:, 0, P * k:P * k + P], ident)
                    last = pe.transpose(M0[:, 160 * k + P:160 * k + CTX], CX[0:TAIL, 1, P * k:P * k + P],
                                        CN[0:TAIL, C_ID:C_ID + TAIL])
                last.then_inc(tensor_ctx, 1)
                pe.wait_ge(scalar_ctx, upto(scalar_ctx, key, "ctxT"))
                for step, bank, w in (("kT", Z[:, 0, :], WKR), ("vT", Z[:, 1, :], WVR)):
                    for m in range(KC):
                        last = plain(bank[:, 160 * m:160 * m + CTX],
                                     [(w[:, k, P * m:P * m + P], CXT[:, k, 0:CTX]) for k in range(KC)])
                    last.then_inc(tensor_ctx, 1)

            def fold(key):
                b = key[1]
                pe.wait_ge(vector_ctx, upto(vector_ctx, ("ctx", b), "kT"))
                if b == 0:
                    pe.wait_ge(vector_vec, upto(vector_vec, ("vec", 0), "v"))
                    pe.wait_ge(scalar_setup, upto(scalar_setup, ("setup", 0), "wqT"))
                    pe.wait_ge(router_loaded, 16 * N_ROUTER)
                for m in range(KC):
                    last = plain(OFF[:, 0, 160 * m:160 * m + CTX],
                                 [(WQT[:, k, P * m:P * m + P], KTT[:, k, 0:CTX]) for k in range(KC)])
                last.then_inc(tensor_fold, 1)
                pe.wait_ge(scalar_ctx, upto(scalar_ctx, ("ctx", b), "vT"))
                for e in range(EXPERTS):
                    last = plain(OFF[:, 1, 160 * e:160 * e + CTX],
                                 [(RW[:, KC + k, e:e + 1].to_broadcast([P, P]), VTT[:, k, 0:CTX]) for k in range(KC)])
                last.then_inc(tensor_fold, 1)
                last = plain(M0[:, 0:EXPERTS],
                             [(CO[:, k, b:b + 1].to_broadcast([P, P]), RW[:, 2 * KC + k, :]) for k in range(KC)])
                last.then_inc(tensor_fold, 1)

            def slice_w(key):
                b, q = key[1:]
                slot = (WS0, WS1)[q % 2]
                pe.wait_ge((slice_even_loaded, slice_odd_loaded)[q % 2], 16 * slices_loaded(b, q))
                if q == 0:
                    pe.wait_ge(vector_fold, upto(vector_fold, ("fold", b), "RC"))
                    pe.wait_ge(scalar_fold, upto(scalar_fold, ("fold", b), "A"))
                elif q >= 2:
                    pe.wait_ge(vector_vw, upto(vector_vw, ("vw", b, q - 2), "l"))
                    pe.wait_ge(scalar_vw, upto(scalar_vw, ("vw", b, q - 2), "t"))
                plain(Z[:, q % 2, 0:QN], [(VTT[:, k, 0:P], slot[:, k, :]) for k in range(KC)])
                bank = (M0[:, 0:QN], OFF[:, 1, 0:QN])[q % 2]
                rows = [VTT[:, k, P:160] for k in range(KC)] + [AN[:, k, :] for k in range(KC)]
                for k in range(2 * KC):
                    last = mm(bank[32 * k:32 * k + 32, :], rows[k], slot[:, k, :], start=True, stop=True)
                last.then_inc(tensor_vw, 1)

            def tail(key):
                b = key[1]
                pe.wait_ge(scalar_vw, upto(scalar_vw, ("vw", b, NQ - 1), "t"))
                for q in range(NQ):
                    last = mm(M0[32 * q:32 * q + 32, 0:QN], CN[:, C_FOLD:C_FOLD + 32], TQ[:, q, :], start=True, stop=True)
                last.then_inc(tensor_tail, 1)

            def w2_transposed(key):
                g = key[1]
                if g == 0:
                    pe.wait_ge(w2_loaded, 16 * (EXPERTS + 1))
                for k in range(KC):
                    if g:
                        pe.wait_ge(scalar_w2t, upto(scalar_w2t, ("w2t", g - 1), f"t{k}"))
                    for r in range(4):
                        last = pe.transpose(S[:, k, P * r:P * r + P], W2R[:, 4 * g + r, P * k:P * k + P], ident)
                    last.then_inc(tensor_w2t, 1)

            def w2(key):
                g = key[1]
                pe.wait_ge(scalar_w2t, upto(scalar_w2t, ("w2t", g), "t1"))
                for i in range(2):
                    if g:
                        pe.wait_ge(vector_w2, upto(vector_w2, ("w2", g - 1), f"m{i}"))
                    for r in range(2):
                        row0 = P * (4 * g + 2 * i + r)
                        last = plain((V0[:, :], OFF[:, 1, :])[i][:, D * r:D * r + D],
                                     [(W2T[:, k, row0:row0 + P], OW[:, k, :]) for k in range(KC)])
                    last.then_inc(tensor_w2, 1)

            def bias_out(key):
                pe.wait_ge(scalar_setup, upto(scalar_setup, ("setup", 0), "wqT"))
                pe.wait_ge(vector_w2, upto(vector_w2, ("w2", EXPERTS - 1), "m1"))
                for e in range(EXPERTS):
                    last = plain((V0[0:64, 0:D], V0[0:64, D:2 * D], S[0:64, 0, 0:D])[e],
                                 [(B2T[:, k, e:e + 1].to_broadcast([P, 64]), OW[:, k, :]) for k in range(KC)])
                last.then_inc(tensor_cb, 1)

            def keyx(key):
                b = key[1]
                pe.wait_ge(vector_keyn, upto(vector_keyn, key, "xh"))
                if b:
                    pe.wait_ge(vector_proj, upto(vector_proj, ("proj", TPB * b - 1, 1), "o"))
                else:
                    pe.wait_ge(vector_bq, upto(vector_bq, ("bq", 0), "bq"))
                for k in range(KC):
                    pe.transpose(V0[:, 160 * k:160 * k + P], XH2[:, 0, P * k:P * k + P], ident)
                    last = pe.transpose(V0[:, 160 * k + P:160 * k + CTX], XH2[0:TAIL, 1, P * k:P * k + P],
                                        CN[0:TAIL, C_ID:C_ID + TAIL])
                last.then_inc(tensor_keyx, 1)

            def pair_keys(key):
                b = key[1]
                pe.wait_ge(scalar_keyx, upto(scalar_keyx, key, "x1"))
                pe.wait_ge(kv_w_loaded, 16 * (4 * (b + 1)))
                for f in range(KC):
                    last = plain(S[:, 0, 160 * f:160 * f + CTX],
                                 [(WKV[:, k, P * f:P * f + P], KX[:, k, 0:CTX]) for k in range(KC)])
                last.then_inc(tensor_key, 1)
                plain(S[:, 1, 0:D], [(KX[:, k, 0:P], WKV[:, k, D:2 * D]) for k in range(KC)]).then_inc(tensor_key, 1)
                pe.wait_ge(vector_keyx, upto(vector_keyx, key, "rep"))
                plain(V0[0:4 * TAIL, 0:D], [(KXR[:, k, :], WKV[:, k, D:2 * D]) for k in range(KC)]).then_inc(tensor_key, 1)

            def norm(key):
                t = key[1]
                pe.wait_ge(vector_norm, upto(vector_norm, key, "xh"))
                for m in range(KC):
                    if t % TPB == 0:
                        pe.wait_ge(vector_vw, upto(vector_vw, ("vw", t // TPB, NQ - 2 + m), "l"))
                    else:
                        pe.wait_ge(vector_z, upto(vector_z, ("z", t - 1, NZ - 2 + m), "s"))
                    for s in range(NSUB):
                        last = pe.transpose(Z[:, m, P * s:P * s + P], XH0[:, s, P * m:P * m + P], ident)
                    last.then_inc(tensor_norm, 1)

            def att(key):
                t, s = key[1:]
                pe.wait_ge(scalar_norm, upto(scalar_norm, ("norm", t), "n1"))
                if s == 0 and t >= 2:
                    pe.wait_ge(scalar_score, upto(scalar_score, ("score", t - 2, 5 * GROUPS - 1), "e"))
                if s >= 2:
                    pe.wait_ge(vector_att, upto(vector_att, ("att", t, s - 2), "t"))
                    pe.wait_ge(scalar_att, upto(scalar_att, ("att", t, s - 2), "e"))
                elif t % TPB == 0:
                    pe.wait_ge(vector_tail, upto(vector_tail, ("tail", t // TPB), "th"))
                    pe.wait_ge(vector_fold, upto(vector_fold, ("fold", t // TPB), "RC"))
                    pe.wait_ge(scalar_vw, upto(scalar_vw, ("vw", t // TPB, NQ - 1), "t"))
                elif s == 0:
                    pe.wait_ge(vector_att, upto(vector_att, ("att", t - 1, 2), "t"))
                    pe.wait_ge(scalar_att, upto(scalar_att, ("att", t - 1, 2), "e"))
                else:
                    pe.wait_ge(vector_evac, upto(vector_evac, ("evac", t - 1, EXPERTS), "o"))
                plain((M0[:, 0:CTX + EXPERTS], OFF[:, 0, 0:CTX + EXPERTS])[s % 2],
                      [(NXf[:, k, P * s:P * s + P], A[:, k, :]) for k in range(KC)]).then_inc(tensor_att, 1)

            def prob(key):
                t, s = key[1:]
                pe.wait_ge(scalar_prob, upto(scalar_prob, key, "p"))
                pe.transpose(Z[:, 0, P * s:P * s + P], PB[:, s, 0:P], ident)
                pe.transpose(Z[0:STACK, 1, P * s:P * s + P], PB[:, s, P:P + STACK], ident).then_inc(tensor_prob, 1)

            def hidden(key):
                t, k = key[1:]
                if k < 2:
                    pe.wait_ge(vector_low, upto(vector_low, ("low", t), "n1"))
                    pe.wait_ge(vector_route, upto(vector_route, ("route", t), "dl"))
                    if t == 0:
                        pe.wait_ge(vector_split, upto(vector_split, ("split", 0), "l"))
                    if t % TPB == 0:
                        pe.wait_ge(tails_placed, 16 * 3 * NQ * (t // TPB + 1))
                else:
                    pe.wait_ge(vector_z, upto(vector_z, ("z", t, k - 2), "s"))
                c = slice(P * k, P * k + P)
                bank = Z[:, k % 2, :]
                for m in range(KC):
                    exact(bank, (WNh[:, m, c], WNl[:, m, c]), (NXh[:, m, :], NXl[:, m, :]), m == 0, False)
                exact(bank, (VWh[:, c], VWl[:, c]), (PTh[:, :], PTl[:, :]), False, False)
                mm(bank, VWD[:, c], PTD[0:STACK, :], start=False, stop=True).then_inc(tensor_z, 1)

            def second(key):
                t, k = key[1:]
                pe.wait_ge(scalar_h, upto(scalar_h, ("h", t, k), "h"))
                pe.wait_ge(gpsimd_h, upto(gpsimd_h, ("h", t, k), "l"))
                first = k in (0, GATES) or (k >= GATES and (k - GATES) % PER == 0)
                last_one = k == GATES - 1 or (k >= GATES and (k - GATES) % PER == PER - 1)
                if first:
                    if k == 0:
                        pe.wait_ge(vector_prob, upto(vector_prob, ("prob", t, NSUB - 1), "lg"))
                        if t:
                            pe.wait_ge(vector_evac, upto(vector_evac, ("evac", t - 1, EXPERTS), "o"))
                        else:
                            pe.wait_ge(vector_split, upto(vector_split, ("split", 1), "l"))
                    elif k == GATES:
                        pe.wait_ge(scalar_gate, upto(scalar_gate, ("gate", t), "g"))
                    else:
                        pe.wait_ge(vector_evac, upto(vector_evac, ("evac", t, (k - GATES) // PER), "o"))
                if last_one and k == GATES - 1 and t == 0:
                    pe.wait_ge(vector_cb, upto(vector_cb, ("cb", 0), "cb"))
                wh, wl = (GWh[:, k, :], GWl[:, k, :]) if k < GATES else (W2h[:, k - GATES, :], W2l[:, k - GATES, :])
                for s in range(NSUB):
                    c = slice(P * s, P * s + P)
                    last = exact(O[:, s, :], (SH[:, k % RING, c], SL[:, k % RING, c]), (wh, wl),
                                 first and s % 2 == 0, False, skip=True)
                    if last_one:
                        j = 0 if k < GATES else 1 + (k - GATES) // PER
                        last = mm(O[:, s, :], BROW[0:64, :], CB[:, j, :], start=False, stop=True, skip_group_check=True)
                last.then_inc(tensor_p, 1)

            def qx(key):
                t = key[1]
                pe.wait_ge(vector_qx, upto(vector_qx, key, "xh"))
                if t % TPB == 0:
                    pe.wait_ge(vector_key, upto(vector_key, ("key", t // TPB), "vt"))
                if t:
                    pe.wait_ge(vector_proj, upto(vector_proj, ("proj", t - 1, 1), "o"))
                for m in range(KC):
                    for s in range(NSUB):
                        last = pe.transpose(S[:, m, P * s:P * s + P], XH1[:, s, P * m:P * m + P], ident)
                    last.then_inc(tensor_qx, 1)

            def query(key):
                t = key[1]
                pe.wait_ge(vector_qlow, upto(vector_qlow, ("qlow", t), "x1"))
                if t == 0:
                    pe.wait_ge(vector_split, upto(vector_split, ("split", 2), "l"))
                for f in range(KC):
                    for k in range(KC):
                        c = slice(P * f, P * f + P)
                        last = exact((V0[:, :], S[:, 0, :])[f], (WQh[:, k, c], WQl[:, k, c]), (XQh[:, k, :], XQl[:, k, :]),
                                     k == 0, k == KC - 1)
                    last.then_inc(tensor_query, 1)

            def most(key):
                t, u = key[1:]
                c, s = divmod(u, NSUB)
                if s == 0:
                    pe.wait_ge(pair_placed[c], 16 * 3 * (t + 1))
                if u == 0:
                    pe.wait_ge(vector_query, upto(vector_query, ("query", t), "q1"))
                    if t % TPB == 0:
                        pe.wait_ge(vector_keyt, upto(vector_keyt, ("keyt", t // TPB), "kt"))
                        pe.wait_ge(keys_placed, 16 * 3 * PAIRS * (t // TPB + 1))
                if u >= 3:
                    pe.wait_ge(vector_most, upto(vector_most, ("most", t, u - 3), "s"))
                mm((S[:, 0, :], S[:, 1, :], V0[:, :])[u % 3][:, 0:2 * CTX], QS[0:STACK, c, P * s:P * s + P],
                   KS[0:STACK, c, :, :].rearrange("p j n -> p (j n)"), start=True, stop=True).then_inc(tensor_most, 1)

            def row(key):
                t = key[1]
                pe.wait_ge(vector_most, upto(vector_most, ("most", t, NSUB * PAIRS - 1), "s"))
                for s in range(NSUB):
                    last = pe.transpose(V0[0:HEADS, P * s:P * s + P], MX[:, s, :, :].rearrange("p j c -> p (j c)"), ident)
                last.then_inc(tensor_row, 1)

            def score(key):
                t, w = key[1:]
                g, i = divmod(w, 5)
                if w == 0:
                    pe.wait_ge(maxima_placed, 16 * 4 * (t + 1))
                if w == 2 and t + 1 < NT:
                    pe.wait_ge(vector_att, upto(vector_att, ("att", t + 1, 2), "t"))
                    pe.wait_ge(scalar_att, upto(scalar_att, ("att", t + 1, 2), "e"))
                if w >= 3:
                    pe.wait_ge(scalar_score, upto(scalar_score, ("score", t, w - 3), "e"))
                bank = (S[:, 0, :], S[:, 1, :], M0[:, :])[w % 3]
                if i < 4:
                    c = 2 * g + i // 2
                    last = mm(bank, KS[:, c, i % 2, 0:P], QS[:, c, :], start=True, stop=True)
                else:
                    for j in range(2):
                        c = 2 * g + j
                        last = mm(bank[0:4 * TAIL, :], KT[:, c, :, :].rearrange("p i n -> p (i n)"), QS[:, c, :],
                                  start=(j == 0), stop=(j == 1))
                last.then_inc(tensor_score, 1)

            def value(key):
                t, g = key[1:]
                pe.wait_ge(scalar_score, upto(scalar_score, ("score", t, 5 * g + 4), "e"))
                if g:
                    pe.wait_ge(scalar_value, upto(scalar_value, ("value", t, g - 1), "v"))
                else:
                    pe.wait_ge(vector_row, upto(vector_row, ("row", t), "l"))
                for i in range(4):
                    mm(V0[32 * i:32 * i + 32, :], VA[:, 4 * g + i, :], E[:, i, :], start=True, stop=False)
                for i in range(4):
                    last = mm(V0[32 * i:32 * i + 32, :], VT1[:, 4 * g + i, :], E[0:4 * TAIL, 4, :], start=False, stop=True)
                last.then_inc(tensor_value, 1)

            def proj(key):
                t, h = key[1:]
                pe.wait_ge(vector_outl, upto(vector_outl, ("outl", t, h), "l"))
                pe.wait_ge(scalar_score, upto(scalar_score, ("score", t, 5 * GROUPS - 1), "e"))
                if t == 0:
                    pe.wait_ge(vector_split, upto(vector_split, ("split", 3), "l"))
                for s in (2 * h, 2 * h + 1):
                    c = slice(P * s, P * s + P)
                    for g in range(GROUPS):
                        last = exact(S[:, h, D * (s % 2):D * (s % 2) + D], (AH[:, g, c], AL[:, g, c]),
                                     (WPh[:, g, :], WPl[:, g, :]), g == 0, g == GROUPS - 1)
                last.then_inc(tensor_proj, 1)

            parts = {"setup": setup, "ctx": context, "vec": vectors, "fold": fold, "bq": query_bias, "vw": slice_w, "tail": tail, "mod": mod, "w2t": w2_transposed, "w2": w2,
                     "cb": bias_out, "keyx": keyx, "key": pair_keys, "norm": norm, "att": att, "prob": prob,
                     "z": hidden, "p": second, "qx": qx, "query": query, "most": most, "row": row, "score": score,
                     "value": value, "proj": proj}
            for key in order("tensor"):
                if key[0] in parts:
                    parts[key[0]](key)


def kernel(**inputs):
    import numpy as np
    import concourse.bacc as bacc
    from concourse.bass_utils import run_bass_kernel_spmd

    nc = bacc.Bacc("TRN2", target_bir_lowering=False, num_devices=1)
    arrays, aps = {}, {}
    for name, value in inputs.items():
        arrays[name] = np.ascontiguousarray(value)
        aps[name] = nc.dram_tensor(name, arrays[name].shape, F32, kind="ExternalInput").ap()
    arrays["shape_constants"] = shape_constants(np)
    consts = nc.dram_tensor("shape_constants", (P, NCONST), F32, kind="ExternalInput").ap()
    out = nc.dram_tensor("out", (BATCH, SEQ, D), F32, kind="ExternalOutput").ap()
    build(nc, aps, out, consts)
    r = run_bass_kernel_spmd(nc, [arrays], core_ids=[0])
    return r.results[0]["out"]
```

```python
from contextlib import ExitStack

import concourse.bass as bass
from concourse import mybir

F32 = mybir.dt.float32
F32R = mybir.dt.float32r
ALU = mybir.AluOpType
ACT = mybir.ActivationFunctionType
AX = mybir.AxisListType

P = 128
NSPLIT = 3
BATCH, SEQ, D, CTX = 2, 1024, 256, 154
KC = D // P
TILE = 512
NSUB = TILE // P
TPB = SEQ // TILE
NT = BATCH * TPB
TAIL = CTX - P
EXPERTS, RH = 3, 512
ZCOLS = D + EXPERTS * RH
NZ = ZCOLS // P
GATES = D // P
PER = RH // P
QN = 448
NQ = ZCOLS // QN
HEADS, DH = 16, D // 16
PAIRS = HEADS // 2
GROUPS = HEADS // 4
STACK = 96
KROWS = STACK + 4
EPS = 1e-5
ERING = 6
RING = 2
SLOTS = 3

C_ID, C_HEAD, C_SPLIT, C_ROW, C_ONE = 0, 128, 130, 131, 135
C_PAIR = 136
C_FOLD = 138
NCONST = 170
N_ROWS = 8
N_ROUTER = 2
N_BROADCAST = 3
V_GAMMA, V_BETA, V_COND, V_B2, V_BSS, V_BQ, V_BK = 0, 2, 4, 8, 14, 22, 24
N_VROWS = 26
N_HIDDEN_BIAS = 7


def shape_constants(np):
    c = np.zeros((P, NCONST), np.float32)
    row = np.arange(P)
    c[:, C_ID:C_ID + P] = np.eye(P)
    c[:, C_HEAD] = row % 32 < DH
    c[:, C_HEAD + 1] = row % 32 >= DH
    c[:, C_SPLIT] = -1.0 * (row % 32 >= DH)
    for i in range(4):
        c[:, C_ROW + i] = (row >= TAIL * i) & (row < TAIL * (i + 1))
    c[:, C_ONE] = 1.0
    c[STACK:KROWS, C_PAIR] = (1, 0, 1, 0)
    c[STACK:KROWS, C_PAIR + 1] = (0, 1, 0, 1)
    c[:, C_FOLD:C_FOLD + 32] = row[:, None] % 32 == np.arange(32)[None, :]
    return c


STEPS = {
    "tensor": {
        "setup": ["wqT"],
        "ctx": ["ctxT", "kT", "vT"],
        "vec": ["v"],
        "fold": ["A", "VR", "RC"],
        "vw": ["m"],
        "tail": ["m"],
        "mod": ["mod"],
        "bq": ["bq"],
        "w2t": ["t0", "t1"],
        "w2": ["m0", "m1"],
        "cb": ["cb"],
        "keyx": ["t"],
        "key": ["k", "v", "vt"],
        "norm": ["t0", "t1"],
        "att": ["s"],
        "prob": ["p"],
        "logit": ["l"],
        "z": ["z"],
        "p": ["p"],
        "qx": ["t0", "t1"],
        "query": ["q0", "q1"],
        "most": ["s"],
        "row": ["m"],
        "score": ["s"],
        "value": ["v"],
        "proj": ["o"],
    },
    "scalar": {
        "setup": ["wqT"],
        "ctx": ["ctxT", "vT"],
        "fold": ["A"],
        "vw": ["h", "t"],
        "silu": ["tc"],
        "splitw": ["h"],
        "split": ["h"],
        "w2t": ["t0", "t1"],
        "w2": ["m0", "m1"],
        "keyx": ["x0", "x1"],
        "norm": ["n0", "n1"],
        "att": ["e"],
        "prob": ["p"],
        "low": ["n0", "n1"],
        "route": ["pm", "pd"],
        "logit": ["ex"],
        "z": ["t"],
        "h": ["h"],
        "gate": ["g"],
        "qx": ["x0", "x1"],
        "query": ["q0", "q1"],
        "row": ["h"],
        "score": ["e"],
        "value": ["v"],
        "out": ["h"],
    },
    "vector": {
        "setup": ["fill"],
        "splitw": ["l"],
        "ctx": ["kT"],
        "vec": ["v"],
        "fold": ["fill", "VR", "RC"],
        "vw": ["l"],
        "tail": ["th", "tl"],
        "silu": ["sc"],
        "mod": ["mod"],
        "bq": ["bq"],
        "w2": ["m0", "m1"],
        "cb": ["cb"],
        "keyn": ["var", "xh"],
        "keyx": ["rep"],
        "key": ["k", "kh", "kl", "v", "vt"],
        "keyt": ["kt"],
        "ln": ["var"],
        "norm": ["xh"],
        "att": ["t"],
        "prob": ["r"],
        "route": ["pl", "dl"],
        "logit": ["l", "s", "prob"],
        "z": ["s"],
        "evac": ["o"],
        "res": ["u", "x"],
        "qn": ["var"],
        "qx": ["xh"],
        "qlow": ["x0", "x1"],
        "query": ["q0", "q1"],
        "most": ["s"],
        "row": ["l"],
        "sums": ["r"],
        "out": ["o"],
        "outl": ["l"],
        "proj": ["o"],
    },
    "gpsimd": {
        "split": ["l"],
        "keyn": ["rstd"],
        "ln": ["rstd"],
        "low": ["n0", "n1"],
        "gate": ["g"],
        "h": ["l"],
        "qn": ["rstd"],
        "bias": ["x"],
        "sum": ["s"],
    },
}


DELAY = {
    "tensor": {"norm": 0, "prob": 1, "qx": 0, "keyx": 1},
    "scalar": {"norm": 2, "out": 3, "qx": 2, "keyx": 0},
    "vector": {"query": 0, "key": 0, "mod": 3, "bq": 7},
    "gpsimd": {},
    "sync": {},
}
PROB_AT, LOW_AT, ROUTE_AT, LOGIT_AT = (1, 2, 3, 4), 3, 6, 0
QX_AT, QLOW_AT, QUERY_AT, BIAS_AT, MOST_AT = 1, 2, 4, 6, 7
MOSTS, ROW_GAP, SCORES, VALUE_LAG = (5, 4), 4, (2, 2), 1
SUMS_LAG, OUTL_LAG, PROJ_LAG = (1, 3), (4, 4), (7, 10)
KEYN_AT, KEYX_AT, KEY_AT, KEYT_AT = 3, 5, 6, 14
SPLITW_AT, SPLITS_AT, SILU_AT, CB_AT, MOD_AT, BQ_AT, KEYS0_AT = 1, (9, 12, 16), 7, 9, 10, 16, 19
SECOND_AT, SECOND_CTX_AT, SECOND_KEYS_AT, SECOND_LAST_AT = 2, 4, 7, 0
RES_AT, KEYS1_LAG = 0, 9


def schedule():
    table = []

    def place(slot, *keys):
        while len(table) <= slot:
            table.append([])
        table[slot] += keys

    def block0(t, at):
        if t % TPB == 0:
            place(at, ("norm", t))
            at += 2
        place(at, ("att", t, 0), ("att", t, 1))
        place(at + 1, ("att", t, 2), ("att", t, 3))
        for s in range(NSUB):
            place(at + PROB_AT[s], ("prob", t, s))
        place(at + LOW_AT, ("low", t))
        if t % TPB:
            place(at + RES_AT, ("res", t - 1))
        place(at + ROUTE_AT, ("route", t))
        at += ROUTE_AT + 1
        for k in range(NZ + 2):
            if k < NZ:
                place(at, ("z", t, k))
            if k == LOGIT_AT:
                place(at, ("logit", t))
            if k == 6 and t + 1 < NT:
                place(at, ("ln", t + 1))
            if k == NZ and (t + 1) % TPB:
                place(at, ("norm", t + 1))
            if k == NZ and (t + 1) % TPB == 0 and t + 1 < NT:
                place(at, ("load", (t + 1) // TPB))
            if 0 <= k - 2:
                place(at + 1, ("p", t, k - 2))
                if k - 2 == GATES - 1:
                    place(at + 1, ("gate", t))
                elif k - 2 >= GATES and (k - 2 - GATES) % PER == PER - 1:
                    place(at + 1, ("evac", t, (k - 2 - GATES) // PER + 1))
            if k < NZ:
                place(at + 1, ("h", t, k))
            at += 2
        if (t + 1) % TPB == 0:
            place(at - 1, ("res", t))
        return at

    def block1(t, at):
        place(at, ("qn", t))
        place(at + QX_AT, ("qx", t))
        place(at + QLOW_AT, ("qlow", t))
        place(at + QUERY_AT, ("query", t))
        place(at + BIAS_AT, ("bias", t))
        at += MOST_AT
        u = 0
        while u < NSUB * PAIRS:
            n = MOSTS[at % 2]
            place(at, *[("most", t, i) for i in range(u, min(u + n, NSUB * PAIRS))])
            u += n
            at += 1
        place(at, ("row", t))
        at += ROW_GAP
        w, g = 0, 0
        while w < 5 * GROUPS:
            n = SCORES[at % 2]
            place(at, *[("score", t, i) for i in range(w, min(w + n, 5 * GROUPS))])
            w += n
            if w >= 5 * g + 5 and g < GROUPS:
                place(at + VALUE_LAG, ("value", t, g))
                if g:
                    place(at + VALUE_LAG, ("sum", t, g))
                g += 1
            at += 1
        at += VALUE_LAG - 1
        if t == NT - 1:
            place(at + SUMS_LAG[0], ("sums", t, 0), ("out", t, 0), ("sums", t, 1))
            place(at + SUMS_LAG[0], ("outl", t, 0), ("out", t, 1), ("outl", t, 1))
            place(at + PROJ_LAG[1], ("proj", t, 0), ("proj", t, 1))
            return at, at + PROJ_LAG[1]
        for h in range(2):
            place(at + SUMS_LAG[h], ("sums", t, h), ("out", t, h))
            place(at + OUTL_LAG[h], ("outl", t, h))
            place(at + PROJ_LAG[h], ("proj", t, h))
        return at, at + PROJ_LAG[1]

    def keys(b, at):
        for stage, lag in (("keyw", 0), ("keyn", KEYN_AT), ("keyx", KEYX_AT), ("key", KEY_AT), ("keyt", KEYT_AT)):
            place(at + lag, (stage, b))

    def context(b, at):
        place(at, ("ctx", b), *([] if b else [("vec", 0)]), ("fold", b))
        for q in range(NQ):
            place(at + 1 + q, ("vw", b, q))
        place(at + 1 + NQ, ("tail", b))
        return at + 2 + NQ

    place(0, ("setup", 0), ("load", 0))
    at0 = context(0, 1)
    place(3, ("ln", 0))
    for g in range(EXPERTS):
        place(at0 + g, ("w2t", g))
        place(at0 + g + 1, ("w2", g))
    place(at0 + SPLITW_AT, ("splitw", 0))
    for i in range(NSPLIT):
        place(at0 + SPLITS_AT[i], ("split", i))
    for stage, lag in (("silu", SILU_AT), ("cb", CB_AT), ("mod", MOD_AT), ("bq", BQ_AT)):
        place(at0 + lag, (stage, 0))
    keys(0, at0 + KEYS0_AT)
    at1 = block0(0, at0)
    middle = block0(1, at1)
    block1(0, at1 + SECOND_AT)
    at2 = context(1, middle)
    at3 = block0(2, at2)
    values, _ = block1(1, middle + SECOND_CTX_AT)
    keys(1, values + KEYS1_LAG)
    end = block0(3, at3)
    values, _ = block1(2, max(at3 + SECOND_AT, values + KEYS1_LAG + SECOND_KEYS_AT))
    block1(3, max(end, values + PROJ_LAG[1]) + SECOND_LAST_AT)
    return table


def order(engine):
    placed = []
    for slot, stages in enumerate(schedule()):
        for key in stages:
            placed.append((slot + DELAY[engine].get(key[0], 0), key))
    placed.sort(key=lambda item: item[0])
    return [key for _, key in placed]


INSTANCE = {
    "vw": lambda b, q: NQ * b + q,
    "att": lambda t, s: NSUB * t + s, "prob": lambda t, s: NSUB * t + s, "most": lambda t, u: NSUB * PAIRS * t + u,
    "z": lambda t, k: NZ * t + k, "h": lambda t, k: NZ * t + k, "p": lambda t, k: NZ * t + k,
    "evac": lambda t, j: EXPERTS * t + j - 1, "sum": lambda t, a: (GROUPS - 1) * t + a - 1, 
    "sums": lambda t, h: 2 * t + h, "out": lambda t, h: 2 * t + h, "outl": lambda t, h: 2 * t + h,
    "proj": lambda t, h: 2 * t + h,
    "score": lambda t, w: 5 * GROUPS * t + w, "value": lambda t, a: GROUPS * t + a,
}


def build(nc, a, out, consts):
    with ExitStack() as ctx:
        def sem(name):
            return ctx.enter_context(nc.semaphore(name))

        def psum(name, shape):
            return ctx.enter_context(nc.psum_tensor(name, shape, F32))

        Z = psum("hidden_banks", [P, 2, 512])
        O = psum("token_banks", [P, NSUB, D])
        OFF = O[:, :, :].rearrange("p (k s) d -> p k (s d)", k=2)
        M0 = psum("misc_bank", [P, 512])
        S = psum("score_banks", [P, 2, 512])
        V0 = psum("value_bank", [P, 512])

        at = [(nc.sbuf_base + 63) // 64 * 64]

        def put(name, shape, dt=F32, offset=None):
            size = 4
            for n in shape[1:]:
                size *= n
            o = at[0] if offset is None else offset
            if offset is None:
                at[0] += (size + 31) // 32 * 32
            return nc.alloc_sbuf_tensor_at(name, shape, dt, offset=o)

        def run(start, parts):
            made = []
            for name, shape, dt in parts:
                made.append(put(name, shape, dt, offset=start))
                size = 4
                for n in shape[1:]:
                    size *= n
                start += (size + 31) // 32 * 32
            return made + [start]

        CN = put("constants", [P, NCONST])
        ident = CN[:, C_ID:C_ID + P]
        WNh = put("hidden_w_high", [P, KC, ZCOLS], F32R)
        WNl = put("hidden_w_low", [P, KC, ZCOLS], F32R)
        VWh = put("context_w_high", [P, ZCOLS], F32R)
        VWl = put("context_w_low", [P, ZCOLS], F32R)
        VWD = put("context_w_tail", [STACK, ZCOLS], F32R)
        W2h = put("expert_out_high", [P, EXPERTS * PER, D], F32R)
        W2l = put("expert_out_low", [P, EXPERTS * PER, D], F32R)
        GWh = put("gate_out_high", [P, KC, D], F32R)
        GWl = put("gate_out_low", [P, KC, D], F32R)
        WQh = put("query_w_high", [P, KC, D], F32R)
        WQl = put("query_w_low", [P, KC, D], F32R)
        WPh = put("proj_w_high", [P, GROUPS, D], F32R)
        WPl = put("proj_w_low", [P, GROUPS, D], F32R)
        A = put("score_w", [P, KC, CTX + EXPERTS])
        VRC = put("router_context", [P, 2, EXPERTS])
        RC = put("router_const", [P, EXPERTS])
        RB = put("router_bias", [P, EXPERTS])
        keys_at = at[0]
        KS = put("pair_keys", [KROWS, PAIRS, 2, CTX], F32R)
        KT = put("pair_keys_tail", [KROWS, PAIRS, 4, TAIL], F32R)
        VA = put("head_values", [P, HEADS, 2 * DH])
        VT1 = put("head_values_tail", [4 * TAIL, HEADS, 2 * DH])
        CB = put("second_bias", [64, 1 + EXPERTS, D], F32R)
        BROW = put("bias_rows", [P, P], F32R)
        BP = put("proj_bias_row", [P, D])
        VC = put("vectors", [P, N_VROWS])
        GAM, BET, BQ0, BK = (VC[:, i:i + KC] for i in (V_GAMMA, V_BETA, V_BQ, V_BK))
        CO = VC[:, V_COND:V_COND + BATCH * KC].rearrange("p (b k) -> p k b", k=KC)
        B2T = VC[:, V_B2:V_B2 + EXPERTS * KC].rearrange("p (e k) -> p k e", k=KC)
        BSS = VC[:, V_BSS:V_BSS + 8]
        COT = put("condition_silu", [P, KC, BATCH])
        MOD = put("modulation", [P, 8, BATCH])
        BQ = put("query_bias", [P, KC, BATCH])
        RW = put("router_w", [P, 3 * KC, EXPERTS])
        HALF = put("minus_half", [P, NSUB])
        ST0 = put("stats0", [P, NSUB, 6])
        MV0 = put("mean_var0", [P, NSUB, 2])
        RS0 = put("rstd0", [P, NSUB])
        ST1 = put("stats1", [P, NSUB, 6])
        MV1 = put("mean_var1", [P, NSUB, 2])
        RS1 = put("rstd1", [P, NSUB])
        WQT = put("score_wq_T", [P, KC, D])
        TC = put("condition_tanh", [P, KC, BATCH])
        ST2 = put("stats2", [P, 2, 6])
        MV2 = put("mean_var2", [P, 2, 2])
        RS2 = put("rstd2", [P, 2])
        SM0 = put("softmax_small", [P, NSUB, 4])
        LG = put("router_logits", [P, NSUB, EXPERTS])
        PR = put("router_probs", [P, NSUB, EXPERTS])
        RT = put("router_small", [P, NSUB, 2])
        MX = put("head_maxima", [P, NSUB, 2, PAIRS])
        tokens_at = at[0]
        X = put("tokens", [P, SLOTS, NSUB, D])
        WQR, WQ1R, GWR, OB, GB, VROWS, WPR, _ = run(keys_at, [
            ("score_wq_raw", [P, KC, D], F32), ("query_w_raw", [P, KC, D], F32),
            ("gate_out_raw", [P, KC, D], F32), ("out_bias_row", [P, D], F32), ("gate_b2_row", [P, D], F32),
            ("vector_rows", [P, P], F32), ("proj_w_raw", [P, GROUPS, D], F32)])
        WSS, _ = run(tokens_at + 4 * NSUB * D, [("modulation_w", [P, 2, KC, 2 * D], F32)])
        R0 = at[0]
        SH, SL, NXh, NXl, PTh, PTl, PTD, TB, ACC, G, end0 = run(R0, [
            ("hidden_high", [P, RING, TILE], F32R), ("hidden_low", [P, RING, TILE], F32R),
            ("normed_high", [P, KC, TILE], F32R), ("normed_low", [P, KC, TILE], F32R),
            ("probs_T_high", [P, TILE], F32R), ("probs_T_low", [P, TILE], F32R),
            ("probs_T_tail", [P, TILE], F32R), ("hidden", [P, 2, TILE], F32),
            ("expert_sum", [P, NSUB, D], F32), ("gate", [P, NSUB, D], F32)])
        PB, EB, _ = run(R0, [("probs", [P, NSUB, D], F32), ("exps", [P, NSUB, CTX], F32)])
        XH0, _ = run(R0 + 4 * 2 * RING * TILE, [("x_hat0", [P, NSUB, D], F32)])
        NXf, _ = run(R0 + 4 * (2 * RING + 2 * KC) * TILE, [("normed", [P, KC, TILE], F32)])
        WS0, _ = run(R0, [("w_slices_even", [P, 2 * KC, QN], F32)])
        CX, CXT, KTT, VTT, AN, WKR, WVR, WS1, TQ, used = run(R0 + 4 * 2 * RING * TILE, [
            ("context", [P, 2, D], F32),
            ("context_T", [P, KC, 160], F32), ("keys_T", [P, KC, 160], F32),
            ("values_T", [P, KC, 160], F32), ("anchor_cols", [P, KC, 32], F32),
            ("wk_raw", [P, KC, D], F32), ("wv_raw", [P, KC, D], F32),
            ("w_slices_odd", [P, 2 * KC, QN], F32), ("tail_quarters", [P, NQ, QN], F32)])
        TH, TL, B1T, end1 = run(used, [
            ("tail_high", [P, QN], F32R), ("tail_low", [P, QN], F32R), ("hidden_bias", [P, QN], F32)])
        TF, _ = run(used - 4 * NQ * QN, [("tail_full", [P, QN], F32)])
        assert used >= end0 - 2 * 4 * NSUB * D
        at[0] = max(end0, end1)
        R1 = at[0]
        QS, XH1, XQh, XQl, QH, QL, ROWS, end2 = run(R1, [
            ("query_stack", [KROWS, PAIRS, TILE], F32R),
            ("x_hat1", [P, NSUB, D], F32), ("query_in_high", [P, KC, TILE], F32R),
            ("query_in_low", [P, KC, TILE], F32R),
            ("queries_high", [P, KC, TILE], F32R), ("queries_low", [P, KC, TILE], F32R),
            ("row_space", [P, 2, TILE], F32)])
        NMH, NML, _ = run(end2 - 2 * 4 * TILE, [
            ("max_high", [HEADS, TILE], F32R), ("max_low", [HEADS, TILE], F32R)])
        SD, _ = run(R1 + 4 * PAIRS * TILE, [("sums_spread", [P, GROUPS, D], F32)])
        E, RAW, SUM, _ = run(R1 + 4 * PAIRS * TILE, [
            ("exp_ring", [P, ERING, TILE], F32),
            ("outs_and_sums", [P, GROUPS, TILE], F32), ("sums", [P, TILE], F32)])
        AH, AL, _ = run(R1, [("outs_high", [P, GROUPS, TILE], F32R), ("outs_low", [P, GROUPS, TILE], F32R)])
        WNR, W2R, W2T, OW, end3 = run(R1, [
            ("hidden_w_raw", [P, KC, ZCOLS], F32), ("w2_raw", [P, EXPERTS * PER, D], F32),
            ("w2_T", [P, KC, EXPERTS * RH], F32), ("out_w", [P, KC, D], F32)])
        CBF, CBH, _ = run(R1, [("second_bias_full", [64, 1 + EXPERTS, D], F32), ("second_bias_high", [64, 1 + EXPERTS, D], F32R)])
        KX, KXR, K1, KMH, KML, VTM, WKV, CX1, XH2, BV, end4 = run(R1, [
            ("ctx_mod_T", [P, KC, 160], F32), ("ctx_tail_rep", [P, KC, 4 * TAIL], F32),
            ("keys1", [P, KC, 160], F32), ("keys1_high", [P, KC, 2, CTX], F32R),
            ("keys1_low", [P, KC, 2, CTX], F32R), ("tail_values", [4 * TAIL, D], F32),
            ("kv_w", [P, KC, 2 * D], F32), ("context1", [P, 2, D], F32), ("x_hat2", [P, 2, D], F32),
            ("value_bias_row", [P, D], F32)])
        at[0] = max(end2, end3, end4)

        steps_of = {}

        def step_sem(engine, stage):
            made = sem(f"{engine}_{stage}")
            steps_of[id(made)] = STEPS[engine][stage]
            return made

        (tensor_setup, tensor_ctx, tensor_vec, tensor_fold, tensor_vw, tensor_tail,
         tensor_mod, tensor_bq, tensor_w2t, tensor_w2, tensor_cb, tensor_keyx,
         tensor_key, tensor_norm, tensor_att, tensor_prob, tensor_logit, tensor_z,
         tensor_p, tensor_qx, tensor_query, tensor_most, tensor_row, tensor_score,
         tensor_value, tensor_proj) = (
            step_sem("tensor", s) for s in STEPS["tensor"])
        (scalar_setup, scalar_ctx, scalar_fold, scalar_vw, scalar_silu, scalar_splitw,
         scalar_split, scalar_w2t, scalar_w2, scalar_keyx, scalar_norm, scalar_att,
         scalar_prob, scalar_low, scalar_route, scalar_logit, scalar_z, scalar_h,
         scalar_gate, scalar_qx, scalar_query, scalar_row, scalar_score, scalar_value,
         scalar_out) = (
            step_sem("scalar", s) for s in STEPS["scalar"])
        (vector_setup, vector_splitw, vector_ctx, vector_vec, vector_fold, vector_vw,
         vector_tail, vector_silu, vector_mod, vector_bq, vector_w2, vector_cb,
         vector_keyn, vector_keyx, vector_key, vector_keyt, vector_ln, vector_norm,
         vector_att, vector_prob, vector_route, vector_logit, vector_z, vector_evac,
         vector_res, vector_qn, vector_qx, vector_qlow, vector_query, vector_most,
         vector_row, vector_sums, vector_out, vector_outl, vector_proj) = (
            step_sem("vector", s) for s in STEPS["vector"])
        (gpsimd_split, gpsimd_keyn, gpsimd_ln, gpsimd_low, gpsimd_gate, gpsimd_h,
         gpsimd_qn, gpsimd_bias, gpsimd_sum) = (
            step_sem("gpsimd", s) for s in STEPS["gpsimd"])
        vector_results = sem("vector_results")
        consts_loaded = sem("consts_loaded")
        rows_loaded = sem("rows_loaded")
        router_loaded = sem("router_loaded")
        broadcasts_loaded = sem("broadcasts_loaded")
        score_w_loaded = sem("score_w_loaded")
        modulation_w_loaded = sem("modulation_w_loaded")
        small_w_loaded = sem("small_w_loaded")
        proj_w_loaded = sem("proj_w_loaded")
        hidden_w_loaded = sem("hidden_w_loaded")
        w2_loaded = sem("w2_loaded")
        x_loaded = [sem(f"x_slot{i}_loaded") for i in range(SLOTS)]
        context_loaded = sem("context_loaded")
        kv_w_loaded = sem("kv_w_loaded")
        hidden_bias_loaded = sem("hidden_bias_loaded")
        slice_even_loaded = sem("slice_even_loaded")
        slice_odd_loaded = sem("slice_odd_loaded")
        tails_placed = sem("tails_placed")
        keys_placed = sem("keys_placed")
        pair_placed = [sem(f"query_pair{c}_placed") for c in range(PAIRS)]
        maxima_placed = sem("maxima_placed")
        stored = sem("stored")

        def instance(key):
            return key[1] if len(key) == 2 else INSTANCE[key[0]](*key[1:])

        def upto(semaphore, key, step):
            names = steps_of[id(semaphore)]
            return instance(key) * len(names) + names.index(step) + 1

        class Count:
            n = 0

            def one(self):
                self.n += 1
                return 1

        for e in STEPS:
            seen = {}
            for key in order(e):
                if key[0] in STEPS[e]:
                    assert instance(key) == seen.get(key[0], 0), (e, key)
                    seen[key[0]] = seen.get(key[0], 0) + 1

        def hidden_columns(lo, hi, rows):
            out_ = []
            if lo < D:
                out_.append((0, min(hi, D) - lo, a["L0_xcond_gate_w1"][rows, lo:min(hi, D)]))
            for e in range(EXPERTS):
                c0 = D + e * RH
                l, h = max(lo, c0), min(hi, c0 + RH)
                if l < h:
                    out_.append((l - lo, h - lo, a["L0_xcond_e_w1"][e, rows, l - c0:h - c0]))
            return out_

        def slices_loaded(b, q):
            each = [2 * len(hidden_columns(i * QN, (i + 1) * QN, slice(0, D))) for i in range(NQ)]
            return b * sum(each[q % 2::2]) + sum(each[q % 2:q + 1:2])

        def hidden_bias(lo, hi):
            out_ = []
            if lo < D:
                out_.append((0, min(hi, D) - lo, a["L0_xcond_gate_b1"][lo:min(hi, D)]))
            for e in range(EXPERTS):
                c0 = D + e * RH
                l, h = max(lo, c0), min(hi, c0 + RH)
                if l < h:
                    out_.append((l - lo, h - lo, a["L0_xcond_e_b1"][e, l - c0:h - c0]))
            return out_

        def feature_rows(w):
            return w.rearrange("(k p) n -> p k n", p=P)

        def columns(v):
            return v.rearrange("(k p) -> p k", p=P)

        def tokens_of(dram, t):
            b, i = t // TPB, t % TPB
            return dram[b, i * TILE:(i + 1) * TILE, :].rearrange("(s p) d -> p s d", p=P)

        def raw(ap):
            return ap.bitcast(F32)

        block = ctx.enter_context(nc.Block())

        @block.sync
        def _(sp):
            def setup(key):
                sp.dma_start(CN[:, :], consts).then_inc(consts_loaded, 16)
                sp.dma_start(WQR[:, :, :], feature_rows(a["L0_xcond_Wq"])).then_inc(score_w_loaded, 16)

            def load(key):
                b = key[1]
                if b:
                    sp.wait_ge(tensor_z, upto(tensor_z, ("z", TPB * b - 1, NZ - 1), "z"))
                sp.dma_start(CX[:, 0, :], a["ctx_1024"][b, 0:P, :]).then_inc(context_loaded, 16)
                sp.dma_start(CX[0:TAIL, 1, :], a["ctx_1024"][b, P:CTX, :]).then_inc(context_loaded, 16)
                if b:
                    sp.dma_start(WKR[:, :, :], feature_rows(a["L0_xcond_Wk"])).then_inc(context_loaded, 16)
                    sp.dma_start(WVR[:, :, :], feature_rows(a["L0_xcond_Wv"])).then_inc(context_loaded, 16)

            def context(key):
                b = key[1]
                if b:
                    sp.wait_ge(tensor_p, upto(tensor_p, ("p", TPB * b - 1, NZ - 1), "p"))
                    sp.wait_ge(gpsimd_h, upto(gpsimd_h, ("h", TPB * b - 1, NZ - 1), "l"))
                for q in range(NQ):
                    if q >= 2:
                        sp.wait_ge(tensor_vw, upto(tensor_vw, ("vw", b, q - 2), "m"))
                    for part in range(2):
                        rows = slice((1 + part) * D, (2 + part) * D)
                        for lo, hi, src in hidden_columns(q * QN, (q + 1) * QN, rows):
                            sp.dma_start((WS0, WS1)[q % 2][:, KC * part:KC * part + KC, lo:hi],
                                         feature_rows(src)).then_inc((slice_even_loaded, slice_odd_loaded)[q % 2], 16)
                    if b == 0 and q == 1:
                        sp.dma_start(X[:, 0, :, :], tokens_of(a["x"], 0)).then_inc(x_loaded[0], 16)
                    if q == 1:
                        sp.wait_ge(vector_fold, upto(vector_fold, ("fold", b), "fill"))
                        for r in range(NQ):
                            for lo, hi, src in hidden_bias(r * QN, (r + 1) * QN):
                                sp.dma_start(B1T[32 * r + TAIL:32 * r + TAIL + 1, lo:hi],
                                             src.partition_broadcast(1)).then_inc(hidden_bias_loaded, 16)
                if b == 0:
                    sp.dma_start(WNR[:, :, 0:D], feature_rows(a["L0_xcond_gate_w1"][0:D, :])).then_inc(hidden_w_loaded, 16)
                    for e in range(EXPERTS):
                        sp.dma_start(WNR[:, :, D + e * RH:D + (e + 1) * RH],
                                      feature_rows(a["L0_xcond_e_w1"][e, 0:D, :])).then_inc(hidden_w_loaded, 16)
                    sp.dma_start(GWR[:, :, :], feature_rows(a["L0_xcond_gate_w2"])).then_inc(small_w_loaded, 16)
                    sp.dma_start(WQ1R[:, :, :], feature_rows(a["L1_xcond_Wq"])).then_inc(small_w_loaded, 16)
                    for dst, src in ((GB, "L0_xcond_gate_b2"), (BP, "L1_xcond_bp"), (OB, "L0_xcond_out_b")):
                        sp.dma_start(dst[:, :], a[src].partition_broadcast(P)).then_inc(broadcasts_loaded, 16)
                    sp.dma_start(WSS[:, 0, :, :], feature_rows(a["L1_xcond_Wss_q"])).then_inc(modulation_w_loaded, 16)
                    sp.dma_start(WSS[:, 1, :, :], feature_rows(a["L1_xcond_Wss_kv"])).then_inc(modulation_w_loaded, 16)

            def tail(key):
                sp.wait_ge(vector_tail, upto(vector_tail, key, "tl"))
                for q in range(NQ):
                    for j, part in enumerate((TH, TH, TL)):
                        sp.dma_start(raw(VWD[32 * j:32 * j + 32, q * QN:(q + 1) * QN]),
                                     raw(part[32 * q:32 * q + 32, :])).then_inc(tails_placed, 16)

            def keyw(key):
                b = key[1]
                if b:
                    sp.wait_ge(tensor_proj, upto(tensor_proj, ("proj", TPB * b - 1, 1), "o"))
                    sp.wait_ge(vector_proj, upto(vector_proj, ("proj", TPB * b - 1, 1), "o"))
                else:
                    sp.wait_ge(tensor_cb, upto(tensor_cb, ("cb", 0), "cb"))
                    sp.wait_ge(vector_cb, upto(vector_cb, ("cb", 0), "cb"))
                    sp.wait_ge(scalar_split, upto(scalar_split, ("split", NSPLIT - 1), "h"))
                    sp.wait_ge(gpsimd_split, upto(gpsimd_split, ("split", NSPLIT - 1), "l"))
                sp.dma_start(CX1[:, 0, :], a["ctx_1024"][b, 0:P, :]).then_inc(kv_w_loaded, 16)
                sp.dma_start(CX1[0:TAIL, 1, :], a["ctx_1024"][b, P:CTX, :]).then_inc(kv_w_loaded, 16)
                sp.dma_start(WKV[:, :, :], feature_rows(a["L1_xcond_Wkv"])).then_inc(kv_w_loaded, 16)
                sp.dma_start(BV[:, :], a["L1_xcond_bkv"][D:2 * D].partition_broadcast(P)).then_inc(kv_w_loaded, 16)
                if b == 0:
                    sp.wait_ge(tensor_mod, upto(tensor_mod, ("mod", 0), "mod"))
                    for t in range(1, SLOTS):
                        sp.dma_start(X[:, t, :, :], tokens_of(a["x"], t)).then_inc(x_loaded[t], 16)

            def pair_keys(key):
                sp.wait_ge(vector_key, upto(vector_key, key, "kl"))
                for c in range(PAIRS):
                    f, r = c // 4, 32 * (c % 4)
                    for j, part in enumerate((KMH, KMH, KML)):
                        sp.dma_start(raw(KS[32 * j:32 * j + 32, c, :, :]),
                                     raw(part[r:r + 32, f, :, :])).then_inc(keys_placed, 16)

            def query(key):
                t = key[1]
                if t:
                    sp.wait_ge(tensor_proj, upto(tensor_proj, ("proj", t - 1, 1), "o"))
                for f in range(KC):
                    sp.wait_ge(scalar_query, upto(scalar_query, key, f"q{f}"))
                    sp.wait_ge(vector_query, upto(vector_query, key, f"q{f}"))
                    for c in range(4 * f, 4 * f + 4):
                        r = 32 * (c % 4)
                        for j, part in enumerate((QH, QL, QH)):
                            sp.dma_start(raw(QS[32 * j:32 * j + 32, c, :]),
                                         raw(part[r:r + 32, f, :])).then_inc(pair_placed[c], 16)

            def row(key):
                sp.wait_ge(scalar_row, upto(scalar_row, key, "h"))
                sp.wait_ge(vector_row, upto(vector_row, key, "l"))
                for j in range(2):
                    for i, part in enumerate((NMH, NML)):
                        dst = STACK + 2 * i + j
                        sp.dma_start(raw(QS[dst:dst + 1, :, :]),
                                     raw(part[PAIRS * j:PAIRS * j + PAIRS, :])).then_inc(maxima_placed, 16)

            def proj(key):
                t, h = key[1:]
                sp.wait_ge(vector_proj, upto(vector_proj, key, "o"))
                sp.dma_start(tokens_of(out, t)[:, 2 * h:2 * h + 2, :],
                             X[:, t % SLOTS, 2 * h:2 * h + 2, :]).then_inc(stored, 16)
                if h:
                    sp.wait_ge(stored, 32 * (t + 1))
                    if t + SLOTS < NT:
                        sp.dma_start(X[:, t % SLOTS, :, :], tokens_of(a["x"], t + SLOTS)).then_inc(x_loaded[t % SLOTS], 16)

            parts = {"setup": setup, "load": load, "ctx": context, "tail": tail, "keyw": keyw, "key": pair_keys, "query": query, "row": row, "proj": proj}
            for key in order("sync"):
                if key[0] in parts:
                    parts[key[0]](key)

        @block.scalar
        def _(act):
            def setup(key):
                act.dma_start(WKR[:, :, :], feature_rows(a["L0_xcond_Wk"])).then_inc(context_loaded, 16)
                act.dma_start(WVR[:, :, :], feature_rows(a["L0_xcond_Wv"])).then_inc(context_loaded, 16)
                act.dma_start(RW[:, :, :], feature_rows(a["L0_xcond_router_W"]),
                              allow_slow_non_contiguous=True).then_inc(router_loaded, 16)
                act.dma_start(RB[:, :], a["L0_xcond_router_b"].partition_broadcast(P)).then_inc(router_loaded, 16)
                act.wait_ge(tensor_setup, upto(tensor_setup, key, "wqT"))
                nc.scalar.copy(WQT[:, :, :], V0[:, :].rearrange("p (k n) -> p k n", k=KC)).then_inc(scalar_setup, 1)

            def silu(key):
                act.wait_ge(vector_vec, upto(vector_vec, ("vec", 0), "v"))
                nc.scalar.activation(TC[:, :, :], CO[:, :, :], ACT.Tanh, scale=0.5).then_inc(scalar_silu, 1)

            def split_hidden(key):
                act.wait_ge(hidden_w_loaded, 16 * (1 + EXPERTS))
                nc.scalar.copy(WNh[:, :, :], WNR[:, :, :]).then_inc(scalar_splitw, 1)

            def split(key):
                high, full, loaded, count = ((GWh, GWR, small_w_loaded, 2),
                                             (WQh, WQ1R, small_w_loaded, 2), (WPh, WPR, proj_w_loaded, 4))[key[1]]
                act.wait_ge(loaded, 16 * count)
                nc.scalar.copy(high[:, :, :], full[:, :, :]).then_inc(scalar_split, 1)

            def context(key):
                b = key[1]
                act.wait_ge(tensor_ctx, upto(tensor_ctx, key, "ctxT"))
                nc.scalar.copy(CXT[:, :, 0:CTX], M0[:, 0:320].rearrange("p (k n) -> p k n", k=KC)[:, :, 0:CTX]).then_inc(scalar_ctx, 1)
                act.wait_ge(tensor_ctx, upto(tensor_ctx, key, "vT"))
                nc.scalar.copy(VTT[:, :, 0:CTX], Z[:, 1, 0:320].rearrange("p (k n) -> p k n", k=KC)[:, :, 0:CTX]).then_inc(scalar_ctx, 1)

            def fold(key):
                act.wait_ge(tensor_fold, upto(tensor_fold, key, "A"))
                nc.scalar.mul(A[:, :, 0:CTX], OFF[:, 0, 0:320].rearrange("p (k n) -> p k n", k=KC)[:, :, 0:CTX],
                                     float(D) ** -0.5).then_inc(scalar_fold, 1)

            def slice_w(key):
                b, q = key[1:]
                if b and q == 0:
                    act.wait_ge(vector_res, upto(vector_res, ("res", TPB * b - 1), "x"))
                act.wait_ge(tensor_vw, upto(tensor_vw, key, "m"))
                nc.scalar.copy(VWh[:, q * QN:(q + 1) * QN], Z[:, q % 2, 0:QN]).then_inc(scalar_vw, 1)
                nc.scalar.copy(TQ[:, q, :], (M0[:, 0:QN], OFF[:, 1, 0:QN])[q % 2]).then_inc(scalar_vw, 1)

            def w2_transposed(key):
                g = key[1]
                for k in range(KC):
                    act.wait_ge(tensor_w2t, upto(tensor_w2t, key, f"t{k}"))
                    nc.scalar.copy(W2T[:, k, PER * P * g:PER * P * (g + 1)], S[:, k, :]).then_inc(scalar_w2t, 1)

            def w2(key):
                g = key[1]
                for i in range(2):
                    act.wait_ge(tensor_w2, upto(tensor_w2, key, f"m{i}"))
                    j = 2 * g + i
                    nc.scalar.mul(W2h[:, 2 * j:2 * j + 2, :], (V0[:, :], M0[:, :])[i].rearrange("p (k n) -> p k n", k=2),
                                         0.5).then_inc(scalar_w2, 1)

            def keyx(key):
                b = key[1]
                act.wait_ge(tensor_keyx, upto(tensor_keyx, key, "t"))
                for m in range(KC):
                    nc.scalar.activation(KX[:, m, 0:CTX], V0[:, 160 * m:160 * m + CTX], ACT.Identity,
                                                scale=MOD[:, 4 + m, b:b + 1], bias=MOD[:, 6 + m, b:b + 1]).then_inc(scalar_keyx, 1)

            def norm(key):
                t = key[1]
                for m in range(KC):
                    act.wait_ge(tensor_norm, upto(tensor_norm, key, f"t{m}"))
                    nc.scalar.activation(NXf[:, m, :], Z[:, m, :], ACT.Identity, scale=GAM[:, m:m + 1],
                                                bias=BET[:, m:m + 1]).then_inc(scalar_norm, 1)

            def low(key):
                act.wait_ge(tensor_norm, upto(tensor_norm, ("norm", key[1]), "t1"))
                act.wait_ge(scalar_norm, upto(scalar_norm, ("norm", key[1]), "n1"))
                for m in range(KC):
                    nc.scalar.copy(NXh[:, m, :], NXf[:, m, :]).then_inc(scalar_low, 1)

            def att(key):
                t, s = key[1:]
                act.wait_ge(vector_att, upto(vector_att, key, "t"))
                nc.scalar.activation(EB[:, s, :], OFF[:, s % 2, 0:CTX], ACT.Exp,
                                            bias=SM0[:, s, 0:1], accum_out=SM0[:, s, 1:2]).then_inc(scalar_att, 1)

            def prob(key):
                t, s = key[1:]
                act.wait_ge(vector_prob, upto(vector_prob, key, "r"))
                nc.scalar.mul(PB[:, s, 0:P], EB[:, s, 0:P], SM0[:, s, 2:3])
                nc.scalar.mul(PB[:, s, P:P + 3 * 32].rearrange("p (j n) -> p j n", j=3)[:, :, 0:TAIL],
                              EB[:, s, P:CTX].unsqueeze(1).to_broadcast([P, 3, TAIL]), SM0[:, s, 2:3]).then_inc(scalar_prob, 1)

            def route(key):
                t = key[1]
                act.wait_ge(tensor_prob, upto(tensor_prob, ("prob", t, NSUB - 1), "p"))
                act.wait_ge(gpsimd_low, upto(gpsimd_low, ("low", t), "n1"))
                nc.scalar.copy(PTh[:, :], Z[:, 0, :]).then_inc(scalar_route, 1)
                nc.scalar.copy(PTD[0:STACK, :], Z[0:STACK, 1, :]).then_inc(scalar_route, 1)

            def logit(key):
                act.wait_ge(vector_logit, upto(vector_logit, key, "s"))
                nc.scalar.activation(PR[:, :, :], LG[:, :, :], ACT.Exp).then_inc(scalar_logit, 1)

            def hidden(key):
                t, k = key[1:]
                g = NZ * t + k
                act.wait_ge(tensor_z, upto(tensor_z, key, "z"))
                if g >= 2:
                    act.wait_ge(gpsimd_h, upto(gpsimd_h, ("h", (g - 2) // NZ, (g - 2) % NZ), "l"))
                nc.scalar.activation(TB[:, k % 2, :], Z[:, k % 2, :], ACT.Tanh, scale=0.5).then_inc(scalar_z, 1)

            def high(key):
                t, k = key[1:]
                g = NZ * t + k
                act.wait_ge(vector_z, upto(vector_z, ("z", t, k), "s"))
                if g >= RING:
                    act.wait_ge(tensor_p, upto(tensor_p, ("p", (g - RING) // NZ, (g - RING) % NZ), "p"))
                nc.scalar.copy(SH[:, k % RING, :], TB[:, k % 2, :]).then_inc(scalar_h, 1)

            def gate(key):
                t = key[1]
                act.wait_ge(tensor_p, upto(tensor_p, ("p", t, GATES - 1), "p"))
                if t % TPB == 0:
                    act.wait_ge(tails_placed, 16 * 3 * NQ * (t // TPB + 1))
                if t:
                    act.wait_ge(vector_res, upto(vector_res, ("res", t - 1), "x"))
                nc.scalar.activation(G[:, :, :], O[:, :, :], ACT.Tanh, scale=0.25).then_inc(scalar_gate, 1)

            def qx(key):
                t = key[1]
                b = t // TPB
                for m in range(KC):
                    act.wait_ge(tensor_qx, upto(tensor_qx, key, f"t{m}"))
                    nc.scalar.mul(XQh[:, m, :], S[:, m, :], MOD[:, m, b:b + 1]).then_inc(scalar_qx, 1)

            def query(key):
                t = key[1]
                b = t // TPB
                for f in range(KC):
                    act.wait_ge(tensor_query, upto(tensor_query, key, f"q{f}"))
                    if t:
                        act.wait_ge(tensor_proj, upto(tensor_proj, ("proj", t - 1, 1), "o"))
                    nc.scalar.activation(QH[:, f, :], (V0[:, :], S[:, 0, :])[f], ACT.Identity,
                                                bias=BQ[:, f, b:b + 1]).then_inc(scalar_query, 1)

            def row(key):
                t = key[1]
                act.wait_ge(tensor_row, upto(tensor_row, key, "m"))
                if t:
                    act.wait_ge(tensor_proj, upto(tensor_proj, ("proj", t - 1, 1), "o"))
                nc.scalar.mul(NMH[:, :], V0[0:HEADS, :], -1.0).then_inc(scalar_row, 1)

            def score(key):
                t, w = key[1:]
                g, i = divmod(w, 5)
                if w >= ERING:
                    act.wait_ge(tensor_value, upto(tensor_value, ("value", t, (w - ERING) // 5), "v"))
                act.wait_ge(tensor_score, upto(tensor_score, key, "s"))
                rows = P if i < 4 else 4 * TAIL
                nc.scalar.activation(E[0:rows, w % ERING, :], (S[0:rows, 0, :], S[0:rows, 1, :], M0[0:rows, :])[w % 3], ACT.Exp).then_inc(scalar_score, 1)

            def value(key):
                t, g = key[1:]
                act.wait_ge(tensor_value, upto(tensor_value, key, "v"))
                if g == 0:
                    act.wait_ge(maxima_placed, 16 * 4 * (t + 1))
                nc.scalar.copy(RAW[:, g, :], V0[:, :]).then_inc(scalar_value, 1)

            def outs(key):
                c = slice(D * key[2], D * key[2] + D)
                act.wait_ge(vector_out, upto(vector_out, key, "o"))
                nc.scalar.copy(AH[:, :, c], RAW[:, :, c]).then_inc(scalar_out, 1)

            parts = {"setup": setup, "ctx": context, "fold": fold, "vw": slice_w, "silu": silu, "splitw": split_hidden, "split": split, "w2t": w2_transposed, "w2": w2,
                     "keyx": keyx, "norm": norm, "low": low, "att": att, "prob": prob, "logit": logit, "qx": qx,
                     "route": route, "z": hidden, "h": high, "gate": gate, "query": query, "row": row, "score": score,
                     "value": value, "out": outs}
            for key in order("scalar"):
                if key[0] in parts:
                    parts[key[0]](key)

        @block.vector
        def _(dve):
            v = nc.vector
            results = Count()

            def statistics(own_sem, key, chunks, stats, mean_var, source):
                for s, rows in chunks:
                    v.bn_stats(stats[0:rows, s, :], source(s)[0:rows, :]).then_inc(vector_results, results.one())
                dve.wait_ge(vector_results, results.n)
                for s, rows in chunks:
                    v.bn_aggr(mean_var[0:rows, s, :], stats[0:rows, s, :]).then_inc(vector_results, results.one())
                dve.wait_ge(vector_results, results.n)
                v.tensor_scalar(mean_var[:, :, 1], mean_var[:, :, 1], EPS, None, ALU.add).then_inc(own_sem, 1)

            def normal_form(chunks, mean_var, rstd, source, dst):
                for s, rows in chunks:
                    last = v.tensor_scalar(dst[0:rows, s, :], source(s)[0:rows, :], mean_var[0:rows, s, 0:1],
                                           rstd[0:rows, s:s + 1], ALU.subtract, ALU.mult)
                return last

            tokens = [(s, P) for s in range(NSUB)]

            def split_low(dst, full, high):
                return v.tensor_tensor(dst, full, raw(high), ALU.subtract)

            def setup(key):
                v.memset(HALF[:, :], -0.5)
                v.memset(VRC[:, 1, :], 0.0)
                v.memset(MV2[:, :, :], 1.0)
                v.memset(VA[:, :, :], 0.0)
                v.memset(VT1[:, :, :], 0.0)
                v.memset(WPR[:, :, :], 0.0).then_inc(vector_setup, 1)
                dve.wait_ge(vector_setup, upto(vector_setup, key, "fill"))
                dve.wait_ge(consts_loaded, 16 * 1)
                for g in range(GROUPS):
                    v.memset(VA[:, 4 * g:4 * g + 4, DH + 4 * g:DH + 4 * g + 4], 1.0)
                    v.tensor_copy(VT1[:, 4 * g:4 * g + 4, DH + 4 * g:DH + 4 * g + 4],
                                  CN[0:4 * TAIL, C_ROW:C_ROW + 4].unsqueeze(2).to_broadcast([4 * TAIL, 4, 4]))

            def vectors(key):
                dve.wait_ge(tensor_vec, upto(tensor_vec, key, "v"))
                v.tensor_copy(VC[:, :], S[:, 0, 0:N_VROWS]).then_inc(vector_vec, 1)

            def silu(key):
                dve.wait_ge(scalar_silu, upto(scalar_silu, key, "tc"))
                v.scalar_tensor_tensor(out=COT[:, :, :], in0=TC[:, :, :], scalar=1.0, in1=CO[:, :, :],
                                              op0=ALU.add, op1=ALU.mult).then_inc(vector_silu, 1)

            def split_hidden(key):
                dve.wait_ge(scalar_splitw, upto(scalar_splitw, key, "h"))
                split_low(WNl[:, :, :], WNR[:, :, :], WNh[:, :, :]).then_inc(vector_splitw, 1)

            def mod(key):
                dve.wait_ge(tensor_mod, upto(tensor_mod, key, "mod"))
                v.scalar_tensor_tensor(out=MOD[:, :, :], in0=V0[:, 0:8 * BATCH].rearrange("p (m b) -> p m b", m=8),
                                             scalar=0.5, in1=BSS[:, :].unsqueeze(2).to_broadcast([P, 8, BATCH]),
                                             op0=ALU.mult, op1=ALU.add).then_inc(vector_results, results.one())
                dve.wait_ge(vector_results, results.n)
                v.tensor_scalar(MOD[:, 0:2, :], MOD[:, 0:2, :], 1.0, None, ALU.add).then_inc(vector_results, results.one())
                v.tensor_scalar(MOD[:, 4:6, :], MOD[:, 4:6, :], 1.0, None, ALU.add).then_inc(vector_mod, 1)

            def query_bias(key):
                dve.wait_ge(tensor_bq, upto(tensor_bq, key, "bq"))
                v.tensor_tensor(BQ[:, :, :], V0[:, 64:64 + KC * BATCH].rearrange("p (f b) -> p f b", f=KC),
                                       BQ0[:, :].unsqueeze(2).to_broadcast([P, KC, BATCH]), ALU.add).then_inc(vector_bq, 1)

            def context(key):
                b = key[1]
                if b:
                    dve.wait_ge(tensor_z, upto(tensor_z, ("z", TPB * b - 1, NZ - 1), "z"))
                v.memset(B1T[:, :], 0.0)
                v.memset(AN[:, :, :], 0.0)
                v.memset(VTT[:, :, CTX:160], 0.0).then_inc(vector_results, results.one())
                dve.wait_ge(tensor_ctx, upto(tensor_ctx, key, "kT"))
                v.tensor_copy(KTT[:, :, 0:CTX], Z[:, 0, 0:320].rearrange("p (k n) -> p k n", k=KC)[:, :, 0:CTX]).then_inc(vector_ctx, 1)

            def fold(key):
                b = key[1]
                dve.wait_ge(vector_vec, upto(vector_vec, ("vec", 0), "v"))
                dve.wait_ge(vector_results, results.n)
                v.tensor_copy(AN[:, :, TAIL:TAIL + 1], CO[:, :, b:b + 1]).then_inc(vector_fold, 1)
                dve.wait_ge(tensor_fold, upto(tensor_fold, key, "VR"))
                v.tensor_copy(VRC[:, 0, :], OFF[:, 1, 0:EXPERTS])
                v.tensor_copy(VRC[0:64, 1, :], OFF[0:64, 1, 4:4 + EXPERTS]).then_inc(vector_fold, 1)
                dve.wait_ge(tensor_fold, upto(tensor_fold, key, "RC"))
                if b == 0:
                    dve.wait_ge(router_loaded, 16 * N_ROUTER)
                v.tensor_copy(A[:, :, CTX:CTX + EXPERTS], RW[:, 0:KC, :])
                v.tensor_tensor(RC[:, :], M0[:, 0:EXPERTS], RB[:, :], ALU.add).then_inc(vector_fold, 1)

            def slice_w(key):
                b, q = key[1:]
                dve.wait_ge(scalar_vw, upto(scalar_vw, key, "h"))
                v.tensor_tensor(VWl[:, q * QN:(q + 1) * QN], Z[:, q % 2, 0:QN],
                                raw(VWh[:, q * QN:(q + 1) * QN]), ALU.subtract).then_inc(vector_vw, 1)

            def tail(key):
                b = key[1]
                dve.wait_ge(tensor_tail, upto(tensor_tail, key, "m"))
                dve.wait_ge(hidden_bias_loaded, 16 * (N_HIDDEN_BIAS * (b + 1)))
                v.tensor_tensor(TF[:, :], M0[:, 0:QN], B1T[:, :], ALU.add).then_inc(vector_results, results.one())
                dve.wait_ge(vector_results, results.n)
                v.tensor_copy(TH[:, :], TF[:, :]).then_inc(vector_tail, 1)
                dve.wait_ge(vector_tail, upto(vector_tail, key, "th"))
                split_low(TL[:, :], TF[:, :], TH[:, :]).then_inc(vector_tail, 1)

            def w2(key):
                g = key[1]
                for i in range(2):
                    j = 2 * g + i
                    dve.wait_ge(scalar_w2, upto(scalar_w2, key, f"m{i}"))
                    v.scalar_tensor_tensor(out=W2l[:, 2 * j:2 * j + 2, :].rearrange("p k n -> p (k n)"),
                                                  in0=(V0[:, :], M0[:, :])[i], scalar=0.5,
                                                  in1=raw(W2h[:, 2 * j:2 * j + 2, :]).rearrange("p k n -> p (k n)"),
                                                  op0=ALU.mult, op1=ALU.subtract).then_inc(vector_w2, 1)

            def bias_out(key):
                dve.wait_ge(tensor_cb, upto(tensor_cb, key, "cb"))
                dve.wait_ge(broadcasts_loaded, 16 * N_BROADCAST)
                dve.wait_ge(vector_splitw, upto(vector_splitw, ("splitw", 0), "l"))
                v.memset(raw(BROW[:, :]), 0.0).then_inc(vector_results, results.one())
                dve.wait_ge(vector_results, results.n)
                for r in (0, 32):
                    v.memset(raw(BROW[r:r + 1, :]), 1.0)
                v.tensor_scalar(CBF[:, 0, :], GB[0:64, :], 2.0, None, ALU.mult)
                v.tensor_tensor(CBF[:, 1:3, :], V0[0:64, :].rearrange("p (e n) -> p e n", e=2),
                                OB[0:64, :].unsqueeze(1).to_broadcast([64, 2, D]), ALU.add)
                v.tensor_tensor(CBF[:, 3, :], S[0:64, 0, 0:D], OB[0:64, :], ALU.add).then_inc(vector_results, results.one())
                dve.wait_ge(vector_results, results.n)
                v.tensor_copy(CBH[:, :, :], CBF[:, :, :]).then_inc(vector_results, results.one())
                dve.wait_ge(vector_results, results.n)
                v.tensor_copy(CB[0:32, :, :], raw(CBH[0:32, :, :]))
                split_low(CB[32:64, :, :], CBF[32:64, :, :], CBH[32:64, :, :]).then_inc(vector_cb, 1)

            def keyn(key):
                b = key[1]
                chunks = [(0, P), (1, TAIL)]
                dve.wait_ge(kv_w_loaded, 16 * (4 * (b + 1)))
                statistics(vector_keyn, key, chunks, ST2, MV2, lambda s: CX1[:, s, :])
                dve.wait_ge(gpsimd_keyn, upto(gpsimd_keyn, key, "rstd"))
                normal_form(chunks, MV2, RS2, lambda s: CX1[:, s, :], XH2).then_inc(vector_keyn, 1)

            def keyx(key):
                for m in range(KC):
                    dve.wait_ge(scalar_keyx, upto(scalar_keyx, key, f"x{m}"))
                    last = v.tensor_copy(KXR[:, m, :].rearrange("p (i n) -> p i n", i=4),
                                         KX[:, m, P:CTX].unsqueeze(1).to_broadcast([P, 4, TAIL]))
                last.then_inc(vector_keyx, 1)

            def ones_rows():
                v.memset(KS[STACK:KROWS, :, :, :].bitcast(F32), 1.0).then_inc(vector_results, results.one())
                dve.wait_ge(vector_results, results.n)
                for j in range(2):
                    last = v.tensor_scalar(KS[STACK:KROWS, :, j, :], raw(KS[STACK:KROWS, :, j, :]),
                                           CN[STACK:KROWS, C_PAIR + j:C_PAIR + j + 1], None, ALU.mult)
                last.then_inc(vector_results, results.one())

            def pair_keys(key):
                dve.wait_ge(tensor_key, upto(tensor_key, key, "k"))
                for f in range(KC):
                    last = v.tensor_scalar(K1[:, f, 0:CTX], S[:, 0, 160 * f:160 * f + CTX], BK[:, f:f + 1],
                                           float(DH) ** -0.5, ALU.add, ALU.mult)
                last.then_inc(vector_key, 1)
                dve.wait_ge(vector_key, upto(vector_key, key, "k"))
                for f in range(KC):
                    for j in range(2):
                        last = v.tensor_scalar(KMH[:, f, j, :], K1[:, f, 0:CTX], CN[:, C_HEAD + j:C_HEAD + j + 1],
                                               None, ALU.mult)
                last.then_inc(vector_key, 1)
                dve.wait_ge(vector_key, upto(vector_key, key, "kh"))
                for f in range(KC):
                    for j in range(2):
                        last = v.scalar_tensor_tensor(out=KML[:, f, j, :], in0=K1[:, f, 0:CTX],
                                                      scalar=CN[:, C_HEAD + j:C_HEAD + j + 1],
                                                      in1=raw(KMH[:, f, j, :]), op0=ALU.mult, op1=ALU.subtract)
                last.then_inc(vector_key, 1)
                if key[1] == 0:
                    ones_rows()
                    v.memset(KT[:, :, :, :].bitcast(F32), 0.0)
                dve.wait_ge(tensor_key, upto(tensor_key, key, "v"))
                v.tensor_tensor(VA[:, :, 0:DH], S[:, 1, 0:D].rearrange("p (h r) -> p h r", r=DH),
                                       BV[:, :].rearrange("p (h r) -> p h r", r=DH), ALU.add).then_inc(vector_key, 1)
                dve.wait_ge(tensor_key, upto(tensor_key, key, "vt"))
                v.tensor_tensor(VTM[:, :], V0[0:4 * TAIL, 0:D], BV[0:4 * TAIL, :], ALU.add).then_inc(vector_results, results.one())
                dve.wait_ge(vector_results, results.n)
                for i in range(4):
                    last = v.tensor_scalar(VT1[:, i::4, 0:DH], VTM[:, :].rearrange("p (h r) -> p h r", r=DH)[:, i::4, :],
                                           CN[0:4 * TAIL, C_ROW + i:C_ROW + i + 1], None, ALU.mult)
                last.then_inc(vector_key, 1)

            def keyt(key):
                b = key[1]
                dve.wait_ge(keys_placed, 16 * 3 * PAIRS * (b + 1))
                for j in range(2):
                    last = v.tensor_copy(KT[:, j::2, 2 * j:2 * j + 2, :], raw(KS[:, j::2, :, P:CTX]))
                last.then_inc(vector_keyt, 1)

            def ln(key):
                t = key[1]
                dve.wait_ge(x_loaded[t % SLOTS], 16 * (t // SLOTS + 1))
                statistics(vector_ln, key, tokens, ST0, MV0, lambda s: X[:, t % SLOTS, s, :])

            def norm(key):
                t = key[1]
                if t % TPB == 0:
                    dve.wait_ge(tensor_tail, upto(tensor_tail, ("tail", t // TPB), "m"))
                    dve.wait_ge(vector_tail, upto(vector_tail, ("tail", t // TPB), "tl"))
                else:
                    dve.wait_ge(tensor_z, upto(tensor_z, ("z", t - 1, NZ - 1), "z"))
                dve.wait_ge(gpsimd_ln, upto(gpsimd_ln, ("ln", t), "rstd"))
                normal_form(tokens, MV0, RS0, lambda s: X[:, t % SLOTS, s, :], XH0).then_inc(vector_norm, 1)

            def att(key):
                t, s = key[1:]
                dve.wait_ge(tensor_att, upto(tensor_att, key, "s"))
                bank = OFF[:, s % 2, 0:CTX]
                if s == 0:
                    v.memset(PB[:, :, P:D], 0.0).then_inc(vector_results, results.one())
                    dve.wait_ge(vector_results, results.n)
                    v.memset(PB[:, :, P:P + 3 * 32].rearrange("p r (j n) -> p r j n", j=3)[:, :, :, TAIL:TAIL + 1], 1.0).then_inc(vector_results, results.one())
                v.tensor_reduce(SM0[:, s, 0:1], bank, AX.X, ALU.max, negate=True)
                logits = OFF[:, s % 2, CTX:CTX + EXPERTS]
                v.tensor_tensor(LG[:, s, :], logits, RC[:, :], ALU.add).then_inc(vector_att, 1)

            def prob(key):
                t, s = key[1:]
                dve.wait_ge(scalar_att, upto(scalar_att, ("att", t, s), "e"))
                v.reciprocal(SM0[:, s, 2:3], SM0[:, s, 1:2]).then_inc(vector_prob, 1)

            def route(key):
                t = key[1]
                dve.wait_ge(scalar_route, upto(scalar_route, key, "pm"))
                v.tensor_tensor(PTl[:, :], Z[:, 0, :], raw(PTh[:, :]), ALU.subtract).then_inc(vector_route, 1)
                dve.wait_ge(scalar_route, upto(scalar_route, key, "pd"))
                v.tensor_tensor(PTD[32:64, :], Z[32:64, 1, :], raw(PTD[32:64, :]), ALU.subtract).then_inc(vector_route, 1)

            def logit(key):
                t = key[1]
                dve.wait_ge(tensor_logit, upto(tensor_logit, key, "l"))
                dve.wait_ge(vector_att, upto(vector_att, ("att", t, NSUB - 1), "t"))
                v.tensor_tensor(LG[:, :, :], LG[:, :, :], OFF[:, 0, 0:4 * NSUB].rearrange("p (s e) -> p s e", e=4)[:, :, 0:EXPERTS],
                                ALU.add).then_inc(vector_logit, 1)
                dve.wait_ge(vector_logit, upto(vector_logit, key, "l"))
                v.tensor_reduce(RT[:, :, 0], LG[:, :, :], AX.X, ALU.max).then_inc(vector_results, results.one())
                dve.wait_ge(vector_results, results.n)
                v.tensor_tensor(LG[:, :, :], LG[:, :, :], RT[:, :, 0:1].to_broadcast([P, NSUB, EXPERTS]),
                                       ALU.subtract).then_inc(vector_logit, 1)
                dve.wait_ge(scalar_logit, upto(scalar_logit, key, "ex"))
                v.tensor_reduce(RT[:, :, 0], PR[:, :, :], AX.X, ALU.add).then_inc(vector_results, results.one())
                dve.wait_ge(vector_results, results.n)
                v.reciprocal(RT[:, :, 1], RT[:, :, 0]).then_inc(vector_results, results.one())
                dve.wait_ge(vector_results, results.n)
                v.tensor_tensor(PR[:, :, :], PR[:, :, :], RT[:, :, 1:2].to_broadcast([P, NSUB, EXPERTS]),
                                       ALU.mult).then_inc(vector_logit, 1)

            def hidden(key):
                t, k = key[1:]
                dve.wait_ge(scalar_z, upto(scalar_z, key, "t"))
                v.scalar_tensor_tensor(out=TB[:, k % 2, :], in0=TB[:, k % 2, :], scalar=1.0, in1=Z[:, k % 2, :],
                                              op0=ALU.add, op1=ALU.mult).then_inc(vector_z, 1)

            def evac(key):
                t, j = key[1:]
                dve.wait_ge(tensor_p, upto(tensor_p, ("p", t, GATES + PER * j - 1), "p"))
                if j == 1:
                    dve.wait_ge(vector_logit, upto(vector_logit, ("logit", t), "prob"))
                    if t % TPB == 0:
                        dve.wait_ge(tails_placed, 16 * 3 * NQ * (t // TPB + 1))
                else:
                    dve.wait_ge(vector_evac, upto(vector_evac, ("evac", t, j - 1), "o"))
                for s in range(NSUB):
                    if j == 1:
                        last = v.tensor_scalar(ACC[:, s, :], O[:, s, :], PR[:, s, 0:1], None, ALU.mult)
                    else:
                        last = v.scalar_tensor_tensor(out=ACC[:, s, :], in0=O[:, s, :], scalar=PR[:, s, j - 1:j],
                                                      in1=ACC[:, s, :], op0=ALU.mult, op1=ALU.add)
                last.then_inc(vector_evac, 1)

            def res(key):
                t = key[1]
                dve.wait_ge(gpsimd_gate, upto(gpsimd_gate, ("gate", t), "g"))
                dve.wait_ge(vector_evac, upto(vector_evac, ("evac", t, EXPERTS), "o"))
                v.tensor_tensor(ACC[:, :, :], G[:, :, :], ACC[:, :, :], ALU.mult).then_inc(vector_res, 1)
                dve.wait_ge(vector_res, upto(vector_res, key, "u"))
                v.tensor_tensor(X[:, t % SLOTS, :, :], ACC[:, :, :], X[:, t % SLOTS, :, :], ALU.add).then_inc(vector_res, 1)

            def qn(key):
                t = key[1]
                dve.wait_ge(vector_res, upto(vector_res, ("res", t), "x"))
                statistics(vector_qn, key, tokens, ST1, MV1, lambda s: X[:, t % SLOTS, s, :])

            def qx(key):
                t = key[1]
                b = t // TPB
                dve.wait_ge(gpsimd_qn, upto(gpsimd_qn, ("qn", t), "rstd"))
                if t:
                    dve.wait_ge(tensor_value, upto(tensor_value, ("value", t - 1, GROUPS - 1), "v"))
                if t % TPB == 0:
                    dve.wait_ge(tensor_key, upto(tensor_key, ("key", b), "vt"))
                normal_form(tokens, MV1, RS1, lambda s: X[:, t % SLOTS, s, :], XH1).then_inc(vector_qx, 1)

            def qlow(key):
                t = key[1]
                b = t // TPB
                for m in range(KC):
                    dve.wait_ge(scalar_qx, upto(scalar_qx, ("qx", t), f"x{m}"))
                    v.scalar_tensor_tensor(out=XQl[:, m, :], in0=S[:, m, :], scalar=MOD[:, m, b:b + 1],
                                                  in1=raw(XQh[:, m, :]), op0=ALU.mult, op1=ALU.subtract).then_inc(vector_qlow, 1)

            def query(key):
                t = key[1]
                b = t // TPB
                for f in range(KC):
                    dve.wait_ge(scalar_query, upto(scalar_query, key, f"q{f}"))
                    v.scalar_tensor_tensor(out=QL[:, f, :], in0=(V0[:, :], S[:, 0, :])[f],
                                                  scalar=BQ[:, f, b:b + 1], in1=raw(QH[:, f, :]),
                                                  op0=ALU.add, op1=ALU.subtract).then_inc(vector_query, 1)

            def most(key):
                t, u = key[1:]
                c, s = divmod(u, NSUB)
                bank = (S[:, 0, :], S[:, 1, :], V0[:, :], M0[:, :])[u % 4]
                dve.wait_ge(tensor_most, upto(tensor_most, key, "s"))
                v.tensor_reduce(MX[:, s, :, c], bank[:, 0:2 * CTX].rearrange("p (j n) -> p j n", j=2),
                                AX.X, ALU.max).then_inc(vector_most, 1)

            def row(key):
                dve.wait_ge(scalar_row, upto(scalar_row, key, "h"))
                v.scalar_tensor_tensor(out=NML[:, :], in0=V0[0:HEADS, :], scalar=-1.0, in1=raw(NMH[:, :]),
                                              op0=ALU.mult, op1=ALU.subtract).then_inc(vector_row, 1)

            def sums(key):
                t, h = key[1:]
                c = slice(D * h, D * h + D)
                dve.wait_ge(gpsimd_sum, upto(gpsimd_sum, ("sum", t, GROUPS - 1), "s"))
                v.reciprocal(SUM[:, c], SUM[:, c]).then_inc(vector_sums, 1)

            def outs(key):
                t, h = key[1:]
                c = slice(D * h, D * h + D)
                dve.wait_ge(vector_sums, upto(vector_sums, ("sums", t, h), "r"))
                if h:
                    dve.wait_ge(vector_out, upto(vector_out, ("out", t, 0), "o"))
                for g in range(GROUPS):
                    v.stream_shuffle(SD[:, g, :], SUM[:, c], [DH + 4 * g] * 32).then_inc(vector_results, results.one())
                dve.wait_ge(vector_results, results.n)
                v.tensor_tensor(RAW[:, :, c], RAW[:, :, c], SD[:, :, :], ALU.mult).then_inc(vector_out, 1)

            def outs_low(key):
                t, h = key[1:]
                c = slice(D * h, D * h + D)
                dve.wait_ge(scalar_out, upto(scalar_out, ("out", t, h), "h"))
                split_low(AL[:, :, c], RAW[:, :, c], AH[:, :, c]).then_inc(vector_outl, 1)

            def proj(key):
                t, h = key[1:]
                dve.wait_ge(gpsimd_bias, upto(gpsimd_bias, ("bias", t), "x"))
                dve.wait_ge(tensor_proj, upto(tensor_proj, key, "o"))
                x = X[:, t % SLOTS, 2 * h:2 * h + 2, :].rearrange("p s d -> p (s d)")
                v.tensor_tensor(x, S[:, h, :], x, ALU.add).then_inc(vector_proj, 1)

            parts = {"setup": setup, "ctx": context, "vec": vectors, "fold": fold, "vw": slice_w, "tail": tail,
                     "silu": silu, "mod": mod, "splitw": split_hidden, "bq": query_bias,  "w2": w2, "cb": bias_out, "keyn": keyn,
                     "keyx": keyx, "key": pair_keys, "keyt": keyt, "ln": ln, "norm": norm, "att": att,
                     "prob": prob, "route": route, "logit": logit, "z": hidden, "evac": evac, "res": res, "qn": qn, "qx": qx,
                     "qlow": qlow, "query": query, "most": most, "row": row, "sums": sums, "out": outs, "outl": outs_low,
                     "proj": proj}
            for key in order("vector"):
                if key[0] in parts:
                    parts[key[0]](key)

        @block.gpsimd
        def _(pool):
            def setup(key):
                rows = [(V_GAMMA, a["L0_xcond_ln_gamma"]), (V_BETA, a["L0_xcond_ln_beta"]),
                        (V_COND, a["cond_1024"].rearrange("b n -> (b n)")),
                        (V_B2, a["L0_xcond_e_b2"].rearrange("e n -> (e n)")),
                        (V_BSS, a["L1_xcond_bss_q"]), (V_BSS + 4, a["L1_xcond_bss_kv"]),
                        (V_BQ, a["L1_xcond_bq"]), (V_BK, a["L1_xcond_bkv"][0:D])]
                assert len(rows) == N_ROWS
                for row0, vector in rows:
                    chunks = vector.shape[0] // P
                    pool.dma_start(VROWS[row0:row0 + chunks, :], vector.rearrange("(k p) -> k p", p=P)).then_inc(rows_loaded, 16)
                for e in range(EXPERTS):
                    pool.dma_start(W2R[:, PER * e:PER * e + PER, :],
                                  feature_rows(a["L0_xcond_e_w2"][e])).then_inc(w2_loaded, 16)
                pool.dma_start(OW[:, :, :], feature_rows(a["L0_xcond_out_w"])).then_inc(w2_loaded, 16)

                heads = a["L1_xcond_Wp"].rearrange("(g i r) n -> i r g n", i=4, r=DH)
                pool.wait_ge(vector_setup, upto(vector_setup, ("setup", 0), "fill"))
                for i in range(4):
                    pool.dma_start(WPR[32 * i:32 * i + DH, :, :], heads[i]).then_inc(proj_w_loaded, 16)

            def rstd(key, var_sem, own_sem, dst, mv):
                pool.wait_ge(var_sem, upto(var_sem, key, "var"))
                nc.gpsimd.tensor_tensor(dst, mv, HALF[:, 0:dst.shape[1]], ALU.pow).then_inc(own_sem, 1)

            def keyn(key):
                rstd(key, vector_keyn, gpsimd_keyn, RS2[:, :], MV2[:, :, 1])

            def ln(key):
                rstd(key, vector_ln, gpsimd_ln, RS0[:, :], MV0[:, :, 1])

            def low(key):
                t = key[1]
                for m in range(KC):
                    pool.wait_ge(scalar_low, upto(scalar_low, ("low", t), f"n{m}"))
                    nc.gpsimd.tensor_tensor(NXl[:, m, :], NXf[:, m, :], raw(NXh[:, m, :]), ALU.subtract).then_inc(gpsimd_low, 1)

            def gate(key):
                pool.wait_ge(scalar_gate, upto(scalar_gate, key, "g"))
                nc.gpsimd.tensor_scalar(G[:, :, :], G[:, :, :], 0.5, 0.5, ALU.mult, ALU.add).then_inc(gpsimd_gate, 1)

            def qn(key):
                rstd(key, vector_qn, gpsimd_qn, RS1[:, :], MV1[:, :, 1])

            def hidden(key):
                t, k = key[1:]
                pool.wait_ge(scalar_h, upto(scalar_h, ("h", t, k), "h"))
                if NZ * t + k >= RING:
                    g = NZ * t + k - RING
                    pool.wait_ge(tensor_p, upto(tensor_p, ("p", g // NZ, g % NZ), "p"))
                nc.gpsimd.tensor_tensor(SL[:, k % RING, :], TB[:, k % 2, :], raw(SH[:, k % RING, :]),
                                               ALU.subtract).then_inc(gpsimd_h, 1)

            def bias(key):
                t = key[1]
                pool.wait_ge(vector_qx, upto(vector_qx, ("qx", t), "xh"))
                nc.gpsimd.tensor_tensor(X[:, t % SLOTS, :, :], X[:, t % SLOTS, :, :],
                                               BP[:, :].unsqueeze(1).to_broadcast([P, NSUB, D]), ALU.add).then_inc(gpsimd_bias, 1)

            def split(key):
                low, full, high = ((GWl, GWR, GWh), (WQl, WQ1R, WQh), (WPl, WPR, WPh))[key[1]]
                pool.wait_ge(scalar_split, upto(scalar_split, key, "h"))
                nc.gpsimd.tensor_tensor(low[:, :, :], full[:, :, :], raw(high[:, :, :]), ALU.subtract).then_inc(gpsimd_split, 1)

            def sums(key):
                t, g = key[1:]
                pool.wait_ge(scalar_value, upto(scalar_value, ("value", t, g), "v"))
                if g > 1:
                    pool.wait_ge(gpsimd_sum, upto(gpsimd_sum, ("sum", t, g - 1), "s"))
                nc.gpsimd.tensor_tensor(SUM[:, :], RAW[:, 0, :] if g == 1 else SUM[:, :], RAW[:, g, :],
                                        ALU.add).then_inc(gpsimd_sum, 1)

            parts = {"setup": setup, "split": split, "sum": sums, "keyn": keyn, "ln": ln, "low": low, "gate": gate, "qn": qn, "h": hidden, "bias": bias}
            for key in order("gpsimd"):
                if key[0] in parts:
                    parts[key[0]](key)

        @block.tensor
        def _(pe):
            mm = nc.tensor.matmul

            def exact(out_, left, right, start, stop, skip=False):
                (lh, ll), (rh, rl) = left, right
                mm(out_, lh, rh, start=start, stop=False, skip_group_check=skip)
                mm(out_, ll, rh, start=False, stop=False, skip_group_check=skip)
                return mm(out_, lh, rl, start=False, stop=stop, skip_group_check=skip)

            def plain(out_, pairs):
                for i, (l, r) in enumerate(pairs):
                    last = mm(out_, l, r, start=(i == 0), stop=(i == len(pairs) - 1))
                return last

            def setup(key):
                pe.wait_ge(consts_loaded, 16 * 1)
                pe.wait_ge(score_w_loaded, 16 * 1)
                for m in range(KC):
                    for k in range(KC):
                        last = pe.transpose(V0[:, D * m + P * k:D * m + P * k + P], WQR[:, k, P * m:P * m + P], ident)
                last.then_inc(tensor_setup, 1)

            def vectors(key):
                pe.wait_ge(rows_loaded, 16 * N_ROWS)
                pe.transpose(S[:, 0, 0:N_VROWS], VROWS[0:N_VROWS, :], CN[0:N_VROWS, C_ID:C_ID + N_VROWS]).then_inc(tensor_vec, 1)

            def mod(key):
                pe.wait_ge(modulation_w_loaded, 16 * 2)
                pe.wait_ge(vector_silu, upto(vector_silu, ("silu", 0), "sc"))
                pe.wait_ge(vector_cb, upto(vector_cb, ("cb", 0), "cb"))
                for w in range(2):
                    for m in range(4):
                        c = BATCH * (4 * w + m)
                        last = plain(V0[:, c:c + BATCH], [(WSS[:, w, k, P * m:P * m + P], COT[:, k, :]) for k in range(KC)])
                last.then_inc(tensor_mod, 1)

            def query_bias(key):
                pe.wait_ge(vector_mod, upto(vector_mod, ("mod", 0), "mod"))
                pe.wait_ge(small_w_loaded, 16 * 2)
                for f in range(KC):
                    last = plain(V0[:, 64 + BATCH * f:64 + BATCH * f + BATCH],
                                 [(WQ1R[:, k, P * f:P * f + P], MOD[:, 2 + k, :]) for k in range(KC)])
                last.then_inc(tensor_bq, 1)

            def context(key):
                b = key[1]
                pe.wait_ge(context_loaded, 16 * (4 * (b + 1)))
                if b:
                    pe.wait_ge(vector_z, upto(vector_z, ("z", TPB * b - 1, NZ - 1), "s"))
                    pe.wait_ge(vector_evac, upto(vector_evac, ("evac", TPB * b - 1, EXPERTS), "o"))
                    pe.wait_ge(scalar_score, upto(scalar_score, ("score", TPB * b - 2, 5 * GROUPS - 1), "e"))
                for k in range(KC):
                    pe.transpose(M0[:, 160 * k:160 * k + P], CX[:, 0, P * k:P * k + P], ident)
                    last = pe.transpose(M0[:, 160 * k + P:160 * k + CTX], CX[0:TAIL, 1, P * k:P * k + P],
                                        CN[0:TAIL, C_ID:C_ID + TAIL])
                last.then_inc(tensor_ctx, 1)
                pe.wait_ge(scalar_ctx, upto(scalar_ctx, key, "ctxT"))
                for step, bank, w in (("kT", Z[:, 0, :], WKR), ("vT", Z[:, 1, :], WVR)):
                    for m in range(KC):
                        last = plain(bank[:, 160 * m:160 * m + CTX],
                                     [(w[:, k, P * m:P * m + P], CXT[:, k, 0:CTX]) for k in range(KC)])
                    last.then_inc(tensor_ctx, 1)

            def fold(key):
                b = key[1]
                pe.wait_ge(vector_ctx, upto(vector_ctx, ("ctx", b), "kT"))
                if b == 0:
                    pe.wait_ge(vector_vec, upto(vector_vec, ("vec", 0), "v"))
                    pe.wait_ge(scalar_setup, upto(scalar_setup, ("setup", 0), "wqT"))
                    pe.wait_ge(router_loaded, 16 * N_ROUTER)
                for m in range(KC):
                    last = plain(OFF[:, 0, 160 * m:160 * m + CTX],
                                 [(WQT[:, k, P * m:P * m + P], KTT[:, k, 0:CTX]) for k in range(KC)])
                last.then_inc(tensor_fold, 1)
                pe.wait_ge(scalar_ctx, upto(scalar_ctx, ("ctx", b), "vT"))
                pe.wait_ge(vector_fold, upto(vector_fold, key, "fill"))
                plain(OFF[:, 1, 0:EXPERTS], [(VTT[:, k, 0:P], RW[:, KC + k, :]) for k in range(KC)])
                for r in (0, 32):
                    last = plain(OFF[r:r + 32, 1, 4:4 + EXPERTS], [(VTT[:, k, P:160], RW[:, KC + k, :]) for k in range(KC)])
                last.then_inc(tensor_fold, 1)
                last = plain(M0[:, 0:EXPERTS],
                             [(CO[:, k, b:b + 1].to_broadcast([P, P]), RW[:, 2 * KC + k, :]) for k in range(KC)])
                last.then_inc(tensor_fold, 1)

            def slice_w(key):
                b, q = key[1:]
                slot = (WS0, WS1)[q % 2]
                pe.wait_ge((slice_even_loaded, slice_odd_loaded)[q % 2], 16 * slices_loaded(b, q))
                if q == 0:
                    pe.wait_ge(vector_fold, upto(vector_fold, ("fold", b), "RC"))
                    pe.wait_ge(scalar_fold, upto(scalar_fold, ("fold", b), "A"))
                elif q >= 2:
                    pe.wait_ge(vector_vw, upto(vector_vw, ("vw", b, q - 2), "l"))
                    pe.wait_ge(scalar_vw, upto(scalar_vw, ("vw", b, q - 2), "t"))
                plain(Z[:, q % 2, 0:QN], [(VTT[:, k, 0:P], slot[:, k, :]) for k in range(KC)])
                bank = (M0[:, 0:QN], OFF[:, 1, 0:QN])[q % 2]
                rows = [VTT[:, k, P:160] for k in range(KC)] + [AN[:, k, :] for k in range(KC)]
                for k in range(2 * KC):
                    last = mm(bank[32 * k:32 * k + 32, :], rows[k], slot[:, k, :], start=True, stop=True)
                last.then_inc(tensor_vw, 1)

            def tail(key):
                b = key[1]
                pe.wait_ge(scalar_vw, upto(scalar_vw, ("vw", b, NQ - 1), "t"))
                for q in range(NQ):
                    last = mm(M0[32 * q:32 * q + 32, 0:QN], CN[:, C_FOLD:C_FOLD + 32], TQ[:, q, :], start=True, stop=True)
                last.then_inc(tensor_tail, 1)

            def w2_transposed(key):
                g = key[1]
                if g == 0:
                    pe.wait_ge(w2_loaded, 16 * (EXPERTS + 1))
                for k in range(KC):
                    if g:
                        pe.wait_ge(scalar_w2t, upto(scalar_w2t, ("w2t", g - 1), f"t{k}"))
                    for r in range(4):
                        last = pe.transpose(S[:, k, P * r:P * r + P], W2R[:, 4 * g + r, P * k:P * k + P], ident)
                    last.then_inc(tensor_w2t, 1)

            def w2(key):
                g = key[1]
                pe.wait_ge(scalar_w2t, upto(scalar_w2t, ("w2t", g), "t1"))
                for i in range(2):
                    if g:
                        pe.wait_ge(vector_w2, upto(vector_w2, ("w2", g - 1), f"m{i}"))
                    for r in range(2):
                        row0 = P * (4 * g + 2 * i + r)
                        last = plain((V0[:, :], M0[:, :])[i][:, D * r:D * r + D],
                                     [(W2T[:, k, row0:row0 + P], OW[:, k, :]) for k in range(KC)])
                    last.then_inc(tensor_w2, 1)

            def bias_out(key):
                pe.wait_ge(scalar_setup, upto(scalar_setup, ("setup", 0), "wqT"))
                pe.wait_ge(vector_w2, upto(vector_w2, ("w2", EXPERTS - 1), "m1"))
                for e in range(EXPERTS):
                    last = plain((V0[0:64, 0:D], V0[0:64, D:2 * D], S[0:64, 0, 0:D])[e],
                                 [(B2T[:, k, e:e + 1].to_broadcast([P, 64]), OW[:, k, :]) for k in range(KC)])
                last.then_inc(tensor_cb, 1)

            def keyx(key):
                b = key[1]
                pe.wait_ge(vector_keyn, upto(vector_keyn, key, "xh"))
                if b:
                    pe.wait_ge(vector_proj, upto(vector_proj, ("proj", TPB * b - 1, 1), "o"))
                else:
                    pe.wait_ge(vector_bq, upto(vector_bq, ("bq", 0), "bq"))
                for k in range(KC):
                    pe.transpose(V0[:, 160 * k:160 * k + P], XH2[:, 0, P * k:P * k + P], ident)
                    last = pe.transpose(V0[:, 160 * k + P:160 * k + CTX], XH2[0:TAIL, 1, P * k:P * k + P],
                                        CN[0:TAIL, C_ID:C_ID + TAIL])
                last.then_inc(tensor_keyx, 1)

            def pair_keys(key):
                b = key[1]
                pe.wait_ge(scalar_keyx, upto(scalar_keyx, key, "x1"))
                pe.wait_ge(kv_w_loaded, 16 * (4 * (b + 1)))
                for f in range(KC):
                    last = plain(S[:, 0, 160 * f:160 * f + CTX],
                                 [(WKV[:, k, P * f:P * f + P], KX[:, k, 0:CTX]) for k in range(KC)])
                last.then_inc(tensor_key, 1)
                plain(S[:, 1, 0:D], [(KX[:, k, 0:P], WKV[:, k, D:2 * D]) for k in range(KC)]).then_inc(tensor_key, 1)
                pe.wait_ge(vector_keyx, upto(vector_keyx, key, "rep"))
                plain(V0[0:4 * TAIL, 0:D], [(KXR[:, k, :], WKV[:, k, D:2 * D]) for k in range(KC)]).then_inc(tensor_key, 1)

            def norm(key):
                t = key[1]
                pe.wait_ge(vector_norm, upto(vector_norm, key, "xh"))
                for m in range(KC):
                    if t % TPB == 0:
                        pe.wait_ge(vector_vw, upto(vector_vw, ("vw", t // TPB, NQ - 2 + m), "l"))
                    else:
                        pe.wait_ge(vector_z, upto(vector_z, ("z", t - 1, NZ - 2 + m), "s"))
                    for s in range(NSUB):
                        last = pe.transpose(Z[:, m, P * s:P * s + P], XH0[:, s, P * m:P * m + P], ident)
                    last.then_inc(tensor_norm, 1)

            def att(key):
                t, s = key[1:]
                pe.wait_ge(scalar_norm, upto(scalar_norm, ("norm", t), "n1"))
                if s >= 2:
                    pe.wait_ge(vector_att, upto(vector_att, ("att", t, s - 2), "t"))
                    pe.wait_ge(scalar_att, upto(scalar_att, ("att", t, s - 2), "e"))
                elif t % TPB == 0:
                    pe.wait_ge(vector_tail, upto(vector_tail, ("tail", t // TPB), "th"))
                    pe.wait_ge(vector_fold, upto(vector_fold, ("fold", t // TPB), "RC"))
                    pe.wait_ge(scalar_vw, upto(scalar_vw, ("vw", t // TPB, NQ - 1), "t"))
                else:
                    pe.wait_ge(vector_evac, upto(vector_evac, ("evac", t - 1, EXPERTS), "o"))
                plain(OFF[:, s % 2, 0:CTX + EXPERTS],
                      [(NXf[:, k, P * s:P * s + P], A[:, k, :]) for k in range(KC)]).then_inc(tensor_att, 1)

            def prob(key):
                t, s = key[1:]
                pe.wait_ge(scalar_prob, upto(scalar_prob, key, "p"))
                pe.transpose(Z[:, 0, P * s:P * s + P], PB[:, s, 0:P], ident)
                pe.transpose(Z[0:STACK, 1, P * s:P * s + P], PB[:, s, P:P + STACK], ident).then_inc(tensor_prob, 1)

            def logit(key):
                t = key[1]
                pe.wait_ge(vector_route, upto(vector_route, ("route", t), "dl"))
                pe.wait_ge(vector_att, upto(vector_att, ("att", t, NSUB - 2), "t"))
                pe.wait_ge(scalar_att, upto(scalar_att, ("att", t, NSUB - 2), "e"))
                for s in range(NSUB):
                    c = slice(P * s, P * s + P)
                    last = plain(OFF[:, 0, 4 * s:4 * s + EXPERTS],
                                 [(raw(PTh[:, c]), VRC[:, 0, :]), (raw(PTl[:, c]), VRC[:, 0, :]),
                                  (raw(PTD[0:STACK, c]), VRC[0:STACK, 1, :])])
                last.then_inc(tensor_logit, 1)

            def hidden(key):
                t, k = key[1:]
                if k < 2:
                    pe.wait_ge(gpsimd_low, upto(gpsimd_low, ("low", t), "n1"))
                    pe.wait_ge(vector_route, upto(vector_route, ("route", t), "dl"))
                    if t == 0:
                        pe.wait_ge(vector_splitw, upto(vector_splitw, ("splitw", 0), "l"))
                    if t % TPB == 0:
                        pe.wait_ge(tails_placed, 16 * 3 * NQ * (t // TPB + 1))
                else:
                    pe.wait_ge(vector_z, upto(vector_z, ("z", t, k - 2), "s"))
                c = slice(P * k, P * k + P)
                bank = Z[:, k % 2, :]
                for m in range(KC):
                    exact(bank, (WNh[:, m, c], WNl[:, m, c]), (NXh[:, m, :], NXl[:, m, :]), m == 0, False)
                exact(bank, (VWh[:, c], VWl[:, c]), (PTh[:, :], PTl[:, :]), False, False)
                mm(bank, VWD[:, c], PTD[0:STACK, :], start=False, stop=True).then_inc(tensor_z, 1)

            def second(key):
                t, k = key[1:]
                pe.wait_ge(scalar_h, upto(scalar_h, ("h", t, k), "h"))
                pe.wait_ge(gpsimd_h, upto(gpsimd_h, ("h", t, k), "l"))
                first = k in (0, GATES) or (k >= GATES and (k - GATES) % PER == 0)
                last_one = k == GATES - 1 or (k >= GATES and (k - GATES) % PER == PER - 1)
                if first:
                    if k == 0:
                        pe.wait_ge(vector_logit, upto(vector_logit, ("logit", t), "l"))
                        pe.wait_ge(vector_att, upto(vector_att, ("att", t, NSUB - 1), "t"))
                        pe.wait_ge(scalar_att, upto(scalar_att, ("att", t, NSUB - 1), "e"))
                        if t:
                            pe.wait_ge(vector_evac, upto(vector_evac, ("evac", t - 1, EXPERTS), "o"))
                        else:
                            pe.wait_ge(gpsimd_split, upto(gpsimd_split, ("split", 0), "l"))
                    elif k == GATES:
                        pe.wait_ge(scalar_gate, upto(scalar_gate, ("gate", t), "g"))
                    else:
                        pe.wait_ge(vector_evac, upto(vector_evac, ("evac", t, (k - GATES) // PER), "o"))
                if last_one and k == GATES - 1 and t == 0:
                    pe.wait_ge(vector_cb, upto(vector_cb, ("cb", 0), "cb"))
                wh, wl = (GWh[:, k, :], GWl[:, k, :]) if k < GATES else (W2h[:, k - GATES, :], W2l[:, k - GATES, :])
                for s in range(NSUB):
                    c = slice(P * s, P * s + P)
                    last = exact(O[:, s, :], (SH[:, k % RING, c], SL[:, k % RING, c]), (wh, wl),
                                 first and s % 2 == 0, False, skip=True)
                    if last_one:
                        j = 0 if k < GATES else 1 + (k - GATES) // PER
                        last = mm(O[:, s, :], BROW[0:64, :], CB[:, j, :], start=False, stop=True, skip_group_check=True)
                last.then_inc(tensor_p, 1)

            def qx(key):
                t = key[1]
                pe.wait_ge(vector_qx, upto(vector_qx, key, "xh"))
                if t % TPB == 0:
                    pe.wait_ge(vector_key, upto(vector_key, ("key", t // TPB), "vt"))
                if t:
                    pe.wait_ge(vector_proj, upto(vector_proj, ("proj", t - 1, 1), "o"))
                for m in range(KC):
                    for s in range(NSUB):
                        last = pe.transpose(S[:, m, P * s:P * s + P], XH1[:, s, P * m:P * m + P], ident)
                    last.then_inc(tensor_qx, 1)

            def query(key):
                t = key[1]
                pe.wait_ge(vector_qlow, upto(vector_qlow, ("qlow", t), "x1"))
                if t == 0:
                    pe.wait_ge(gpsimd_split, upto(gpsimd_split, ("split", 1), "l"))
                for f in range(KC):
                    for k in range(KC):
                        c = slice(P * f, P * f + P)
                        last = exact((V0[:, :], S[:, 0, :])[f], (WQh[:, k, c], WQl[:, k, c]), (XQh[:, k, :], XQl[:, k, :]),
                                     k == 0, k == KC - 1)
                    last.then_inc(tensor_query, 1)

            def most(key):
                t, u = key[1:]
                c, s = divmod(u, NSUB)
                if s == 0:
                    pe.wait_ge(pair_placed[c], 16 * 3 * (t + 1))
                if u == 0:
                    pe.wait_ge(vector_query, upto(vector_query, ("query", t), "q1"))
                    if t % TPB == 0:
                        pe.wait_ge(vector_keyt, upto(vector_keyt, ("keyt", t // TPB), "kt"))
                        pe.wait_ge(keys_placed, 16 * 3 * PAIRS * (t // TPB + 1))
                if u == 3 and (t + 1) % TPB == 0 and t + 1 < NT:
                    pe.wait_ge(vector_tail, upto(vector_tail, ("tail", (t + 1) // TPB), "th"))
                if u >= 4:
                    pe.wait_ge(vector_most, upto(vector_most, ("most", t, u - 4), "s"))
                mm((S[:, 0, :], S[:, 1, :], V0[:, :], M0[:, :])[u % 4][:, 0:2 * CTX], QS[0:STACK, c, P * s:P * s + P],
                   KS[0:STACK, c, :, :].rearrange("p j n -> p (j n)"), start=True, stop=True).then_inc(tensor_most, 1)

            def row(key):
                t = key[1]
                pe.wait_ge(vector_most, upto(vector_most, ("most", t, NSUB * PAIRS - 1), "s"))
                for s in range(NSUB):
                    last = pe.transpose(V0[0:HEADS, P * s:P * s + P], MX[:, s, :, :].rearrange("p j c -> p (j c)"), ident)
                last.then_inc(tensor_row, 1)

            def score(key):
                t, w = key[1:]
                g, i = divmod(w, 5)
                if w == 0:
                    pe.wait_ge(maxima_placed, 16 * 4 * (t + 1))
                if w >= 3:
                    pe.wait_ge(scalar_score, upto(scalar_score, ("score", t, w - 3), "e"))
                bank = (S[:, 0, :], S[:, 1, :], M0[:, :])[w % 3]
                if i < 4:
                    c = 2 * g + i // 2
                    last = mm(bank, KS[:, c, i % 2, 0:P], QS[:, c, :], start=True, stop=True)
                else:
                    for j in range(2):
                        c = 2 * g + j
                        last = mm(bank[0:4 * TAIL, :], KT[:, c, :, :].rearrange("p i n -> p (i n)"), QS[:, c, :],
                                  start=(j == 0), stop=(j == 1))
                last.then_inc(tensor_score, 1)

            def value(key):
                t, g = key[1:]
                pe.wait_ge(scalar_score, upto(scalar_score, ("score", t, 5 * g + 4), "e"))
                if g:
                    pe.wait_ge(scalar_value, upto(scalar_value, ("value", t, g - 1), "v"))
                else:
                    pe.wait_ge(vector_row, upto(vector_row, ("row", t), "l"))
                for i in range(4):
                    mm(V0[32 * i:32 * i + 32, :], VA[:, 4 * g + i, :], E[:, (5 * g + i) % ERING, :], start=True, stop=False)
                for i in range(4):
                    last = mm(V0[32 * i:32 * i + 32, :], VT1[:, 4 * g + i, :], E[0:4 * TAIL, (5 * g + 4) % ERING, :], start=False, stop=True)
                last.then_inc(tensor_value, 1)

            def proj(key):
                t, h = key[1:]
                pe.wait_ge(vector_outl, upto(vector_outl, ("outl", t, h), "l"))
                pe.wait_ge(scalar_score, upto(scalar_score, ("score", t, 5 * GROUPS - 1), "e"))
                if t == 0:
                    pe.wait_ge(gpsimd_split, upto(gpsimd_split, ("split", 2), "l"))
                for s in (2 * h, 2 * h + 1):
                    c = slice(P * s, P * s + P)
                    for g in range(GROUPS):
                        last = exact(S[:, h, D * (s % 2):D * (s % 2) + D], (AH[:, g, c], AL[:, g, c]),
                                     (WPh[:, g, :], WPl[:, g, :]), g == 0, g == GROUPS - 1)
                last.then_inc(tensor_proj, 1)

            parts = {"setup": setup, "ctx": context, "vec": vectors, "fold": fold, "bq": query_bias, "vw": slice_w, "tail": tail, "mod": mod, "w2t": w2_transposed, "w2": w2,
                     "cb": bias_out, "keyx": keyx, "key": pair_keys, "norm": norm, "att": att, "prob": prob, "logit": logit,
                     "z": hidden, "p": second, "qx": qx, "query": query, "most": most, "row": row, "score": score,
                     "value": value, "proj": proj}
            for key in order("tensor"):
                if key[0] in parts:
                    parts[key[0]](key)


def kernel(**inputs):
    import numpy as np
    import concourse.bacc as bacc
    from concourse.bass_utils import run_bass_kernel_spmd

    nc = bacc.Bacc("TRN2", target_bir_lowering=False, num_devices=1)
    arrays, aps = {}, {}
    for name, value in inputs.items():
        arrays[name] = np.ascontiguousarray(value)
        aps[name] = nc.dram_tensor(name, arrays[name].shape, F32, kind="ExternalInput").ap()
    arrays["shape_constants"] = shape_constants(np)
    consts = nc.dram_tensor("shape_constants", (P, NCONST), F32, kind="ExternalInput").ap()
    out = nc.dram_tensor("out", (BATCH, SEQ, D), F32, kind="ExternalOutput").ap()
    build(nc, aps, out, consts)
    r = run_bass_kernel_spmd(nc, [arrays], core_ids=[0])
    return r.results[0]["out"]
```
